# Optimizing a Trainium2 kernel written in Bass

```python
import numpy as np
import jax
import jax.numpy as jnp

def _softmax(x, axis=-1):
    return jax.nn.softmax(x, axis=axis)

def _gelu(x):
    return jax.nn.gelu(x, approximate=True)

def _silu(x):
    return jax.nn.silu(x)

def _sigmoid(x):
    return jax.nn.sigmoid(x)

def _layernorm(x, axis=-1, eps=1e-05):
    m = jnp.mean(x, axis=axis, keepdims=True)
    v = jnp.var(x, axis=axis, keepdims=True)
    return (x - m) / jnp.sqrt(v + eps)

def _scatter_add(tgt, idx, src, axis=0):
    return tgt.at[idx].add(src)

def _segment_sum(src, seg, n):
    return jax.ops.segment_sum(src, seg, n)
kernel_name = 'mk_gnn_resnorm_d4_gnn_r64_1f97db'

def setup_inputs(seed: int=0):
    np.random.seed(seed)
    _w = jnp.asarray

    def _rec_inputs():
        import jax
        import jax.numpy as jnp
        _gk = jax.random.key(seed)
        x = -0.0001006 + 1 * jax.random.normal(jax.random.fold_in(_gk, 1), (100000, 96), jnp.float32)
        src = jax.random.randint(jax.random.fold_in(_gk, 2), (50000,), 0, 100000, jnp.int32)
        dst = jnp.minimum((100000 * jax.random.uniform(jax.random.fold_in(_gk, 3), (50000,)) ** 2.0).astype(jnp.int32), 99999)
        _o = jnp.argsort(dst, stable=True)
        src = src[_o]
        dst = dst[_o]
        edge_weight1 = 0.000614103 + 0.999867 * jax.random.normal(jax.random.fold_in(_gk, 12), (50000, 1), jnp.float32)
        return (x, src, dst, edge_weight1)
    x, src, dst, edge_weight1 = _rec_inputs()

    def _L0_gnn_setup():
        import jax, jax.numpy as jnp
        import numpy as np
        K = 10
        ALPHA = 0.1
        BETA = 0.9
        N_NODES = 50000
        N_EDGES = 12500
        D_FEAT = 96
        key = jax.random.key(seed)
        k1, k2, k3 = jax.random.split(key, 3)
        x = jax.random.normal(k1, (N_NODES, D_FEAT), dtype=jnp.float32)
        row = jax.random.randint(k2, (N_EDGES,), 0, N_NODES, dtype=jnp.int64)
        col = jax.random.randint(k3, (N_EDGES,), 0, N_NODES, dtype=jnp.int64)
        edge_index = jnp.stack([row, col], axis=0)
        return {'x': x, 'edge_index': edge_index}
    _L0_gnn_all = _L0_gnn_setup()
    _L0_gnn_in = {k: v for k, v in _L0_gnn_all.items() if k in ()}
    del _L0_gnn_all

    def _L1_gnn_setup():
        import jax, jax.numpy as jnp
        import numpy as np
        N = 50000
        E = 12500
        C_IN = 96
        C_OUT = 96
        key = jax.random.key(seed)
        k1, k2, k3 = jax.random.split(key, 3)
        x = jax.random.normal(k1, (N, C_IN), dtype=jnp.float32)
        edge_index = jax.random.randint(k2, (2, E), 0, N, dtype=jnp.int64)
        W = jax.random.normal(k3, (C_IN, C_OUT), dtype=jnp.float32) / np.sqrt(C_IN)
        b = jnp.zeros((C_OUT,), dtype=jnp.float32)
        prelu_a = jnp.full((1,), 0.25, dtype=jnp.float32)
        return {'x': x, 'W': W, 'b': b, 'prelu_a': prelu_a, 'edge_index': edge_index}
    _L1_gnn_all = _L1_gnn_setup()
    _L1_gnn_in = {k: v for k, v in _L1_gnn_all.items() if k in ('W', 'b', 'prelu_a')}
    del _L1_gnn_all

    def _L2_gnn_setup():
        import jax, jax.numpy as jnp
        import numpy as np
        N, C, E = (50000, 96, 12500)
        SCALES = (2, 3, 4)
        BN_EPS = 1e-05

        def _cheb(x, prop, w, b):
            K = w.shape[0]
            Tx0 = x
            out = Tx0 @ w[0]
            if K > 1:
                Tx1 = prop(Tx0)
                out = out + Tx1 @ w[1]
                for k in range(2, K):
                    Tx2 = 2.0 * prop(Tx1) - Tx0
                    out = out + Tx2 @ w[k]
                    Tx0, Tx1 = (Tx1, Tx2)
            return out + b
        key = jax.random.key(seed)
        ks = jax.random.split(key, 16)
        inp = {'x': jax.random.normal(ks[0], (N, C), dtype=jnp.float32), 'edge_index': jax.random.randint(ks[1], (2, E), 0, N, dtype=jnp.int64)}
        s = 1.0 / np.sqrt(C)
        for i, k in enumerate(SCALES):
            inp[f'w{k}'] = jax.random.uniform(ks[2 + 2 * i], (k, C, C), jnp.float32, -s, s)
            inp[f'b{k}'] = jax.random.uniform(ks[3 + 2 * i], (C,), jnp.float32, -s, s)
        s3 = 1.0 / np.sqrt(3 * C)
        inp['attn_w'] = jax.random.uniform(ks[8], (3 * C, 3), jnp.float32, -s3, s3)
        inp['attn_b'] = jax.random.uniform(ks[9], (3,), jnp.float32, -s3, s3)
        inp['fus_w'] = jax.random.uniform(ks[10], (3 * C, C), jnp.float32, -s3, s3)
        inp['fus_b'] = jax.random.uniform(ks[11], (C,), jnp.float32, -s3, s3)
        inp['bn_gamma'] = jnp.ones((C,), jnp.float32)
        inp['bn_beta'] = jnp.zeros((C,), jnp.float32)
        return inp
    _L2_gnn_all = _L2_gnn_setup()
    _L2_gnn_in = {k: v for k, v in _L2_gnn_all.items() if k in ('w2', 'b2', 'w3', 'b3', 'w4', 'b4', 'attn_w', 'attn_b', 'fus_w', 'fus_b', 'bn_gamma', 'bn_beta')}
    del _L2_gnn_all

    def _L3_gnn_setup():
        import jax, jax.numpy as jnp
        import numpy as np
        N = 50000
        E = 12500
        C = 96

        def _lin_params(key, fan_in, fan_out):
            k1, k2 = jax.random.split(key)
            bound = 1.0 / np.sqrt(fan_in)
            W = jax.random.uniform(k1, (fan_in, fan_out), minval=-bound, maxval=bound, dtype=jnp.float32)
            b = jax.random.uniform(k2, (fan_out,), minval=-bound, maxval=bound, dtype=jnp.float32)
            return (W, b)

        def _gine_conv(x, src, dst, e, W1, b1, W2, b2):
            msg = jax.nn.relu(x[src] + e)
            agg = jax.ops.segment_sum(msg, dst, num_segments=x.shape[0])
            h = x + agg
            h = jax.nn.relu(h @ W1 + b1)
            h = jax.nn.relu(h @ W2 + b2)
            return h
        key = jax.random.key(seed)
        ks = jax.random.split(key, 10)
        x = jax.random.normal(ks[0], (N, C), dtype=jnp.float32)
        edge_index = jax.random.randint(ks[1], (2, E), 0, N, dtype=jnp.int64)
        edge_attr = jax.random.normal(ks[2], (E, 1), dtype=jnp.float32)
        W_l0, b_l0 = _lin_params(ks[3], 1, C)
        W_l1, b_l1 = _lin_params(ks[4], C, C)
        W00, b00 = _lin_params(ks[5], C, C)
        W01, b01 = _lin_params(ks[6], C, C)
        W10, b10 = _lin_params(ks[7], C, C)
        W11, b11 = _lin_params(ks[8], C, C)
        return {'x': x, 'edge_index': edge_index, 'edge_attr': edge_attr, 'W_l0': W_l0, 'b_l0': b_l0, 'W_l1': W_l1, 'b_l1': b_l1, 'W00': W00, 'b00': b00, 'W01': W01, 'b01': b01, 'W10': W10, 'b10': b10, 'W11': W11, 'b11': b11}
    _L3_gnn_all = _L3_gnn_setup()
    _L3_gnn_in = {k: v for k, v in _L3_gnn_all.items() if k in ('W_l0', 'b_l0', 'W_l1', 'b_l1', 'W00', 'b00', 'W01', 'b01', 'W10', 'b10', 'W11', 'b11')}
    del _L3_gnn_all
    return {'x': x, 'src': src, 'dst': dst, 'edge_weight1': edge_weight1, 'L1_gnn_W': _L1_gnn_in['W'], 'L1_gnn_b': _L1_gnn_in['b'], 'L1_gnn_prelu_a': _L1_gnn_in['prelu_a'], 'L2_gnn_w2': _L2_gnn_in['w2'], 'L2_gnn_b2': _L2_gnn_in['b2'], 'L2_gnn_w3': _L2_gnn_in['w3'], 'L2_gnn_b3': _L2_gnn_in['b3'], 'L2_gnn_w4': _L2_gnn_in['w4'], 'L2_gnn_b4': _L2_gnn_in['b4'], 'L2_gnn_attn_w': _L2_gnn_in['attn_w'], 'L2_gnn_attn_b': _L2_gnn_in['attn_b'], 'L2_gnn_fus_w': _L2_gnn_in['fus_w'], 'L2_gnn_fus_b': _L2_gnn_in['fus_b'], 'L2_gnn_bn_gamma': _L2_gnn_in['bn_gamma'], 'L2_gnn_bn_beta': _L2_gnn_in['bn_beta'], 'L3_gnn_W_l0': _L3_gnn_in['W_l0'], 'L3_gnn_b_l0': _L3_gnn_in['b_l0'], 'L3_gnn_W_l1': _L3_gnn_in['W_l1'], 'L3_gnn_b_l1': _L3_gnn_in['b_l1'], 'L3_gnn_W00': _L3_gnn_in['W00'], 'L3_gnn_b00': _L3_gnn_in['b00'], 'L3_gnn_W01': _L3_gnn_in['W01'], 'L3_gnn_b01': _L3_gnn_in['b01'], 'L3_gnn_W10': _L3_gnn_in['W10'], 'L3_gnn_b10': _L3_gnn_in['b10'], 'L3_gnn_W11': _L3_gnn_in['W11'], 'L3_gnn_b11': _L3_gnn_in['b11']}

def reference(x, src, dst, edge_weight1, L1_gnn_W, L1_gnn_b, L1_gnn_prelu_a, L2_gnn_w2, L2_gnn_b2, L2_gnn_w3, L2_gnn_b3, L2_gnn_w4, L2_gnn_b4, L2_gnn_attn_w, L2_gnn_attn_b, L2_gnn_fus_w, L2_gnn_fus_b, L2_gnn_bn_gamma, L2_gnn_bn_beta, L3_gnn_W_l0, L3_gnn_b_l0, L3_gnn_W_l1, L3_gnn_b_l1, L3_gnn_W00, L3_gnn_b00, L3_gnn_W01, L3_gnn_b01, L3_gnn_W10, L3_gnn_b10, L3_gnn_W11, L3_gnn_b11):
    import jax
    import jax.numpy as jnp

    def _L0_gnn_ref(x, edge_index):
        import jax, jax.numpy as jnp
        import numpy as np
        K = 10
        ALPHA = 0.1
        BETA = 0.9
        N_NODES = 50000
        N_EDGES = 12500
        D_FEAT = 96
        n = x.shape[0]
        row, col = (edge_index[0], edge_index[1])
        ones = jnp.ones((edge_index.shape[1],), dtype=x.dtype)
        deg_row = jnp.maximum(jax.ops.segment_sum(ones, row, num_segments=n), 1.0)
        deg_col = jnp.maximum(jax.ops.segment_sum(ones, col, num_segments=n), 1.0)
        w = jax.lax.rsqrt(deg_row[row] * deg_col[col])

        def spmm(feat):
            msg = feat[col] * w[:, None]
            return jax.ops.segment_sum(msg, row, num_segments=n)
        h = x
        out = h
        for _ in range(K):
            out = spmm(out) * BETA + h * ALPHA
        theta = BETA ** K + ALPHA * sum((BETA ** i for i in range(K)))
        return out / jnp.asarray(theta, dtype=x.dtype)

    def _L1_gnn_ref(x, W, b, prelu_a, edge_index):
        import jax, jax.numpy as jnp
        import numpy as np
        N = 50000
        E = 12500
        C_IN = 96
        C_OUT = 96
        n = x.shape[0]
        row, col = (edge_index[0], edge_index[1])
        loop = jnp.arange(n, dtype=edge_index.dtype)
        row = jnp.concatenate([row, loop])
        col = jnp.concatenate([col, loop])
        deg = jax.ops.segment_sum(jnp.ones_like(col, dtype=x.dtype), col, num_segments=n)
        dinv = jnp.where(deg > 0, jax.lax.rsqrt(deg), jnp.zeros_like(deg))
        norm = dinv[row] * dinv[col]
        h = x @ W
        msg = h[row] * norm[:, None]
        out = jax.ops.segment_sum(msg, col, num_segments=n) + b
        return jnp.where(out >= 0, out, prelu_a * out)

    def _L2_gnn_ref(x, edge_index, w2, b2, w3, b3, w4, b4, attn_w, attn_b, fus_w, fus_b, bn_gamma, bn_beta):
        import jax, jax.numpy as jnp
        import numpy as np
        N, C, E = (50000, 96, 12500)
        SCALES = (2, 3, 4)
        BN_EPS = 1e-05

        def _cheb(x, prop, w, b):
            K = w.shape[0]
            Tx0 = x
            out = Tx0 @ w[0]
            if K > 1:
                Tx1 = prop(Tx0)
                out = out + Tx1 @ w[1]
                for k in range(2, K):
                    Tx2 = 2.0 * prop(Tx1) - Tx0
                    out = out + Tx2 @ w[k]
                    Tx0, Tx1 = (Tx1, Tx2)
            return out + b
        n = x.shape[0]
        row, col = (edge_index[0], edge_index[1])
        deg = jax.ops.segment_sum(jnp.ones(row.shape[0], x.dtype), row, num_segments=n)
        dis = jnp.where(deg > 0, jax.lax.rsqrt(jnp.maximum(deg, 1.0)), 0.0)
        wn = -(dis[row] * dis[col])

        def prop(h):
            return jax.ops.segment_sum(wn[:, None] * h[row], col, num_segments=n)
        feats = [_cheb(x, prop, w2, b2), _cheb(x, prop, w3, b3), _cheb(x, prop, w4, b4)]
        concat = jnp.concatenate(feats, axis=1)
        scale_w = jax.nn.softmax(concat @ attn_w + attn_b, axis=1)
        fused = jnp.concatenate([feats[i] * scale_w[:, i:i + 1] for i in range(3)], axis=1)
        h = fused @ fus_w + fus_b
        mean = jnp.mean(h, axis=0)
        var = jnp.mean((h - mean) ** 2, axis=0)
        h = (h - mean) * jax.lax.rsqrt(var + BN_EPS) * bn_gamma + bn_beta
        return jax.nn.relu(h)

    def _L3_gnn_ref(x, edge_index, edge_attr, W_l0, b_l0, W_l1, b_l1, W00, b00, W01, b01, W10, b10, W11, b11):
        import jax, jax.numpy as jnp
        import numpy as np
        N = 50000
        E = 12500
        C = 96

        def _lin_params(key, fan_in, fan_out):
            k1, k2 = jax.random.split(key)
            bound = 1.0 / np.sqrt(fan_in)
            W = jax.random.uniform(k1, (fan_in, fan_out), minval=-bound, maxval=bound, dtype=jnp.float32)
            b = jax.random.uniform(k2, (fan_out,), minval=-bound, maxval=bound, dtype=jnp.float32)
            return (W, b)

        def _gine_conv(x, src, dst, e, W1, b1, W2, b2):
            msg = jax.nn.relu(x[src] + e)
            agg = jax.ops.segment_sum(msg, dst, num_segments=x.shape[0])
            h = x + agg
            h = jax.nn.relu(h @ W1 + b1)
            h = jax.nn.relu(h @ W2 + b2)
            return h
        src, dst = (edge_index[0], edge_index[1])
        e = jax.nn.relu(edge_attr @ W_l0 + b_l0) @ W_l1 + b_l1
        h = _gine_conv(x, src, dst, e, W00, b00, W01, b01)
        h = jax.nn.relu(h)
        h = _gine_conv(h, src, dst, e, W10, b10, W11, b11)
        h = jax.nn.relu(h)
        return h
    edge_index = jnp.stack([src, dst])
    x = _layernorm(x + _L0_gnn_ref(x, edge_index), axis=-1)
    x = _layernorm(x + _L1_gnn_ref(x, L1_gnn_W, L1_gnn_b, L1_gnn_prelu_a, edge_index), axis=-1)
    x = _layernorm(x + _L2_gnn_ref(x, edge_index, L2_gnn_w2, L2_gnn_b2, L2_gnn_w3, L2_gnn_b3, L2_gnn_w4, L2_gnn_b4, L2_gnn_attn_w, L2_gnn_attn_b, L2_gnn_fus_w, L2_gnn_fus_b, L2_gnn_bn_gamma, L2_gnn_bn_beta), axis=-1)
    x = _layernorm(x + _L3_gnn_ref(x, edge_index, edge_weight1, L3_gnn_W_l0, L3_gnn_b_l0, L3_gnn_W_l1, L3_gnn_b_l1, L3_gnn_W00, L3_gnn_b00, L3_gnn_W01, L3_gnn_b01, L3_gnn_W10, L3_gnn_b10, L3_gnn_W11, L3_gnn_b11), axis=-1)
    return x

_drawn_inputs = setup_inputs


def setup_inputs(seed=0):
    import zlib

    import numpy as np

    out = dict(_drawn_inputs(seed))
    spreads = {'L1_gnn_b': (0.0, 0.1), 'L2_gnn_bn_gamma': (1.0, 0.2), 'L2_gnn_bn_beta': (0.0, 0.1)}
    factors = {'edge_weight1': 3.53,
     'L2_gnn_b2': 5.921,
     'L2_gnn_b3': 6.239,
     'L2_gnn_b4': 3.812,
     'L2_gnn_attn_b': 5.706,
     'L2_gnn_fus_b': 8.0,
     'L3_gnn_W_l0': 3.534,
     'L3_gnn_b_l0': 3.115,
     'L3_gnn_b_l1': 7.647,
     'L3_gnn_b00': 8.0,
     'L3_gnn_b01': 7.748,
     'L3_gnn_b10': 3.487}
    for name, (base, spread) in spreads.items():
        noise = np.random.default_rng([zlib.crc32(name.encode()), seed]).standard_normal(out[name].shape)
        drawn = base * np.exp(spread * noise) if base else spread * noise
        out[name] = jnp.asarray(drawn.astype(out[name].dtype))
    for name, factor in factors.items():
        out[name] = (out[name] * factor).astype(out[name].dtype)
    return out
```

```python
from contextlib import ExitStack

import concourse.bass as bass
from concourse import mybir

P = 128
C = 96
GROUP = 14
QUADS = ((0, 4), (4, 4), (8, 4), (12, 2))
LASTS = 16
NOWHERE = 1 << 20
K_HOPS, ALPHA, BETA = 10, 0.1, 0.9
THETA = BETA ** K_HOPS + ALPHA * sum(BETA ** i for i in range(K_HOPS))
LN_EPS = 1e-5
BN_EPS = 1e-5

ALU = mybir.AluOpType
ACT = mybir.ActivationFunctionType
F32 = mybir.dt.float32
BF16 = mybir.dt.bfloat16
I32 = mybir.dt.int32
AX_X = mybir.AxisListType.X


class Order:

    def __init__(self, eng, sem):
        self.eng, self.sem, self.count = eng, sem, 0

    def step(self, ins):
        ins.then_inc(self.sem, 1)
        self.count = self.count + 1

    def wait(self):
        self.eng.wait_ge(self.sem, self.count)


def loop(eng, n, body, order=None):
    start = order.count if order else 0
    body(0, True, n == 1)
    per = order.count - start if order else 0
    if n > 2:
        with eng.Fori(1, n - 1) as i:
            if order:
                order.count = i * per + start
            body(i, False, False)
    if n > 1:
        if order:
            order.count = start + (n - 1) * per
        body(n - 1, False, True)


def spread(ap, n):
    return ap.unsqueeze(2).to_broadcast([P, ap.shape[1], n])


class Phase:

    def __init__(self, nc, name, sems):
        self.nc, self.name, self.names = nc, name, sems

    def __enter__(self):
        self.stack = ExitStack()
        self.sems = {s: self.nc.alloc_semaphore(f"{self.name}_{s}") for s in self.names}
        return self

    def sbuf(self, name, shape, dtype=F32):
        return self.stack.enter_context(self.nc.sbuf_tensor(f"{self.name}_{name}", shape, dtype))

    def psum(self, name, shape, dtype=F32):
        return self.stack.enter_context(self.nc.psum_tensor(f"{self.name}_{name}", shape, dtype))

    def block(self):
        return self.stack.enter_context(self.nc.Block())

    def __exit__(self, *failed):
        self.stack.close()
        if not failed[0]:
            self.nc.clear_and_free_semaphores(list(self.sems.values()))
            self.nc.all_engine_barrier()


def constants(nc, k):
    with Phase(nc, "const", ["made", "loaded"]) as ph:
        made, loaded = ph.sems["made"], ph.sems["loaded"]
        block = ph.block()

        @block.gpsimd
        def _(pool):
            nc.gpsimd.memset(k.ident[:, :], 0.0).then_inc(made, 1)
            nc.gpsimd.memset(k.before[:, :, :], 1.0).then_inc(made, 1)
            nc.gpsimd.memset(k.later[:, :, :], 1.0).then_inc(made, 1)
            nc.gpsimd.memset(k.first_row[:, :], 1.0).then_inc(made, 1)
            nc.gpsimd.memset(k.edge_rows[:, :], 0.0).then_inc(made, 1)
            nc.gpsimd.memset(k.ones_bf[:, :], 1.0).then_inc(made, 1)
            nc.gpsimd.memset(k.zeros_bf[:, :], 0.0).then_inc(made, 1)
            nc.gpsimd.memset(k.ones[:, :], 1.0).then_inc(made, 1)
            nc.gpsimd.iota(k.iota[:, :], pattern=[[1, 512]], base=0, channel_multiplier=0,
                           allow_small_or_imprecise_dtypes=True).then_inc(made, 1)
            nc.gpsimd.iota(k.edge_row[:, :], pattern=[[1, k.T]], base=0, channel_multiplier=k.T,
                           allow_small_or_imprecise_dtypes=True).then_inc(made, 1)
            nc.gpsimd.memset(k.zeros_f[:, :], 0.0).then_inc(made, 1)
            nc.gpsimd.memset(k.valid[:, :], 1.0).then_inc(made, 1)
            nc.gpsimd.memset(k.final_row[:, :], 1.0).then_inc(made, 1)
            nc.gpsimd.memset(k.pick_row[:, :], 0.0).then_inc(made, 1)
            nc.gpsimd.memset(k.after_row[:, :], 1.0).then_inc(made, 1)
            pool.wait_ge(made, 15)

            def keep(ap, op, base, cm, step, n, fill):
                nc.gpsimd.affine_select(out=ap, in_=ap, compare_op=op, fill=fill, base=base,
                                        pattern=[[step, n]], channel_multiplier=cm).then_inc(made, 1)

            keep(k.ident[:, :], ALU.not_equal, 0, 1, -1, P, 1.0)
            keep(k.before[:, 0, :], ALU.is_gt, 0, -1, 1, P, 0.0)
            keep(k.before[:, 1, :], ALU.is_gt, 0, 1, -1, P, 0.0)
            keep(k.later[:, 0, :], ALU.is_gt, 0, -1, 1, P, 0.0)
            keep(k.later[:, 1, :], ALU.is_gt, 0, 1, -1, P, 0.0)
            keep(k.first_row[:, :], ALU.is_equal, 0, 1, 0, P, 0.0)
            keep(k.edge_rows[:, 0:1], ALU.not_equal, 0, 1, 0, 1, 1.0)
            keep(k.edge_rows[:, 1:2], ALU.not_equal, 1 - P, 1, 0, 1, 1.0)
            nc.gpsimd.affine_select(out=k.valid[:, :], in_=k.valid[:, :], compare_op=ALU.is_ge, fill=0.0,
                                    base=k.N - 1 - (k.NP - P * GROUP), pattern=[[-1, GROUP]],
                                    channel_multiplier=-GROUP).then_inc(made, 1)
            keep(k.final_row[:, :], ALU.is_equal, 1 - P, 1, 0, P, 0.0)
            keep(k.pick_row[:, :], ALU.not_equal, 1, -1, 1, GROUP, 1.0)
            keep(k.after_row[:, :], ALU.is_ge, 0, -1, 1, GROUP, 0.0)
            pool.wait_ge(made, 27)
            nc.gpsimd.memset(k.pick_row[0:1, GROUP - 1:GROUP], 1.0).then_inc(made, 1)
            pool.wait_ge(made, 28)

        @block.vector
        def _(dve):
            dve.wait_ge(made, 28)
            nc.vector.tensor_scalar(k.rest[:, :, :], k.before[:, :, :], -1.0, 1.0,
                                    ALU.mult, ALU.add).then_inc(made, 1)
            dve.wait_ge(made, 29)


def gather_edges(nc, k, src, dst, weight, table):
    T, E, N = k.T, k.E, k.N
    full, rem = E // T, E % T
    with Phase(nc, "edges", ["filled", "loaded", "packed", "stored"]) as ph:
        filled, loaded, packed, stored = (ph.sems[s] for s in ph.names)
        ends = ph.sbuf("ends", [P, 2, T], I32)
        weights = ph.sbuf("weights", [P, T])
        rows = ph.sbuf("rows", [P, T, 4])
        block = ph.block()

        @block.sync
        def _(sp):
            sp.wait_ge(filled, 2)
            n = 0
            for what, into in ((src, ends[:, 0, :]), (dst, ends[:, 1, :]), (weight, weights[:, :])):
                sp.dma_start(into[0:full, :], what[0:full * T].rearrange("(p t) -> p t", t=T)).then_inc(loaded, 16)
                n += 16
                if rem:
                    sp.dma_start(into[full:full + 1, 0:rem],
                                 what[full * T:E].rearrange("(p t) -> p t", p=1)).then_inc(loaded, 16)
                    n += 16
            sp.wait_ge(loaded, n)
            sp.wait_ge(packed, 4)
            sp.dma_start(table.rearrange("(p t) c -> p t c", p=P), rows[:, :, :]).then_inc(stored, 16)
            sp.wait_ge(stored, 16)

        @block.vector
        def _(dve):
            nc.vector.memset(ends[:, :, :], N).then_inc(filled, 1)
            nc.vector.memset(weights[:, :], 0.0).then_inc(filled, 1)
            nc.vector.memset(rows[:, :, 3:4], 0.0).then_inc(packed, 1)
            dve.wait_ge(loaded, 16 * (6 if rem else 3))
            nc.vector.tensor_copy(rows[:, :, 0], ends[:, 0, :]).then_inc(packed, 1)
            nc.vector.tensor_copy(rows[:, :, 1], ends[:, 1, :]).then_inc(packed, 1)
            nc.vector.tensor_copy(rows[:, :, 2], weights[:, :]).then_inc(packed, 1)


def radix_pass(nc, k, name, unsorted, by_rank, field, shift, buckets):
    T = k.T
    pairs = T // (2 * GROUP)
    B = buckets
    with Phase(nc, name, ["loaded", "own", "onehot", "counted", "prefix", "digit", "own2",
                          "hot", "added", "partial", "read", "total", "rows_ready", "scat0", "scat1"]) as ph:
        s = ph.sems
        scattered = (s["scat0"], s["scat1"])
        edges = ph.sbuf("edges", [P, T, 4])
        key = ph.sbuf("key", [P, T], I32)
        digit = ph.sbuf("digit", [P, T])
        hot = ph.sbuf("hot", [P, 2, 2, B], BF16)
        sums = ph.sbuf("sums", [P, 2, B])
        base = ph.sbuf("base", [P, B])
        product = ph.sbuf("product", [P, 2, B], BF16)
        rank = ph.sbuf("rank", [P, GROUP])
        whole = ph.sbuf("whole", [P, GROUP], I32)
        bits = ph.sbuf("bits", [P, 3, GROUP], I32)
        turned = ph.sbuf("turned", [P, GROUP])
        row = ph.sbuf("row", [P, 2, GROUP], I32)
        moved = ph.sbuf("moved", [P, 2, GROUP, 4])
        count = ph.psum("count", [P, 512])
        running = ph.psum("running", [P, 512])
        block = ph.block()

        def make_hot(tile_pair, slot):
            return nc.vector.tensor_tensor(
                hot[:, slot, :, :], k.iota[:, 0:B].unsqueeze(1).to_broadcast([P, 2, B]),
                spread(digit[:, bass.ds(tile_pair * 2, 2)], B), ALU.is_equal)

        @block.sync
        def _(sp):
            sp.dma_start(edges[:, :, :], unsorted.rearrange("(p t) c -> p t c", p=P)).then_inc(s["loaded"], 16)
            sp.wait_ge(s["loaded"], 16)

        @block.vector
        def _(dve):
            own = Order(dve, s["own"])
            dve.wait_ge(s["loaded"], 16)
            own.step(nc.vector.tensor_copy(key[:, :], edges[:, :, field]))
            own.wait()
            own.step(nc.vector.tensor_scalar(key[:, :], key[:, :], shift, B_MASK(B),
                                             ALU.logical_shift_right, ALU.bitwise_and))
            own.wait()
            own.step(nc.vector.tensor_copy(digit[:, :], key[:, :]))
            own.wait()

            def histogram(i, first, last):
                for g in range(GROUP):
                    if not (first and g < 2):
                        dve.wait_ge(s["counted"], i * GROUP + g - 1)
                    make_hot(i * GROUP + g, g % 2).then_inc(s["onehot"], 1)
            loop(dve, pairs, histogram)

            dve.wait_ge(s["total"], 1)
            own.step(nc.vector.tensor_copy(sums[:, 0, :], count[:, 0:B]))
            at, reach = 0, 1
            while reach < B:
                own.wait()
                own.step(nc.vector.tensor_copy(sums[:, 1 - at, 0:reach], sums[:, at, 0:reach]))
                own.step(nc.vector.tensor_tensor(sums[:, 1 - at, reach:B], sums[:, at, reach:B],
                                                 sums[:, at, 0:B - reach], ALU.add))
                at, reach = 1 - at, reach * 2
            own.wait()
            nc.vector.tensor_tensor(base[:, :], sums[:, at, :], count[:, 0:B], ALU.subtract)\
              .then_inc(s["prefix"], 1)

            def ranks(i, first, last):
                for h in range(2):
                    if not first:
                        dve.wait_ge(scattered[h], i * (16 * GROUP))
                    own.step(nc.vector.tensor_copy(moved[:, h, :, :], edges[:, bass.ds((i * 2 + h) * GROUP, GROUP), :]))
                    for g in range(GROUP):
                        t = h * GROUP + g
                        if t % 2 == 0:
                            if not (first and t < 4):
                                dve.wait_ge(s["added"], i * (2 * GROUP) + t - 2)
                            make_hot(i * GROUP + t // 2, (t // 2) % 2).then_inc(s["hot"], 1)
                            dve.wait_ge(s["hot"], i * GROUP + t // 2 + 1)
                        dve.wait_ge(s["partial"], i * (2 * GROUP) + t + 1)
                        nc.vector.tensor_tensor_reduce(
                            product[:, t % 2, :], running[:, 0:B], hot[:, (t // 2) % 2, t % 2, :], 1.0, 0.0,
                            ALU.mult, ALU.add, rank[:, g:g + 1]).then_inc(s["read"], 1)
                    dve.wait_ge(s["read"], i * (2 * GROUP) + (h + 1) * GROUP)
                    own.step(nc.vector.tensor_copy(whole[:, :], rank[:, :]))
                    own.wait()
                    own.step(nc.vector.tensor_scalar(bits[:, 0, :], whole[:, :], P - 1, None, ALU.bitwise_and))
                    own.step(nc.vector.tensor_scalar(bits[:, 1, :], whole[:, :], 7, None, ALU.logical_shift_right))
                    own.step(nc.vector.tensor_scalar(bits[:, 2, :], whole[:, :], 7, 1,
                                                     ALU.logical_shift_right, ALU.bitwise_and))
                    own.wait()
                    own.step(nc.vector.tensor_scalar(turned[:, :], bits[:, 0, :], -2.0, P - 1.0, ALU.mult, ALU.add))
                    own.wait()
                    own.step(nc.vector.tensor_tensor(turned[:, :], turned[:, :], bits[:, 2, :], ALU.mult))
                    own.wait()
                    own.step(nc.vector.tensor_tensor(turned[:, :], turned[:, :], bits[:, 0, :], ALU.add))
                    own.wait()
                    nc.vector.scalar_tensor_tensor(row[:, h, :], turned[:, :], float(T), bits[:, 1, :],
                                                   ALU.mult, ALU.add).then_inc(s["rows_ready"], 1)
            loop(dve, pairs, ranks, own)

        @block.tensor
        def _(pe):
            nc.tensor.matmul(count[:, 0:B], k.zeros_bf[:, 0:P], k.zeros_bf[:, 0:B], start=True, stop=False)

            def histogram(i, first, last):
                for g in range(GROUP):
                    pe.wait_ge(s["onehot"], i * GROUP + g + 1)
                    nc.tensor.matmul(count[:, 0:B], k.ones_bf[:, :], hot[:, g % 2, 0, :], start=False, stop=False)
                    nc.tensor.matmul(count[:, 0:B], k.ones_bf[:, :], hot[:, g % 2, 1, :], start=False, stop=False)\
                      .then_inc(s["counted"], 1)
            loop(pe, pairs, histogram)
            nc.tensor.matmul(count[:, 0:B], k.zeros_bf[:, 0:P], k.zeros_bf[:, 0:B], start=False, stop=True)\
              .then_inc(s["total"], 1)
            pe.wait_ge(s["prefix"], 1)
            nc.tensor.matmul(running[:, 0:B], k.first_row[:, :], base[:, :], start=True, stop=True)

            def ranks(i, first, last):
                for t in range(2 * GROUP):
                    if t % 2 == 0:
                        pe.wait_ge(s["hot"], i * GROUP + t // 2 + 1)
                    one = hot[:, (t // 2) % 2, t % 2, :]
                    nc.tensor.matmul(running[:, 0:B], k.before[:, t % 2, :], one, start=False, stop=True,
                                     skip_group_check=True)\
                      .then_inc(s["partial"], 1)
                    pe.wait_ge(s["read"], i * (2 * GROUP) + t + 1)
                    nc.tensor.matmul(running[:, 0:B], k.rest[:, t % 2, :], one, start=False, stop=True,
                                     skip_group_check=True)\
                      .then_inc(s["added"], 1)
            loop(pe, pairs, ranks)

        @block.gpsimd
        def _(pool):
            def scatter(i, first, last):
                for h in range(2):
                    pool.wait_ge(s["rows_ready"], i * 2 + h + 1)
                    pool.nop(nofuse=True)
                    for g in range(GROUP):
                        pool.indirect_dma_start(
                            out=by_rank[:, :], out_offset=bass.IndirectOffsetOnAxis(ap=row[:, h, g:g + 1], axis=0),
                            in_=moved[:, h, g, :], in_offset=None).then_inc(scattered[h], 16)
            loop(pool, pairs, scatter)
            for h in range(2):
                pool.wait_ge(scattered[h], pairs * 16 * GROUP)


def B_MASK(buckets):
    return (1 << (buckets - 1).bit_length()) - 1


class Side:

    def __init__(self, name, stack, nc, T):
        def sb(what, shape, dtype=F32):
            return stack.enter_context(nc.sbuf_tensor(f"{name}_{what}", shape, dtype))
        self.name = name
        self.key = sb("key", [P, T])
        self.other = sb("other", [P, T], I32)
        self.carry = sb("carry", [P, T + 1])
        self.end = sb("end", [P, T], I32)
        self.degree = sb("degree", [P, T])
        self.in_last = sb("in_last", [P, T])
        self.last_keys = sb("last_keys", [LASTS, T])
        self.met = sb("met", [P, T, 4])


def edge_pass(nc, k, name, side, finish, width=C, table=None, index=None, weight=None, added=None, scale=None):
    T, W = k.T, width
    pairs = T // (2 * GROUP)
    sems = ["own", "gathered0", "gathered1", "features0", "features1", "staged", "scaled", "keys", "onehot",
            "weighed", "lasts", "carried", "summed", "copied", "pool_own", "targets", "act_own"] + finish.SEMS
    with Phase(nc, name, sems) as ph:
        s = ph.sems
        gathered = (s["gathered0"], s["gathered1"])
        features = (s["features0"], s["features1"])
        rows = ph.sbuf("rows", [P, 2, GROUP, W])
        same = ph.sbuf("same", [P, 2, 4, P])
        follows = ph.sbuf("follows", [LASTS, 2, 4, P])
        picks = ph.sbuf("picks", [P, 2, GROUP, LASTS])
        keys = ph.sbuf("keys", [P, 2, GROUP])
        last_keys = ph.sbuf("last_keys", [LASTS, 2, GROUP])
        lasts = ph.sbuf("lasts", [LASTS, 2, W])
        held = ph.sbuf("held", [1, W])
        sums = ph.sbuf("sums", [P, 2, GROUP, W])
        if scale is not None:
            scales = ph.sbuf("scales", [P, 2, GROUP])
        if table is not None:
            wanted = ph.sbuf("wanted", [P, 2, GROUP], I32)
        if added is not None:
            feats = ph.sbuf("feats", [P, 2, GROUP, W])
            added_rows = added.rearrange("(p t) c -> p t c", p=P)
        turned = [ph.psum(f"turned{n}", [P, 4, P]) for n in range(2)]
        total = [ph.psum(f"total{n}", [P, 4, W]) for n in range(2)]
        lasting = ph.psum("lasting", [LASTS, W])
        ph.edge = dict(side=side, sums=sums, same=same, keys=keys, pairs=pairs)
        finish.buffers(ph, k)
        block = ph.block()

        @block.sync
        def _(sp):
            def body(i, first, last):
                for h in range(2):
                    if added is not None:
                        if not first:
                            sp.wait_ge(s["weighed"], i * 2 + h - 1)
                        sp.dma_start(feats[:, h, :, :], added_rows[:, bass.ds((i * 2 + h) * GROUP, GROUP), :])\
                          .then_inc(features[h], 16)
                    finish.sync(ph, sp, i, h, first)
            loop(sp, pairs, body)
            finish.sync_end(ph, sp)

        @block.gpsimd
        def _(pool):
            own = Order(pool, s["pool_own"])

            def gather(i, h, first):
                if not first:
                    pool.wait_ge(s["summed"], i * 8 + h * 4 - 4)
                own.step(nc.gpsimd.tensor_copy(wanted[:, h, :], index[:, bass.ds((i * 2 + h) * GROUP, GROUP)]))
                own.wait()
                pool.nop(nofuse=True)
                for g in range(GROUP):
                    pool.indirect_dma_start(
                        out=rows[:, h, g, :], out_offset=None, in_=table,
                        in_offset=bass.IndirectOffsetOnAxis(ap=wanted[:, h, g:g + 1], axis=0))\
                        .then_inc(gathered[h], 16)

            if table is not None:
                gather(0, 0, True)

            def body(i, first, last):
                if table is not None:
                    gather(i, 1, first)
                finish.pool(ph, pool, i, 0, first)
                if table is not None and not last:
                    gather(i + 1, 0, False)
                finish.pool(ph, pool, i, 1, first)
            loop(pool, pairs, body, own)
            finish.pool_end(ph, pool)

        @block.vector
        def _(dve):
            own = Order(dve, s["own"])
            own.step(nc.vector.memset(picks[:, :, :, :], 0.0))
            if table is None:
                own.step(nc.vector.memset(rows[:, :, :, :], 1.0))
            own.wait()

            def body(i, first, last):
                for h in range(2):
                    b = i * 2 + h
                    at = bass.ds(b * GROUP, GROUP)
                    if not first:
                        dve.wait_ge(s["summed"], i * 8 + h * 4 - 4)
                    nc.vector.tensor_copy(keys[:, h, :], side.key[:, at]).then_inc(s["staged"], 1)
                    own.step(nc.vector.tensor_copy(last_keys[:, h, :], side.last_keys[:, at]))
                    diagonal = picks[:, h, :, :].rearrange("p g l -> p (g l)")[:, 1:2 + (GROUP - 1) * (LASTS + 1):LASTS + 1]
                    own.step(nc.vector.tensor_copy(diagonal, side.in_last[:, at]))
                    if scale is not None:
                        if not first:
                            dve.wait_ge(s["copied"], i * 8 + h * 4 - 4)
                        nc.vector.tensor_copy(scales[:, h, :], scale[:, at]).then_inc(s["scaled"], 1)
                    if table is not None:
                        dve.wait_ge(gathered[h], i * (16 * GROUP) + 16 * GROUP)
                    if weight is not None:
                        own.step(nc.vector.tensor_tensor(rows[:, h, :, :], rows[:, h, :, :],
                                                         spread(weight[:, at], W), ALU.mult))
                    if added is not None:
                        dve.wait_ge(features[h], i * 16 + 16)
                        own.step(nc.vector.tensor_tensor(rows[:, h, :, :], rows[:, h, :, :],
                                                         feats[:, h, :, :], ALU.add))
                        own.wait()
                        own.step(nc.vector.tensor_scalar(rows[:, h, :, :], rows[:, h, :, :], 0.0, None, ALU.max))
                    own.wait()
                    dve.sem_inc(s["weighed"], 1)

                    for q, (g0, n) in enumerate(QUADS):
                        dve.wait_ge(s["keys"], i * 8 + h * 4 + q + 1)
                        if not (first and h == 0 and q < 2):
                            dve.wait_ge(s["summed"], i * 8 + h * 4 + q - 1)
                        nc.vector.tensor_tensor(same[:, q % 2, 0:n, :], turned[q % 2][:, 0:n, :],
                                                spread(keys[:, h, g0:g0 + n], P), ALU.is_equal)\
                          .then_inc(s["onehot"], 1)
                        nc.vector.tensor_tensor(follows[:, q % 2, 0:n, :], turned[q % 2][0:LASTS, 0:n, :],
                                                last_keys[:, h, g0:g0 + n].unsqueeze(2).to_broadcast([LASTS, n, P]),
                                                ALU.is_equal).then_inc(s["onehot"], 1)
                        finish.quad(ph, dve, own, i, h, q, g0, n)
                    finish.vector(ph, dve, own, i, h, first)
            loop(dve, pairs, body, own)

        @block.tensor
        def _(pe):
            def turn(i, h, q, first):
                g0, n = QUADS[q]
                if q == 0:
                    pe.wait_ge(s["staged"], i * 2 + h + 1)
                if not (first and h == 0 and q < 2):
                    pe.wait_ge(s["onehot"], i * 16 + h * 8 + 2 * q - 2)
                for g in range(g0, g0 + n):
                    ins = nc.tensor.transpose(turned[q % 2][:, g - g0, :], keys[:, h, g:g + 1].to_broadcast([P, P]),
                                              k.ident[:, :])
                ins.then_inc(s["keys"], 1)

            def body(i, first, last):
                for h in range(2):
                    turn(i, h, 0, first)
                    turn(i, h, 1, first)
                    pe.wait_ge(s["weighed"], i * 2 + h + 1)
                    if not (first and h == 0):
                        pe.wait_ge(s["carried"], i * 2 + h)
                    for g in range(GROUP):
                        ins = nc.tensor.matmul(lasting[:, :], picks[:, h, g, :], rows[:, h, g, :],
                                               start=(g == 0), stop=(g == GROUP - 1))
                    ins.then_inc(s["lasts"], 1)
                    for q, (g0, n) in enumerate(QUADS):
                        pe.wait_ge(s["onehot"], i * 16 + h * 8 + 2 * q + 2)
                        if q == 0:
                            pe.wait_ge(s["carried"], i * 2 + h + 1)
                        if not (first and h == 0 and q < 2):
                            pe.wait_ge(s["copied"], i * 8 + h * 4 + q - 1)
                        for g in range(g0, g0 + n):
                            nc.tensor.matmul(total[q % 2][:, g - g0, :], same[:, q % 2, g - g0, :], rows[:, h, g, :],
                                             start=True, stop=False)
                            ins = nc.tensor.matmul(total[q % 2][:, g - g0, :], follows[:, q % 2, g - g0, :],
                                                   lasts[:, h, :], start=False, stop=True)
                        ins.then_inc(s["summed"], 1)
                        if q + 2 < len(QUADS):
                            turn(i, h, q + 2, first)
                    finish.tensor(ph, pe, i, h, first)
            loop(pe, pairs, body)

        @block.scalar
        def _(act):
            own = Order(act, s["act_own"])
            own.step(nc.scalar.activation(held[:, :], k.zeros_f[0:1, 0:W], ACT.Copy))

            def body(i, first, last):
                for h in range(2):
                    act.wait_ge(s["lasts"], i * 2 + h + 1)
                    own.wait()
                    own.step(nc.scalar.activation(lasts[:, h, :], lasting[:, :], ACT.Copy))
                    own.wait()
                    nc.scalar.activation(lasts[0:1, h, :], held[:, :], ACT.Copy).then_inc(s["carried"], 1)
                    if scale is not None:
                        act.wait_ge(s["scaled"], i * 2 + h + 1)
                    finish.slot_free(ph, act, i, h, first)
                    for q, (g0, n) in enumerate(QUADS):
                        act.wait_ge(s["summed"], i * 8 + h * 4 + q + 1)
                        if q == len(QUADS) - 1:
                            act.wait_ge(s["carried"], i * 2 + h + 1)
                            own.step(nc.scalar.activation(held[:, :], total[q % 2][0:1, n - 1, :], ACT.Copy))
                        if scale is None:
                            nc.scalar.activation(sums[:, h, g0:g0 + n, :], total[q % 2][:, 0:n, :], ACT.Copy)\
                              .then_inc(s["copied"], 1)
                            continue
                        for g in range(g0, g0 + n):
                            ins = nc.scalar.activation(sums[:, h, g, :], total[q % 2][:, g - g0, :], ACT.Copy,
                                                       scale=scales[:, h, g:g + 1])
                        ins.then_inc(s["copied"], 1)
                    finish.scalar(ph, act, own, i, h, first)
            loop(act, pairs, body, own)


class Finish:
    SEMS = []

    def buffers(self, ph, k): pass
    def sync(self, ph, sp, i, h, first): pass
    def sync_end(self, ph, sp): pass
    def pool(self, ph, pool, i, h, first): pass
    def pool_end(self, ph, pool): pass
    def quad(self, ph, dve, own, i, h, q, g0, n): pass
    def vector(self, ph, dve, own, i, h, first): pass
    def tensor(self, ph, pe, i, h, first): pass
    def slot_free(self, ph, act, i, h, first): pass
    def scalar(self, ph, act, own, i, h, first): pass


class Store(Finish):
    SEMS = ["stored0", "stored1", "residual0", "residual1", "finished"]

    def __init__(self, nc, out, residual=None):
        self.nc, self.out, self.residual = nc, out.rearrange("(p t) c -> p t c", p=P), residual
        if residual is not None:
            self.residual = residual.rearrange("(p t) c -> p t c", p=P)

    def buffers(self, ph, k):
        if self.residual is not None:
            self.res = ph.sbuf("res", [P, 2, GROUP, C])

    def sync(self, ph, sp, i, h, first):
        s = ph.sems
        b = i * 2 + h
        if self.residual is not None:
            if not first:
                sp.wait_ge(s["finished"], b - 1)
            sp.dma_start(self.res[:, h, :, :], self.residual[:, bass.ds(b * GROUP, GROUP), :])\
              .then_inc(s[f"residual{h}"], 16)
            sp.wait_ge(s["finished"], b + 1)
        else:
            sp.wait_ge(s["copied"], b * 4 + 4)
        sp.dma_start(self.out[:, bass.ds(b * GROUP, GROUP), :], ph.edge["sums"][:, h, :, :]).then_inc(s[f"stored{h}"], 16)

    def sync_end(self, ph, sp):
        for h in range(2):
            sp.wait_ge(ph.sems[f"stored{h}"], 16 * ph.edge["pairs"])

    def vector(self, ph, dve, own, i, h, first):
        if self.residual is not None:
            s, sums = ph.sems, ph.edge["sums"]
            dve.wait_ge(s["copied"], (i * 2 + h) * 4 + 4)
            dve.wait_ge(s[f"residual{h}"], i * 16 + 16)
            self.nc.vector.scalar_tensor_tensor(sums[:, h, :, :], self.res[:, h, :, :], ALPHA, sums[:, h, :, :],
                                                ALU.mult, ALU.add).then_inc(s["finished"], 1)

    def slot_free(self, ph, act, i, h, first):
        if not first:
            act.wait_ge(ph.sems[f"stored{h}"], i * 16)


class Scatter(Finish):
    SEMS = ["scattered0", "scattered1"]

    def __init__(self, nc, k, out, end):
        self.nc, self.k, self.out, self.end = nc, k, out, end

    def buffers(self, ph, k):
        self.target = ph.sbuf("target", [P, 2, GROUP], I32)

    def pool(self, ph, pool, i, h, first):
        s = ph.sems
        b = i * 2 + h
        if not first:
            pool.wait_ge(s[f"scattered{h}"], i * (16 * GROUP))
        self.nc.gpsimd.tensor_copy(self.target[:, h, :], self.end[:, bass.ds(b * GROUP, GROUP)])\
            .then_inc(s["targets"], 1)
        pool.wait_ge(s["targets"], b + 1)
        self.ready(ph, pool, b)
        pool.nop(nofuse=True)
        for g in range(GROUP):
            pool.indirect_dma_start(
                out=self.out, out_offset=bass.IndirectOffsetOnAxis(ap=self.target[:, h, g:g + 1], axis=0),
                in_=self.rows(ph, h, g), in_offset=None, bounds_check=self.k.N - 1, oob_is_err=False)\
                .then_inc(s[f"scattered{h}"], 16)

    def ready(self, ph, pool, b):
        pool.wait_ge(ph.sems["copied"], b * 4 + 4)

    def rows(self, ph, h, g):
        return ph.edge["sums"][:, h, g, :]

    def pool_end(self, ph, pool):
        for h in range(2):
            pool.wait_ge(ph.sems[f"scattered{h}"], 16 * GROUP * ph.edge["pairs"])

    def slot_free(self, ph, act, i, h, first):
        if not first:
            act.wait_ge(ph.sems[f"scattered{h}"], i * (16 * GROUP))


class MapNodes(Finish):
    SEMS = ["scattered0", "scattered1", "rows_ready", "compared"]

    def __init__(self, nc, k, side, out):
        self.nc, self.k, self.side, self.out = nc, k, side, out

    def buffers(self, ph, k):
        self.after = ph.sbuf("after", [P, 4, P])
        self.later = ph.sbuf("later", [P, GROUP])
        self.target = ph.sbuf("target", [P, 2, GROUP], I32)
        self.entry = ph.sbuf("entry", [P, 2, GROUP, 2])

    def quad(self, ph, dve, own, i, h, q, g0, n):
        nc, s = self.nc, ph.sems
        dve.wait_ge(s["onehot"], i * 16 + h * 8 + 2 * q + 2)
        own.step(nc.vector.tensor_tensor(
            self.after[:, 0:n, :].rearrange("p (a b) q -> p a b q", b=2),
            ph.edge["same"][:, q % 2, 0:n, :].rearrange("p (a b) q -> p a b q", b=2),
            self.k.later[:, :, :].unsqueeze(1).to_broadcast([P, n // 2, 2, P]), ALU.mult))
        own.wait()
        own.step(nc.vector.tensor_reduce(self.later[:, g0:g0 + n], self.after[:, 0:n, :], AX_X, ALU.add))

    def vector(self, ph, dve, own, i, h, first):
        nc, s, side = self.nc, ph.sems, self.side
        b = i * 2 + h
        at = bass.ds(b * GROUP, GROUP)
        own.wait()
        if not first:
            dve.wait_ge(s[f"scattered{h}"], i * (16 * GROUP))
        own.step(nc.vector.tensor_tensor(self.later[:, :], self.later[:, :],
                                         side.carry[:, bass.ds(b * GROUP + 1, GROUP)], ALU.add))
        own.wait()
        own.step(nc.vector.scalar_tensor_tensor(self.target[:, h, :], self.later[:, :], float(NOWHERE),
                                                ph.edge["keys"][:, h, :], ALU.mult, ALU.add))
        own.step(nc.vector.tensor_copy(self.entry[:, h, :, 0], self.k.edge_row[:, at]))
        dve.wait_ge(s["copied"], b * 4 + 4)
        own.step(nc.vector.tensor_copy(self.entry[:, h, :, 1], ph.edge["sums"][:, h, :, 0]))
        own.wait()
        own.step(nc.vector.tensor_copy(side.end[:, at], self.target[:, h, :]))
        own.step(nc.vector.tensor_copy(side.degree[:, at], self.entry[:, h, :, 1]))
        own.wait()
        dve.sem_inc(s["rows_ready"], 1)

    def slot_free(self, ph, act, i, h, first):
        if not first:
            act.wait_ge(ph.sems["rows_ready"], i * 2 + h - 1)

    def pool(self, ph, pool, i, h, first):
        pool.wait_ge(ph.sems["rows_ready"], i * 2 + h + 1)
        pool.nop(nofuse=True)
        for g in range(GROUP):
            pool.indirect_dma_start(
                out=self.out, out_offset=bass.IndirectOffsetOnAxis(ap=self.target[:, h, g:g + 1], axis=0),
                in_=self.entry[:, h, g, :], in_offset=None, bounds_check=self.k.N - 1, oob_is_err=False)\
                .then_inc(ph.sems[f"scattered{h}"], 16)

    def pool_end(self, ph, pool):
        for h in range(2):
            pool.wait_ge(ph.sems[f"scattered{h}"], 16 * GROUP * ph.edge["pairs"])


def load_side(nc, k, side, table, field, weight=None):
    T = k.T
    nb = T // GROUP
    with Phase(nc, f"load_{side.name}", ["loaded", "own", "keyed", "spread"]) as ph:
        s = ph.sems
        edges = ph.sbuf("edges", [P, T, 4])
        masked = ph.sbuf("masked", [LASTS, nb, GROUP])
        picked = ph.sbuf("picked", [LASTS, nb])
        shifted = ph.sbuf("shifted", [LASTS, nb])
        last_key = ph.psum("last_key", [P, T])
        block = ph.block()

        @block.sync
        def _(sp):
            sp.dma_start(edges[:, :, :], table.rearrange("(p t) c -> p t c", p=P)).then_inc(s["loaded"], 16)
            sp.wait_ge(s["loaded"], 16)

        @block.vector
        def _(dve):
            own = Order(dve, s["own"])
            own.step(nc.vector.memset(side.carry[:, :], 0.0))
            dve.wait_ge(s["loaded"], 16)
            own.step(nc.vector.tensor_copy(side.key[:, :], edges[:, :, field]))
            own.step(nc.vector.tensor_copy(side.other[:, :], edges[:, :, 1 - field]))
            if weight is not None:
                own.step(nc.vector.tensor_copy(weight[:, :], edges[:, :, 2]))
            own.wait()
            own.step(nc.vector.tensor_tensor(side.carry[:, 1:T], side.key[:, 1:T], side.key[:, 0:T - 1], ALU.is_equal))
            own.wait()
            even = side.carry[:, 0:T].rearrange("p (a b) -> p a b", b=2)
            own.step(nc.vector.tensor_tensor(even, even, k.edge_rows[:, :].unsqueeze(1).to_broadcast([P, T // 2, 2]),
                                             ALU.mult))
            own.wait()
            dve.sem_inc(s["keyed"], 1)
            dve.wait_ge(s["spread"], 1)
            own.step(nc.vector.tensor_tensor(side.in_last[:, :], side.key[:, :], last_key[:, :], ALU.is_equal))
            own.step(nc.vector.tensor_tensor(masked[:, :, :], last_key[0:LASTS, :].rearrange("p (b g) -> p b g", g=GROUP),
                                             k.pick_row[:, :].unsqueeze(1).to_broadcast([LASTS, nb, GROUP]), ALU.mult))
            own.wait()
            own.step(nc.vector.tensor_reduce(picked[:, :], masked[:, :, :], AX_X, ALU.add))
            own.wait()
            own.step(nc.vector.tensor_scalar(shifted[:, :], picked[:, :], 1.0, None, ALU.add))
            own.wait()
            own.step(nc.vector.tensor_scalar(shifted[0:1, 1:nb], picked[0:1, 0:nb - 1], 1.0, None, ALU.add))
            own.step(nc.vector.memset(shifted[0:1, 0:1], 0.0))
            own.wait()
            own.step(nc.vector.tensor_tensor(
                side.last_keys[:, :].rearrange("p (b g) -> p b g", g=GROUP),
                shifted[:, :].unsqueeze(2).to_broadcast([LASTS, nb, GROUP]),
                k.after_row[:, :].unsqueeze(1).to_broadcast([LASTS, nb, GROUP]), ALU.mult))
            own.wait()
            own.step(nc.vector.tensor_scalar(side.last_keys[:, :], side.last_keys[:, :], -1.0, None, ALU.add))
            own.wait()

        @block.tensor
        def _(pe):
            pe.wait_ge(s["keyed"], 1)
            for odd in range(2):
                ins = nc.tensor.matmul(last_key[:, odd:T:2], (k.first_row if odd else k.final_row)[:, :],
                                       side.key[:, odd:T:2], start=(odd == 0), stop=(odd == 1), skip_group_check=True)
            ins.then_inc(s["spread"], 1)


def fill_rows(nc, k, name, fills):
    with Phase(nc, name, ["made", "stored"]) as ph:
        made, stored = ph.sems["made"], ph.sems["stored"]
        tiles = []
        for n, (table, values) in enumerate(fills):
            rows = table.shape[0] // P
            per = max(d for d in range(1, rows + 1) if rows % d == 0 and d * table.shape[1] <= 4096)
            tiles.append((ph.sbuf(f"tile{n}", [P, per, table.shape[1]]), per, rows // per, values))
        block = ph.block()

        @block.vector
        def _(dve):
            n = 0
            for tile, per, times, values in tiles:
                for c, value in enumerate(values):
                    whole = tile[:, :, :] if len(values) == 1 else tile[:, :, c:c + 1]
                    nc.vector.memset(whole, value).then_inc(made, 1)
                    n += 1
            dve.wait_ge(made, n)

        @block.sync
        def _(sp):
            sp.wait_ge(made, sum(len(values) for _, values in fills))
            n = 0
            for (table, _), (tile, per, times, _) in zip(fills, tiles):
                for m in range(times):
                    sp.dma_start(table[m * per * P:(m + 1) * per * P, :].rearrange("(p t) c -> p t c", p=P),
                                 tile[:, :, :]).then_inc(stored, 16)
                    n += 16
            sp.wait_ge(stored, n)


def join_maps(nc, k, by_src, by_dst, joined):
    n = k.NP // P
    with Phase(nc, "join", ["loaded", "joined", "stored"]) as ph:
        s = ph.sems
        one = ph.sbuf("one", [P, n, 2])
        two = ph.sbuf("two", [P, n, 2])
        both = ph.sbuf("both", [P, n, 4])
        block = ph.block()

        @block.sync
        def _(sp):
            sp.dma_start(one[:, :, :], by_src.rearrange("(p t) c -> p t c", p=P)).then_inc(s["loaded"], 16)
            sp.dma_start(two[:, :, :], by_dst.rearrange("(p t) c -> p t c", p=P)).then_inc(s["loaded"], 16)
            sp.wait_ge(s["joined"], 2)
            sp.dma_start(joined.rearrange("(p t) c -> p t c", p=P), both[:, :, :]).then_inc(s["stored"], 16)
            sp.wait_ge(s["stored"], 16)

        @block.vector
        def _(dve):
            dve.wait_ge(s["loaded"], 32)
            nc.vector.tensor_copy(both[:, :, 0:2], one[:, :, :]).then_inc(s["joined"], 1)
            nc.vector.tensor_copy(both[:, :, 2:4], two[:, :, :]).then_inc(s["joined"], 1)


def gather_map(nc, k, side, joined):
    pairs = k.T // (2 * GROUP)
    with Phase(nc, f"met_{side.name}", ["own", "g0", "g1", "kept"]) as ph:
        s = ph.sems
        gathered = (s["g0"], s["g1"])
        wanted = ph.sbuf("wanted", [P, 2, GROUP], I32)
        got = ph.sbuf("got", [P, 2, GROUP, 4])
        block = ph.block()

        @block.gpsimd
        def _(pool):
            own = Order(pool, s["own"])

            def body(i, first, last):
                for h in range(2):
                    if not first:
                        pool.wait_ge(s["kept"], i * 2 + h - 1)
                    own.step(nc.gpsimd.tensor_copy(wanted[:, h, :], side.other[:, bass.ds((i * 2 + h) * GROUP, GROUP)]))
                    own.wait()
                    pool.nop(nofuse=True)
                    for g in range(GROUP):
                        pool.indirect_dma_start(
                            out=got[:, h, g, :], out_offset=None, in_=joined,
                            in_offset=bass.IndirectOffsetOnAxis(ap=wanted[:, h, g:g + 1], axis=0))\
                            .then_inc(gathered[h], 16)
            loop(pool, pairs, body, own)

        @block.vector
        def _(dve):
            def body(i, first, last):
                for h in range(2):
                    dve.wait_ge(gathered[h], i * (16 * GROUP) + 16 * GROUP)
                    nc.vector.tensor_copy(side.met[:, bass.ds((i * 2 + h) * GROUP, GROUP), :], got[:, h, :, :])\
                      .then_inc(s["kept"], 1)
            loop(dve, pairs, body)


def norm_buffers(ph):
    return (ph.sbuf("stats", [P, GROUP, 6]), ph.sbuf("moments", [P, 2, GROUP, 2]),
            ph.sbuf("spread", [P, 2, GROUP]), ph.sbuf("inverse", [P, 2, GROUP]), ph.sbuf("shift", [P, 2, GROUP]),
            ph.sbuf("varied", [P, 2, GROUP]))


NORM_SEMS = ["moments", "spread", "coefficients", "normed"]


def norm_vector(nc, ph, dve, own, bufs, rows, b, h):
    s = ph.sems
    stats, moments, deviation, inverse, shift, varied = bufs
    for g in range(GROUP):
        own.step(nc.vector.bn_stats(stats[:, g, :], rows[:, g, :]))
    own.wait()
    dve.nop(nofuse=True)
    for g in range(GROUP):
        own.step(nc.vector.bn_aggr(moments[:, h, g, :], stats[:, g, :]))
    own.wait()
    nc.vector.tensor_scalar(varied[:, h, :], moments[:, h, :, 1], LN_EPS, None, ALU.add).then_inc(s["moments"], 1)
    dve.wait_ge(s["spread"], b + 1)
    own.step(nc.vector.reciprocal(inverse[:, h, :], deviation[:, h, :]))
    own.wait()
    nc.vector.scalar_tensor_tensor(shift[:, h, :], moments[:, h, :, 0], -1.0, inverse[:, h, :],
                                   ALU.mult, ALU.mult).then_inc(s["coefficients"], 1)


def norm_root(nc, ph, act, bufs, b, h):
    act.wait_ge(ph.sems["moments"], b + 1)
    nc.scalar.activation(bufs[2][:, h, :], bufs[5][:, h, :], ACT.Sqrt).then_inc(ph.sems["spread"], 1)


def norm_apply(nc, ph, act, bufs, rows, out, b, h):
    act.wait_ge(ph.sems["coefficients"], b + 1)
    for g in range(GROUP):
        ins = nc.scalar.activation(out[:, g, :], rows[:, g, :], ACT.Identity,
                                   bias=bufs[4][:, h, g:g + 1], scale=bufs[3][:, h, g:g + 1])
    ins.then_inc(ph.sems["normed"], 1)


class NormScatter(Scatter):
    SEMS = Scatter.SEMS + NORM_SEMS + ["residual0", "residual1", "propagated", "mixed"]

    def __init__(self, nc, k, out, end, residual):
        super().__init__(nc, k, out, end)
        self.residual = residual.rearrange("(p t) c -> p t c", p=P)

    def buffers(self, ph, k):
        super().buffers(ph, k)
        self.norm = norm_buffers(ph)
        self.res = ph.sbuf("res", [P, 2, GROUP, C])
        self.normed = ph.sbuf("normed", [P, 2, GROUP, C])

    def sync(self, ph, sp, i, h, first):
        if not first:
            sp.wait_ge(ph.sems["mixed"], i * 2 + h - 1)
        sp.dma_start(self.res[:, h, :, :], self.residual[:, bass.ds((i * 2 + h) * GROUP, GROUP), :])\
          .then_inc(ph.sems[f"residual{h}"], 16)

    def vector(self, ph, dve, own, i, h, first):
        nc, s, sums = self.nc, ph.sems, ph.edge["sums"]
        b = i * 2 + h
        dve.wait_ge(s["copied"], b * 4 + 4)
        dve.wait_ge(s[f"residual{h}"], i * 16 + 16)
        own.step(nc.vector.scalar_tensor_tensor(sums[:, h, :, :], self.res[:, h, :, :], ALPHA, sums[:, h, :, :],
                                                ALU.mult, ALU.add))
        own.wait()
        nc.vector.scalar_tensor_tensor(sums[:, h, :, :], sums[:, h, :, :], 1.0 / THETA, self.res[:, h, :, :],
                                       ALU.mult, ALU.add).then_inc(s["mixed"], 1)
        dve.wait_ge(s["mixed"], b + 1)
        norm_vector(nc, ph, dve, own, self.norm, sums[:, h], b, h)

    def scalar(self, ph, act, own, i, h, first):
        b = i * 2 + h
        norm_root(self.nc, ph, act, self.norm, b, h)
        if not first:
            act.wait_ge(ph.sems[f"scattered{h}"], i * (16 * GROUP))
        norm_apply(self.nc, ph, act, self.norm, ph.edge["sums"][:, h], self.normed[:, h], b, h)

    def slot_free(self, ph, act, i, h, first):
        if not first:
            act.wait_ge(ph.sems["normed"], i * 2 + h - 1)

    def ready(self, ph, pool, b):
        pool.wait_ge(ph.sems["normed"], b + 1)

    def rows(self, ph, h, g):
        return self.normed[:, h, g, :]


class MixHops(Scatter):
    SEMS = Scatter.SEMS + ["hops0", "hops1", "hop_turned", "hop_copied", "mixed", "mixed_out"]

    def __init__(self, nc, k, out, end, hop1, hop2, folded):
        super().__init__(nc, k, out, end)
        self.hops = [hop.rearrange("(p t) c -> p t c", p=P) for hop in (hop1, hop2)]
        self.folded = folded

    def buffers(self, ph, k):
        super().buffers(ph, k)
        self.loaded = ph.sbuf("hops", [P, 2, 2, GROUP, C])
        self.turned = ph.sbuf("hops_turned", [C, 2, 3, P])
        self.mixed = ph.sbuf("mixed", [P, 2, GROUP, MIX])
        self.turning = ph.psum("turning", [C, 3, P])
        self.mixing = ph.psum("mixing", [P, 512])

    def sync(self, ph, sp, i, h, first):
        s = ph.sems
        if not first:
            sp.wait_ge(s["mixed"], i * (2 * GROUP) + (h - 1) * GROUP)
        for j in range(2):
            sp.dma_start(self.loaded[:, h, j, :, :], self.hops[j][:, bass.ds((i * 2 + h) * GROUP, GROUP), :])\
              .then_inc(s[f"hops{h}"], 16)

    def tensor(self, ph, pe, i, h, first):
        nc, s = self.nc, ph.sems
        pe.wait_ge(s[f"hops{h}"], i * 32 + 32)
        pe.wait_ge(s["copied"], (i * 2 + h) * 4 + 4)
        for g in range(GROUP):
            t = h * GROUP + g
            if not (first and t == 0):
                pe.wait_ge(s["hop_copied"], i * (2 * GROUP) + t)
            for j in range(3):
                source = self.loaded[:, h, j, g, :] if j < 2 else ph.edge["sums"][:, h, g, :]
                ins = nc.tensor.transpose(self.turning[:, j, :], source, self.k.ident[:, :])
            ins.then_inc(s["hop_turned"], 1)
            pe.wait_ge(s["hop_copied"], i * (2 * GROUP) + t + 1)
            if not (first and t == 0):
                pe.wait_ge(s["mixed_out"], i * (2 * GROUP) + t)
            for j in range(3):
                ins = nc.tensor.matmul(self.mixing[:, 0:MIX], self.turned[:, t % 2, j, :],
                                       self.folded[0:C, j + 1, :], start=(j == 0), stop=(j == 2))
            ins.then_inc(s["mixed"], 1)

    def scalar(self, ph, act, own, i, h, first):
        nc, s = self.nc, ph.sems
        if not first:
            act.wait_ge(s[f"scattered{h}"], i * (16 * GROUP))
        for g in range(GROUP):
            t = h * GROUP + g
            act.wait_ge(s["hop_turned"], i * (2 * GROUP) + t + 1)
            nc.scalar.activation(self.turned[:, t % 2, :, :], self.turning[:, :, :], ACT.Copy).then_inc(s["hop_copied"], 1)
            act.wait_ge(s["mixed"], i * (2 * GROUP) + t + 1)
            nc.scalar.activation(self.mixed[:, h, g, :], self.mixing[:, 0:MIX], ACT.Copy).then_inc(s["mixed_out"], 1)

    def slot_free(self, ph, act, i, h, first):
        if not first:
            act.wait_ge(ph.sems["mixed"], i * (2 * GROUP) + (h - 1) * GROUP)

    def ready(self, ph, pool, b):
        pool.wait_ge(ph.sems["mixed_out"], b * GROUP + GROUP)

    def rows(self, ph, h, g):
        return self.mixed[:, h, g, :]


MIX = 3 * C + 4


def prepare(nc, k, src, dst):
    with Phase(nc, "prepare", ["own", "rooted", "degrees"]) as ph:
        s = ph.sems
        T = k.T
        deg = ph.sbuf("deg", [P, 6, T])
        root = ph.sbuf("root", [P, 6, T])
        inv = ph.sbuf("inv", [P, 6, T])
        lost = ph.sbuf("lost", [P, T])
        place = ph.sbuf("place", [P, T])
        block = ph.block()

        @block.vector
        def _(dve):
            own = Order(dve, s["own"])
            own.step(nc.vector.tensor_scalar(k.from_x[:, :], src.other[:, :], float(k.N - 1), None, ALU.min))
            own.step(nc.vector.tensor_scalar(k.key_x[:, :], src.key[:, :], float(k.N - 1), None, ALU.min))
            own.step(nc.vector.tensor_scalar(deg[:, 0, :], src.met[:, :, 3], 1.0, None, ALU.max))
            own.step(nc.vector.tensor_scalar(deg[:, 1, :], src.degree[:, :], 1.0, None, ALU.max))
            own.step(nc.vector.tensor_scalar(deg[:, 2, :], dst.met[:, :, 3], 1.0, None, ALU.add))
            own.step(nc.vector.tensor_scalar(deg[:, 3, :], dst.degree[:, :], 1.0, None, ALU.add))
            own.step(nc.vector.tensor_scalar(deg[:, 4, :], dst.met[:, :, 1], 1.0, None, ALU.max))
            own.wait()
            dve.sem_inc(s["degrees"], 1)
            dve.wait_ge(s["rooted"], 1)
            own.step(nc.vector.reciprocal(inv[:, 0:5, :], root[:, 0:5, :]))
            own.wait()
            own.step(nc.vector.tensor_scalar(k.w_hop[:, :], inv[:, 0, :], BETA, None, ALU.mult))
            own.step(nc.vector.tensor_copy(k.s_hop[:, :], inv[:, 1, :]))
            own.step(nc.vector.tensor_copy(k.w_gcn[:, :], inv[:, 2, :]))
            own.step(nc.vector.tensor_copy(k.s_gcn[:, :], inv[:, 3, :]))
            own.step(nc.vector.tensor_scalar(lost[:, :], dst.met[:, :, 1], 0.0, None, ALU.is_gt))
            own.wait()
            own.step(nc.vector.tensor_tensor(k.w_cheb[:, :], inv[:, 4, :], lost[:, :], ALU.mult))
            own.wait()
            own.step(nc.vector.scalar_tensor_tensor(k.w_cheb2[:, :], k.w_cheb[:, :], -1.0, k.w_cheb[:, :],
                                                    ALU.mult, ALU.mult))
            own.step(nc.vector.tensor_scalar(lost[:, :], dst.met[:, :, 2], 0.0, float(k.EP + 1), ALU.is_lt, ALU.mult))
            own.wait()
            own.step(nc.vector.tensor_tensor(k.i_cheb[:, :], dst.met[:, :, 2], lost[:, :], ALU.add))
            own.wait()
            own.step(nc.vector.tensor_scalar(lost[:, :], src.met[:, :, 0], 0.0, None, ALU.is_lt))
            own.step(nc.vector.tensor_scalar(place[:, :], src.other[:, :], float(k.EP + 1), None, ALU.add))
            own.wait()
            own.step(nc.vector.tensor_tensor(place[:, :], place[:, :], lost[:, :], ALU.mult))
            own.wait()
            own.step(nc.vector.tensor_tensor(k.i_odd[:, :], place[:, :], src.met[:, :, 0], ALU.add))
            own.step(nc.vector.tensor_scalar(lost[:, :], lost[:, :], -float(k.EP + k.NP), float(k.EP + k.NP),
                                             ALU.mult, ALU.add))
            own.wait()
            own.step(nc.vector.tensor_tensor(place[:, :], place[:, :], lost[:, :], ALU.add))
            own.wait()
            own.step(nc.vector.tensor_tensor(k.i_even[:, :], place[:, :], src.met[:, :, 0], ALU.add))
            own.wait()

        @block.scalar
        def _(act):
            act.wait_ge(s["degrees"], 1)
            nc.scalar.activation(root[:, 0:5, :], deg[:, 0:5, :], ACT.Sqrt).then_inc(s["rooted"], 1)


def gather_rows(nc, k, name, table, index, out):
    pairs = k.T // (2 * GROUP)
    out_rows = out.rearrange("(p t) c -> p t c", p=P)
    with Phase(nc, name, ["own", "g0", "g1", "s0", "s1"]) as ph:
        s = ph.sems
        gathered, stored = (s["g0"], s["g1"]), (s["s0"], s["s1"])
        wanted = ph.sbuf("wanted", [P, 2, GROUP], I32)
        got = ph.sbuf("got", [P, 2, GROUP, C])
        block = ph.block()

        @block.gpsimd
        def _(pool):
            own = Order(pool, s["own"])

            def body(i, first, last):
                for h in range(2):
                    if not first:
                        pool.wait_ge(stored[h], i * 16)
                    own.step(nc.gpsimd.tensor_copy(wanted[:, h, :], index[:, bass.ds((i * 2 + h) * GROUP, GROUP)]))
                    own.wait()
                    pool.nop(nofuse=True)
                    for g in range(GROUP):
                        pool.indirect_dma_start(
                            out=got[:, h, g, :], out_offset=None, in_=table,
                            in_offset=bass.IndirectOffsetOnAxis(ap=wanted[:, h, g:g + 1], axis=0))\
                            .then_inc(gathered[h], 16)
            loop(pool, pairs, body, own)

        @block.sync
        def _(sp):
            def body(i, first, last):
                for h in range(2):
                    sp.wait_ge(gathered[h], i * (16 * GROUP) + 16 * GROUP)
                    sp.dma_start(out_rows[:, bass.ds((i * 2 + h) * GROUP, GROUP), :], got[:, h, :, :])\
                      .then_inc(stored[h], 16)
            loop(sp, pairs, body)
            for h in range(2):
                sp.wait_ge(stored[h], 16 * pairs)


def edge_features(nc, k, W0, b0, W1, b1, out):
    pairs = k.T // (2 * GROUP)
    out_rows = out.rearrange("(p t) c -> p t c", p=P)
    with Phase(nc, "features", ["loaded", "staged", "turned", "relu", "product", "biased", "s0", "s1"]) as ph:
        s = ph.sems
        stored = (s["s0"], s["s1"])
        w0 = ph.sbuf("w0", [C, 1])
        c0 = ph.sbuf("c0", [C, 1])
        w1 = ph.sbuf("w1", [C, C])
        c1 = ph.sbuf("c1", [P, C])
        weights = ph.sbuf("weights", [P, 2, GROUP])
        hidden = ph.sbuf("hidden", [C, 2, 4, P])
        made = ph.sbuf("made", [P, 2, GROUP, C])
        turned = [ph.psum(f"turned{n}", [C, 4, P]) for n in range(2)]
        product = [ph.psum(f"product{n}", [P, 4, C]) for n in range(2)]
        block = ph.block()

        @block.sync
        def _(sp):
            with nc.allow_non_contiguous_dma(reason="one column of 96"):
                sp.dma_start(w0[:, :], W0.rearrange("o c -> c o")).then_inc(s["loaded"], 16)
                sp.dma_start(c0[:, :], b0.rearrange("(c o) -> c o", o=1)).then_inc(s["loaded"], 16)
            sp.dma_start(w1[:, :], W1).then_inc(s["loaded"], 16)
            sp.dma_start(c1[:, :], b1.rearrange("(o c) -> o c", o=1).to_broadcast([P, C])).then_inc(s["loaded"], 16)

            def body(i, first, last):
                for h in range(2):
                    sp.wait_ge(s["biased"], i * 8 + h * 4 + 4)
                    sp.dma_start(out_rows[:, bass.ds((i * 2 + h) * GROUP, GROUP), :], made[:, h, :, :])\
                      .then_inc(stored[h], 16)
            loop(sp, pairs, body)
            for h in range(2):
                sp.wait_ge(stored[h], 16 * pairs)

        @block.vector
        def _(dve):
            dve.wait_ge(s["loaded"], 64)

            def body(i, first, last):
                for h in range(2):
                    if not first:
                        dve.wait_ge(s["turned"], i * 8 + h * 4 - 4)
                        dve.wait_ge(stored[h], i * 16)
                    nc.vector.tensor_copy(weights[:, h, :], k.edge_weight[:, bass.ds((i * 2 + h) * GROUP, GROUP)])\
                      .then_inc(s["staged"], 1)
                    for q, (g0, n) in enumerate(QUADS):
                        dve.wait_ge(s["product"], i * 8 + h * 4 + q + 1)
                        nc.vector.tensor_tensor(made[:, h, g0:g0 + n, :], product[q % 2][:, 0:n, :],
                                                c1[:, :].unsqueeze(1).to_broadcast([P, n, C]), ALU.add)\
                          .then_inc(s["biased"], 1)
            loop(dve, pairs, body)

        @block.scalar
        def _(act):
            act.wait_ge(s["loaded"], 64)

            def body(i, first, last):
                for h in range(2):
                    for q, (g0, n) in enumerate(QUADS):
                        at = i * 8 + h * 4 + q
                        act.wait_ge(s["turned"], at + 1)
                        if not (first and h * 4 + q < 2):
                            act.wait_ge(s["product"], at - 1)
                        nc.scalar.activation(hidden[:, q % 2, 0:n, :], turned[q % 2][:, 0:n, :], ACT.Relu,
                                             bias=c0[:, 0:1], scale=w0[:, 0:1]).then_inc(s["relu"], 1)
            loop(act, pairs, body)

        @block.tensor
        def _(pe):
            pe.wait_ge(s["loaded"], 64)

            def body(i, first, last):
                for h in range(2):
                    pe.wait_ge(s["staged"], i * 2 + h + 1)
                    for q, (g0, n) in enumerate(QUADS):
                        at = i * 8 + h * 4 + q
                        if not (first and h * 4 + q < 2):
                            pe.wait_ge(s["relu"], at - 1)
                        for g in range(g0, g0 + n):
                            ins = nc.tensor.transpose(turned[q % 2][:, g - g0, :],
                                                      weights[:, h, g:g + 1].to_broadcast([P, C]), k.ident[:, :])
                        ins.then_inc(s["turned"], 1)
                        pe.wait_ge(s["relu"], at + 1)
                        if not (first and h * 4 + q < 2):
                            pe.wait_ge(s["biased"], at - 1)
                        for j in range(n):
                            ins = nc.tensor.matmul(product[q % 2][:, j, :], hidden[:, q % 2, j, :], w1[:, :],
                                                   start=True, stop=True)
                        ins.then_inc(s["product"], 1)
            loop(pe, pairs, body)


def fold_weights(nc, k, w, b, attn_w, attn_b, fus_w, fus_b, folded):
    terms = {(0, 0): [(0, 1.0)], (0, 1): [(0, 1.0), (2, -1.0)], (0, 2): [(0, 1.0), (2, -1.0)],
             (1, 0): [(1, 1.0)], (1, 1): [(1, 1.0)], (1, 2): [(1, 1.0), (3, -3.0)],
             (2, 1): [(2, 2.0)], (2, 2): [(2, 2.0)], (3, 2): [(3, 4.0)]}
    made = [(i, j) for i in range(3) for j in range(i + 2)]
    slot = {ij: n for n, ij in enumerate(made)}
    order = sorted(terms)
    with Phase(nc, "fold", ["loaded", "own", "turned", "copied", "combined", "multiplied", "folded"]) as ph:
        s = ph.sems
        raw = ph.sbuf("raw", [C, len(made), C])
        flat = ph.sbuf("flat", [C, len(made), C])
        right = ph.sbuf("right", [C, 3, C + 4])
        left = ph.sbuf("left", [C, 3, 3, C + 1])
        extra = ph.sbuf("extra", [C + 1, MIX])
        turned = ph.psum("turned", [C, C])
        product = ph.psum("product", [C + 1, 512])
        block = ph.block()

        @block.sync
        def _(sp):
            n = 0
            for i, j in made:
                sp.dma_start(raw[:, slot[i, j], :], w[i][j]).then_inc(s["loaded"], 16)
                n += 16
            sp.wait_ge(s["own"], 3)
            for i in range(3):
                sp.dma_start(right[:, i, 0:C], fus_w[i * C:(i + 1) * C, :]).then_inc(s["loaded"], 16)
                with nc.allow_non_contiguous_dma(reason="small"):
                    sp.dma_start(right[:, i, C:C + 3], attn_w[i * C:(i + 1) * C, :]).then_inc(s["loaded"], 16)
                    sp.dma_start(left[:, 0, i, C:C + 1], b[i].rearrange("(c o) -> c o", o=1)).then_inc(s["loaded"], 16)
                sp.dma_start(extra[C:C + 1, i * C:(i + 1) * C], fus_b.rearrange("(o c) -> o c", o=1))\
                  .then_inc(s["loaded"], 16)
                n += 64
            sp.dma_start(extra[C:C + 1, 3 * C:3 * C + 3], attn_b.rearrange("(o c) -> o c", o=1)).then_inc(s["loaded"], 16)
            sp.wait_ge(s["loaded"], n + 16)

        n_loaded = 16 * (len(made) + 13)

        @block.vector
        def _(dve):
            own = Order(dve, s["own"])
            own.step(nc.vector.memset(right[:, :, C + 3:C + 4], 0.0))
            own.step(nc.vector.memset(extra[:, :], 0.0))
            own.step(nc.vector.memset(folded[:, :, :], 0.0))
            dve.wait_ge(s["loaded"], n_loaded)
            for n in range(len(made)):
                dve.wait_ge(s["turned"], n + 1)
                nc.vector.tensor_copy(flat[:, n, :], turned[:, :]).then_inc(s["copied"], 1)
            dve.wait_ge(s["copied"], len(made))
            for j in range(4):
                here = [i for jj, i in order if jj == j]
                if j > 0:
                    dve.wait_ge(s["folded"], j)
                for i in here:
                    parts = terms[j, i]
                    a, fa = parts[0]
                    own.step(nc.vector.tensor_scalar(left[:, j % 3, i, 0:C], flat[:, slot[i, a], :], fa, None, ALU.mult))
                    for a, fa in parts[1:]:
                        own.wait()
                        own.step(nc.vector.scalar_tensor_tensor(left[:, j % 3, i, 0:C], flat[:, slot[i, a], :], fa,
                                                                left[:, j % 3, i, 0:C], ALU.mult, ALU.add))
                own.wait()
                dve.sem_inc(s["combined"], 1)
                dve.wait_ge(s["multiplied"], j + 1)
                M = C + 1 if j == 0 else C
                lo = min(here) * C
                if j == 0:
                    nc.vector.tensor_tensor(folded[0:M, j, :], product[0:M, 0:MIX], extra[0:M, :], ALU.add)\
                      .then_inc(s["folded"], 1)
                else:
                    nc.vector.tensor_copy(folded[0:M, j, lo:MIX], product[0:M, lo:MIX]).then_inc(s["folded"], 1)
            dve.wait_ge(s["folded"], 4)

        @block.tensor
        def _(pe):
            pe.wait_ge(s["loaded"], n_loaded)
            for n in range(len(made)):
                if n:
                    pe.wait_ge(s["copied"], n)
                nc.tensor.transpose(turned[:, :], raw[:, n, :], k.ident[0:C, 0:C]).then_inc(s["turned"], 1)
            for j in range(4):
                here = [i for jj, i in order if jj == j]
                pe.wait_ge(s["combined"], j + 1)
                if j:
                    pe.wait_ge(s["folded"], j)
                M = C + 1 if j == 0 else C
                for i in here:
                    nc.tensor.matmul(product[0:M, i * C:(i + 1) * C], left[:, j % 3, i, 0:M], right[:, i, 0:C],
                                     start=True, stop=True)
                for i in here:
                    ins = nc.tensor.matmul(product[0:M, 3 * C:MIX], left[:, j % 3, i, 0:M], right[:, i, C:C + 4],
                                           start=(i == here[0]), stop=(i == here[-1]))
                ins.then_inc(s["multiplied"], 1)


class NodePass:
    weights = None
    width = C
    hidden = None
    norm = False
    SEMS = []
    loads = ()
    out_table = None
    also = None

    def __init__(self, nc, k, name):
        self.nc, self.k, self.name = nc, k, name

    def buffers(self, ph): pass
    def setup_sync(self, ph, sp): return 0
    def before(self, ph, dve, own, i, h, first): pass
    def take(self, ph, dve, own, i, h, q, first, product, g0, n): pass
    def after(self, ph, dve, own, i, h, first, last): pass
    def scalar_extra(self, ph, act, i, h, first): pass
    def scalar_setup(self, ph, act): pass
    def tensor_extra(self, ph, pe, i, h, first, last): pass
    def tensor_setup(self, ph, pe): pass
    def scalar_before(self, ph, act, i, h, first): pass
    def tensor_end(self, ph, pe): pass
    def vector_end(self, ph, dve, own): pass


def node_rows(table, b):
    return table.rearrange("(b p g) c -> p b (g c)", p=P, g=GROUP)[:, bass.ds(b, 1), :]


def flat(tile):
    return tile.rearrange("p g c -> p (g c)").unsqueeze(1)


def partial_rows(k, table, tile, load):
    start = k.NP - P * GROUP
    full, rem = (k.N - start) // GROUP, (k.N - start) % GROUP
    pairs = [(tile[0:full, :, :], table[start:start + full * GROUP, :].rearrange("(p g) c -> p g c", g=GROUP))]
    if rem:
        pairs.append((tile[full:full + 1, 0:rem, :],
                      table[start + full * GROUP:k.N, :].rearrange("(p g) c -> p g c", p=1)))
    return [(a, b) if load else (b, a) for a, b in pairs]


def whole_table(k, table):
    return table[0:k.NP - P * GROUP, :]


def run_node_pass(nc, k, d):
    pairs = k.NP // (2 * P * GROUP)
    names = ["own", "setup", "used", "turned", "copied", "product", "hidden", "activated", "given", "taken",
             "rows_done", "spare", "cleared"] + [f"in{h}" for h in range(2)] + [f"out{h}" for h in range(2)] + NORM_SEMS
    if d.also is not None:
        names += ["also0", "also1", "second"]
    with Phase(nc, d.name, names + d.SEMS) as ph:
        s = ph.sems
        arrived = (s["in0"], s["in1"])
        left = (s["out0"], s["out1"])
        ph.tiles = {n: ph.sbuf(n, [P, 2, GROUP, cols]) for n, _, cols in d.loads}
        ph.rows = ph.sbuf("rows", [P, 2, GROUP, C])
        ph.normed = ph.sbuf("normed", [P, 2, GROUP, C]) if d.norm else None
        ph.norm = norm_buffers(ph) if d.norm else None
        d.buffers(ph)
        if d.weights is not None:
            K = d.weights.shape[0]
            turned_rows = ph.sbuf("turned_rows", [K, 2, 4, P])
            turned = [ph.psum(f"turned{n}", [C, 4, P]) for n in range(2)]
            per = 4 if d.width <= C else 1
            product = [ph.psum(f"product{n}", [P, per, d.width if per > 1 else 512]) for n in range(2)]
            if d.hidden is not None:
                hidden_rows = ph.sbuf("hidden_rows", [C, 2, 4, P])
                hidden = [ph.psum(f"hidden{n}", [C, 4, P]) for n in range(2)]
        block = ph.block()
        per_block = len(d.loads)

        @block.sync
        def _(sp):
            n_setup = d.setup_sync(ph, sp)
            assert n_setup == d.n_setup

            def body(i, first, last):
                for h in range(2):
                    b = i * 2 + h
                    if not first:
                        sp.wait_ge(s["used"], b - 1)
                    for n, table, cols in d.loads:
                        if table.shape[0] == k.N and last and h == 1:
                            sp.wait_ge(s["cleared"], 1)
                            parts = partial_rows(k, table, ph.tiles[n][:, h, :, :], True)
                            for m, (into, what) in enumerate(parts):
                                sp.dma_start(into, what).then_inc(arrived[h], 16)
                        else:
                            src = whole_table(k, table) if table.shape[0] == k.N else table
                            sp.dma_start(flat(ph.tiles[n][:, h, :, :]), node_rows(src, b)).then_inc(arrived[h], 16)
            loop(sp, pairs, body)

        @block.gpsimd
        def _(pool):
            def body(i, first, last):
                for h in range(2):
                    b = i * 2 + h
                    done = s["normed"] if d.norm else s["rows_done"]
                    tile = ph.normed if d.norm else ph.rows
                    pool.wait_ge(done, b + 1)
                    if d.out_table.shape[0] == k.N and last and h == 1:
                        for into, what in partial_rows(k, d.out_table, tile[:, h, :, :], False):
                            pool.dma_start(into, what).then_inc(k.stored if d.final else left[h], 16)
                    else:
                        table = whole_table(k, d.out_table) if d.out_table.shape[0] == k.N else d.out_table
                        pool.dma_start(node_rows(table, b), flat(tile[:, h, :, :])).then_inc(left[h], 16)
                    if d.also is not None:
                        pool.wait_ge(s["second"], b + 1)
                        pool.dma_start(node_rows(d.also, b), flat(ph.second[:, h, :, :])).then_inc(s[f"also{h}"], 16)
            loop(pool, pairs, body)
            pool.wait_ge(left[0], 16 * pairs)
            pool.wait_ge(left[1], 16 * (pairs - (1 if d.final else 0)))
            if d.final:
                start = k.NP - P * GROUP
                pool.wait_ge(k.stored, 32 if (k.N - start) % GROUP else 16)
            if d.also is not None:
                for h in range(2):
                    pool.wait_ge(s[f"also{h}"], 16 * pairs)

        @block.vector
        def _(dve):
            own = Order(dve, s["own"])
            if d.n_setup:
                dve.wait_ge(s["setup"], 16 * d.n_setup)
            if d.weights is not None and d.weights.shape[0] == C + 1:
                nc.vector.memset(turned_rows[C:C + 1, :, :, :], 1.0).then_inc(s["spare"], 1)

            def body(i, first, last):
                for h in range(2):
                    b = i * 2 + h
                    for n, table, cols in d.loads:
                        if table.shape[0] == k.N and last and h == 1:
                            if not first:
                                dve.wait_ge(s["used"], b - 1)
                            nc.vector.memset(ph.tiles[n][:, h, :, :], 0.0).then_inc(s["cleared"], 1)
                    extra = 0
                    for n, table, cols in d.loads:
                        if table.shape[0] == k.N and last and h == 1:
                            extra = len(partial_rows(k, table, ph.tiles[n][:, h, :, :], True)) - 1
                    dve.wait_ge(arrived[h], i * (16 * per_block) + 16 * (per_block + extra))
                    if not d.norm and not first:
                        dve.wait_ge(left[h], i * 16)
                    if d.norm and not first:
                        dve.wait_ge(s["normed"], b - 1)
                    d.before(ph, dve, own, i, h, first)
                    if d.weights is not None:
                        if d.width <= C:
                            for q, (g0, n) in enumerate(QUADS):
                                at = i * 8 + h * 4 + q
                                dve.wait_ge(s["product"], at + 1)
                                d.take(ph, dve, own, i, h, q, first, product[q % 2], g0, n).then_inc(s["taken"], 1)
                        else:
                            for g in range(GROUP):
                                dve.wait_ge(s["product"], (i * 2 + h) * GROUP + g + 1)
                                d.take(ph, dve, own, i, h, 0, first, product[g % 2], g, 1).then_inc(s["taken"], 1)
                    d.after(ph, dve, own, i, h, first, last)
                    if d.norm:
                        own.wait()
                        norm_vector(nc, ph, dve, own, ph.norm, ph.rows[:, h], b, h)
            loop(dve, pairs, body, own)
            d.vector_end(ph, dve, own)

        @block.scalar
        def _(act):
            d.scalar_setup(ph, act)

            def body(i, first, last):
                for h in range(2):
                    b = i * 2 + h
                    d.scalar_before(ph, act, i, h, first)
                    if d.weights is not None:
                        for q, (g0, n) in enumerate(QUADS):
                            at = i * 8 + h * 4 + q
                            act.wait_ge(s["turned"], at + 1)
                            if not (first and h * 4 + q < 2):
                                if d.hidden is not None:
                                    act.wait_ge(s["hidden"], at - 1)
                                elif d.width <= C:
                                    act.wait_ge(s["product"], at - 1)
                                else:
                                    back = (h * 4 + q - 2) % 8
                                    done = (back // 4) * GROUP + QUADS[back % 4][0] + QUADS[back % 4][1]
                                    act.wait_ge(s["product"], i * (2 * GROUP) + done - (2 * GROUP if h * 4 + q < 2 else 0))
                            nc.scalar.activation(turned_rows[0:C, q % 2, 0:n, :], turned[q % 2][:, 0:n, :], ACT.Copy)\
                              .then_inc(s["copied"], 1)
                            if d.hidden is not None:
                                act.wait_ge(s["hidden"], at + 1)
                                if not (first and h * 4 + q < 2):
                                    act.wait_ge(s["product"], at - 1)
                                nc.scalar.activation(hidden_rows[:, q % 2, 0:n, :], hidden[q % 2][:, 0:n, :], ACT.Relu,
                                                     bias=d.hidden[1][:, 0:1]).then_inc(s["activated"], 1)
                    d.scalar_extra(ph, act, i, h, first)
                    if d.norm:
                        norm_root(nc, ph, act, ph.norm, b, h)
                        if not first:
                            act.wait_ge(left[h], i * 16)
                        norm_apply(nc, ph, act, ph.norm, ph.rows[:, h], ph.normed[:, h], b, h)
            loop(act, pairs, body)

        @block.tensor
        def _(pe):
            if d.weights is None:
                return
            if d.n_setup:
                pe.wait_ge(s["setup"], 16 * d.n_setup)
            if d.weights.shape[0] == C + 1:
                pe.wait_ge(s["spare"], 1)
            d.tensor_setup(ph, pe)

            def turn(i, h, q, first):
                g0, n = QUADS[q]
                if q == 0:
                    pe.wait_ge(s["given"], i * 2 + h + 1)
                if not (first and h * 4 + q < 2):
                    pe.wait_ge(s["copied"], i * 8 + h * 4 + q - 1)
                for g in range(g0, g0 + n):
                    ins = nc.tensor.transpose(turned[q % 2][:, g - g0, :], ph.given[:, h, g, :], k.ident[:, :])
                ins.then_inc(s["turned"], 1)

            def body(i, first, last):
                for h in range(2):
                    turn(i, h, 0, first)
                    for q, (g0, n) in enumerate(QUADS):
                        at = i * 8 + h * 4 + q
                        if q + 1 < len(QUADS):
                            turn(i, h, q + 1, first)
                        pe.wait_ge(s["copied"], at + 1)
                        left_side = turned_rows
                        if d.hidden is not None:
                            if not (first and h * 4 + q < 2):
                                pe.wait_ge(s["activated"], at - 1)
                            nc.tensor.matmul(hidden[q % 2][:, 0:n, :].rearrange("c g p -> c (g p)"), d.hidden[0][:, :],
                                             turned_rows[0:C, q % 2, 0:n, :].rearrange("c g p -> c (g p)"),
                                             start=True, stop=True).then_inc(s["hidden"], 1)
                            pe.wait_ge(s["activated"], at + 1)
                            left_side = hidden_rows
                        if d.width <= C:
                            if not (first and h * 4 + q < 2):
                                pe.wait_ge(s["taken"], at - 1)
                            for j in range(n):
                                ins = nc.tensor.matmul(product[q % 2][:, j, 0:d.width], left_side[:, q % 2, j, :], d.weights,
                                                       start=True, stop=True)
                            ins.then_inc(s["product"], 1)
                        else:
                            for j in range(n):
                                g = g0 + j
                                if not (first and h * GROUP + g < 2):
                                    pe.wait_ge(s["taken"], (i * 2 + h) * GROUP + g - 1)
                                nc.tensor.matmul(product[g % 2][:, 0, 0:d.width], left_side[:, q % 2, j, :], d.weights,
                                                 start=True, stop=True).then_inc(s["product"], 1)
                    d.tensor_extra(ph, pe, i, h, first, last)
            loop(pe, pairs, body)
            d.tensor_end(ph, pe)


def row_of(vector):
    return vector.rearrange("(o c) -> o c", o=1).to_broadcast([P, vector.shape[0]])


class StartPass(NodePass):
    norm, n_setup, final = True, 0, False

    def __init__(self, nc, k, name, x, scaled, out):
        super().__init__(nc, k, name)
        self.loads, self.also, self.out_table = (("x", x, C),), scaled, out

    def buffers(self, ph):
        ph.second = ph.sbuf("second", [P, 2, GROUP, C])

    def before(self, ph, dve, own, i, h, first):
        nc = self.nc
        if not first:
            dve.wait_ge(ph.sems[f"also{h}"], i * 16)
        nc.vector.tensor_scalar(ph.second[:, h, :, :], ph.tiles["x"][:, h, :, :], ALPHA, None, ALU.mult)\
          .then_inc(ph.sems["second"], 1)
        own.step(nc.vector.tensor_scalar(ph.rows[:, h, :, :], ph.tiles["x"][:, h, :, :], 1.0 + ALPHA / THETA, None,
                                         ALU.mult))
        dve.wait_ge(ph.sems["second"], i * 2 + h + 1)
        own.wait()
        dve.sem_inc(ph.sems["used"], 1)


class GcnPass(NodePass):
    norm, n_setup, final = True, 3, False

    def __init__(self, nc, k, name, x, sums, joined, W, b, slope, out):
        super().__init__(nc, k, name)
        self.loads, self.out_table = (("x", x, C), ("sums", sums, C), ("map", joined, 4)), out
        self.W, self.b, self.slope = W, b, slope

    def buffers(self, ph):
        self.w = ph.sbuf("w", [C + 1, C])
        self.weights = self.w[:, :]
        self.a = ph.sbuf("a", [P, 1])
        ph.given = ph.tiles["sums"]
        self.degree = ph.sbuf("degree", [P, GROUP])
        self.low = ph.sbuf("low", [P, GROUP, C])

    def setup_sync(self, ph, sp):
        sp.dma_start(self.w[0:C, :], self.W).then_inc(ph.sems["setup"], 16)
        sp.dma_start(self.w[C:C + 1, :], self.b.rearrange("(o c) -> o c", o=1)).then_inc(ph.sems["setup"], 16)
        sp.dma_start(self.a[:, :], row_of(self.slope)).then_inc(ph.sems["setup"], 16)
        return 3

    def before(self, ph, dve, own, i, h, first):
        nc, x, sums = self.nc, ph.tiles["x"], ph.tiles["sums"]
        own.step(nc.vector.tensor_scalar(self.degree[:, :], ph.tiles["map"][:, h, :, 3], 1.0, None, ALU.add))
        own.wait()
        own.step(nc.vector.reciprocal(self.degree[:, :], self.degree[:, :]))
        own.wait()
        own.step(nc.vector.tensor_tensor(ph.rows[:, h, :, :], x[:, h, :, :], spread(self.degree[:, :], C), ALU.mult))
        own.wait()
        nc.vector.tensor_tensor(sums[:, h, :, :], sums[:, h, :, :], ph.rows[:, h, :, :], ALU.add)\
          .then_inc(ph.sems["given"], 1)
        dve.wait_ge(ph.sems["given"], i * 2 + h + 1)

    def take(self, ph, dve, own, i, h, q, first, product, g0, n):
        return self.nc.vector.tensor_copy(ph.rows[:, h, g0:g0 + n, :], product[:, 0:n, :])

    def after(self, ph, dve, own, i, h, first, last):
        nc, rows = self.nc, ph.rows[:, h, :, :]
        dve.wait_ge(ph.sems["taken"], i * 8 + h * 4 + 4)
        own.step(nc.vector.tensor_scalar(self.low[:, :, :], rows, 0.0, self.a[:, 0:1], ALU.min, ALU.mult))
        own.wait()
        own.step(nc.vector.scalar_tensor_tensor(rows, rows, 0.0, self.low[:, :, :], ALU.max, ALU.add))
        own.wait()
        own.step(nc.vector.tensor_tensor(rows, rows, ph.tiles["x"][:, h, :, :], ALU.add))
        own.wait()
        dve.sem_inc(ph.sems["used"], 1)


class ChebPass(NodePass):
    norm, n_setup, final, width = False, 0, False, MIX
    SEMS = ["scored", "exponent", "shaped", "squared", "counted"]

    def __init__(self, nc, k, name, x, mixed, joined, folded, totals, out):
        super().__init__(nc, k, name)
        self.loads, self.out_table = (("x", x, C), ("mixed", mixed, MIX), ("map", joined, 4)), out
        self.weights, self.totals = folded[:, 0, :], totals
        self.hidden = None

    def buffers(self, ph):
        ph.given = ph.tiles["x"]
        self.root = ph.sbuf("root", [P, 2, GROUP])
        self.factor = ph.sbuf("factor", [P, 2, GROUP])
        self.has = ph.sbuf("has", [P, GROUP])
        self.score = ph.sbuf("score", [P, 2, GROUP, 3])
        self.most = ph.sbuf("most", [P, GROUP])
        self.part = ph.sbuf("part", [P, GROUP, C])
        self.both = ph.sbuf("both", [P, 2, GROUP, 2, C])
        self.valid = ph.sbuf("valid", [P, GROUP])
        self.total = ph.psum("total", [1, 512])

    def before(self, ph, dve, own, i, h, first):
        nc, s = self.nc, ph.sems
        b = i * 2 + h
        own.step(nc.vector.tensor_scalar(self.factor[:, h, :], ph.tiles["map"][:, h, :, 1], 1.0, None, ALU.max))
        own.step(nc.vector.tensor_scalar(self.has[:, :], ph.tiles["map"][:, h, :, 1], 0.0, -1.0, ALU.is_gt, ALU.mult))
        own.wait()
        dve.sem_inc(s["given"], 1)
        dve.wait_ge(s["shaped"], b + 1)
        own.step(nc.vector.reciprocal(self.factor[:, h, :], self.root[:, h, :]))
        own.wait()
        own.step(nc.vector.tensor_tensor(self.factor[:, h, :], self.factor[:, h, :], self.has[:, :], ALU.mult))
        own.wait()

    def take(self, ph, dve, own, i, h, q, first, product, g, n):
        mixed = ph.tiles["mixed"]
        return self.nc.vector.scalar_tensor_tensor(mixed[:, h, g, :], mixed[:, h, g, :], self.factor[:, h, g:g + 1],
                                                   product[:, 0, 0:MIX], ALU.mult, ALU.add)

    def after(self, ph, dve, own, i, h, first, last):
        nc, s, mixed, rows = self.nc, ph.sems, ph.tiles["mixed"], ph.rows[:, h, :, :]
        b = i * 2 + h
        score = self.score[:, h, :, :]
        dve.wait_ge(s["taken"], b * GROUP + GROUP)
        scores = mixed[:, h, :, 3 * C:3 * C + 3]
        own.step(nc.vector.tensor_reduce(self.most[:, :], scores, AX_X, ALU.max))
        own.wait()
        nc.vector.tensor_tensor(score, scores, spread(self.most[:, :], 3), ALU.subtract).then_inc(s["scored"], 1)
        dve.wait_ge(s["exponent"], b + 1)
        own.step(nc.vector.tensor_reduce(self.most[:, :], score, AX_X, ALU.add))
        own.wait()
        own.step(nc.vector.reciprocal(self.most[:, :], self.most[:, :]))
        own.wait()
        own.step(nc.vector.tensor_tensor(score, score, spread(self.most[:, :], 3), ALU.mult))
        own.wait()
        own.step(nc.vector.tensor_tensor(rows, mixed[:, h, :, 0:C], spread(score[:, :, 0], C), ALU.mult))
        for n in (1, 2):
            own.step(nc.vector.tensor_tensor(self.part[:, :, :], mixed[:, h, :, n * C:(n + 1) * C],
                                             spread(score[:, :, n], C), ALU.mult))
            own.wait()
            own.step(nc.vector.tensor_tensor(rows, rows, self.part[:, :, :], ALU.add))
            own.wait()
        if not first:
            dve.wait_ge(s["counted"], b - 1)
        own.step(nc.vector.tensor_copy(self.both[:, h, :, 0, :], rows))
        own.step(nc.vector.tensor_tensor(self.both[:, h, :, 1, :], rows, rows, ALU.mult))
        own.wait()
        dve.sem_inc(s["squared"], 1)
        dve.sem_inc(s["rows_done"], 1)
        dve.sem_inc(s["used"], 1)

    def scalar_before(self, ph, act, i, h, first):
        act.wait_ge(ph.sems["given"], i * 2 + h + 1)
        self.nc.scalar.activation(self.root[:, h, :], self.factor[:, h, :], ACT.Sqrt).then_inc(ph.sems["shaped"], 1)

    def scalar_extra(self, ph, act, i, h, first):
        b = i * 2 + h
        act.wait_ge(ph.sems["scored"], b + 1)
        self.nc.scalar.activation(self.score[:, h, :, :], self.score[:, h, :, :], ACT.Exp).then_inc(ph.sems["exponent"], 1)

    def tensor_setup(self, ph, pe):
        self.nc.tensor.matmul(self.total[0:1, 0:2 * C], self.k.zeros_f[:, 0:1], self.k.zeros_f[:, 0:2 * C],
                              start=True, stop=False)

    def tensor_extra(self, ph, pe, i, h, first, last):
        nc = self.nc
        pe.wait_ge(ph.sems["squared"], i * 2 + h + 1)
        for g in range(GROUP):
            count = self.k.valid[:, g:g + 1] if last and h == 1 else self.k.ones[:, 0:1]
            ins = nc.tensor.matmul(self.total[0:1, 0:2 * C], count, self.both[:, h, g, :, :].rearrange("p a c -> p (a c)"),
                                   start=False, stop=(last and h == 1 and g == GROUP - 1))
        ins.then_inc(ph.sems["counted"], 1)

    def vector_end(self, ph, dve, own):
        dve.wait_ge(ph.sems["counted"], self.k.NP // (P * GROUP))
        own.step(self.nc.vector.tensor_copy(self.totals[:, :], self.total[0:1, 0:2 * C]))
        own.wait()


class NormPass(NodePass):
    norm, n_setup, final = True, 0, False

    def __init__(self, nc, k, name, x, h, coefficients, out):
        super().__init__(nc, k, name)
        self.loads, self.out_table, self.co = (("x", x, C), ("h", h, C)), out, coefficients

    def before(self, ph, dve, own, i, h, first):
        nc, rows, mid = self.nc, ph.rows[:, h, :, :], ph.tiles["h"][:, h, :, :]
        wide = lambda n: self.co[:, n, :].unsqueeze(1).to_broadcast([P, GROUP, C])
        own.step(nc.vector.tensor_tensor(mid, mid, wide(0), ALU.mult))
        own.wait()
        own.step(nc.vector.tensor_tensor(mid, mid, wide(1), ALU.add))
        own.wait()
        own.step(nc.vector.scalar_tensor_tensor(rows, mid, 0.0, ph.tiles["x"][:, h, :, :], ALU.max, ALU.add))
        own.wait()
        dve.sem_inc(ph.sems["used"], 1)


class GinePass(NodePass):
    n_setup = 4

    def __init__(self, nc, k, name, x, sums, W0, b0, W1, b1, out, skip=None, final=False):
        super().__init__(nc, k, name)
        self.loads = (("x", x, C), ("sums", sums, C)) + ((("skip", skip, C),) if skip is not None else ())
        self.out_table, self.skip, self.final, self.norm = out, skip, final, skip is not None
        self.sources = (W0, b0, W1, b1)

    def buffers(self, ph):
        self.w0, self.w1 = ph.sbuf("w0", [C, C]), ph.sbuf("w1", [C, C])
        self.c0, self.c1 = ph.sbuf("c0", [C, 1]), ph.sbuf("c1", [P, C])
        self.weights, self.hidden = self.w1[:, :], (self.w0, self.c0)
        ph.given = ph.tiles["sums"]

    def setup_sync(self, ph, sp):
        W0, b0, W1, b1 = self.sources
        setup = ph.sems["setup"]
        sp.dma_start(self.w0[:, :], W0).then_inc(setup, 16)
        sp.dma_start(self.w1[:, :], W1).then_inc(setup, 16)
        with self.nc.allow_non_contiguous_dma(reason="one column of 96"):
            sp.dma_start(self.c0[:, :], b0.rearrange("(c o) -> c o", o=1)).then_inc(setup, 16)
        sp.dma_start(self.c1[:, :], row_of(b1)).then_inc(setup, 16)
        return 4

    def scalar_setup(self, ph, act):
        act.wait_ge(ph.sems["setup"], 64)

    def before(self, ph, dve, own, i, h, first):
        sums = ph.tiles["sums"]
        self.nc.vector.tensor_tensor(sums[:, h, :, :], sums[:, h, :, :], ph.tiles["x"][:, h, :, :], ALU.add)\
            .then_inc(ph.sems["given"], 1)

    def take(self, ph, dve, own, i, h, q, first, product, g0, n):
        return self.nc.vector.tensor_tensor(ph.rows[:, h, g0:g0 + n, :], product[:, 0:n, :],
                                            self.c1[:, :].unsqueeze(1).to_broadcast([P, n, C]), ALU.add)

    def after(self, ph, dve, own, i, h, first, last):
        nc, rows = self.nc, ph.rows[:, h, :, :]
        dve.wait_ge(ph.sems["taken"], i * 8 + h * 4 + 4)
        if self.skip is not None:
            own.step(nc.vector.scalar_tensor_tensor(rows, rows, 0.0, ph.tiles["skip"][:, h, :, :], ALU.max, ALU.add))
            own.wait()
        else:
            own.step(nc.vector.tensor_scalar(rows, rows, 0.0, None, ALU.max))
            own.wait()
            dve.sem_inc(ph.sems["rows_done"], 1)
        dve.sem_inc(ph.sems["used"], 1)


def batch_norm(nc, k, totals, gamma, beta, coefficients):
    with Phase(nc, "batch", ["loaded", "own", "rooted", "varied", "ready", "wide"]) as ph:
        s = ph.sems
        given = ph.sbuf("given", [1, 2, C])
        mean = ph.sbuf("mean", [1, 2, C])
        square = ph.sbuf("square", [1, C])
        root = ph.sbuf("root", [1, C])
        pair = ph.sbuf("pair", [1, 2, C])
        wide = ph.psum("wide_rows", [P, 512])
        block = ph.block()

        @block.sync
        def _(sp):
            sp.dma_start(given[:, 0, :], gamma.rearrange("(o c) -> o c", o=1)).then_inc(s["loaded"], 16)
            sp.dma_start(given[:, 1, :], beta.rearrange("(o c) -> o c", o=1)).then_inc(s["loaded"], 16)
            sp.wait_ge(s["loaded"], 32)

        @block.vector
        def _(dve):
            own = Order(dve, s["own"])
            own.step(nc.vector.tensor_scalar(mean[:, :, :].rearrange("p a c -> p (a c)"), totals[:, :], 1.0 / k.N, None,
                                             ALU.mult))
            own.wait()
            own.step(nc.vector.tensor_tensor(square[:, :], mean[:, 0, :], mean[:, 0, :], ALU.mult))
            own.wait()
            own.step(nc.vector.scalar_tensor_tensor(square[:, :], mean[:, 1, :], BN_EPS, square[:, :],
                                                    ALU.add, ALU.subtract))
            own.wait()
            dve.sem_inc(s["varied"], 1)
            dve.wait_ge(s["rooted"], 1)
            dve.wait_ge(s["loaded"], 32)
            own.step(nc.vector.reciprocal(square[:, :], root[:, :]))
            own.wait()
            own.step(nc.vector.tensor_tensor(pair[:, 0, :], square[:, :], given[:, 0, :], ALU.mult))
            own.wait()
            own.step(nc.vector.tensor_tensor(square[:, :], mean[:, 0, :], pair[:, 0, :], ALU.mult))
            own.wait()
            nc.vector.tensor_tensor(pair[:, 1, :], given[:, 1, :], square[:, :], ALU.subtract).then_inc(s["ready"], 1)
            dve.wait_ge(s["wide"], 1)
            own.step(nc.vector.tensor_copy(coefficients[:, :, :].rearrange("p a c -> p (a c)"), wide[:, 0:2 * C]))
            own.wait()

        @block.scalar
        def _(act):
            act.wait_ge(s["varied"], 1)
            nc.scalar.activation(root[:, :], square[:, :], ACT.Sqrt).then_inc(s["rooted"], 1)

        @block.tensor
        def _(pe):
            pe.wait_ge(s["ready"], 1)
            nc.tensor.matmul(wide[:, 0:2 * C], k.ones[0:1, :], pair[:, :, :].rearrange("p a c -> p (a c)"),
                             start=True, stop=True).then_inc(s["wide"], 1)


class Resident:

    def __init__(self, nc, stack, N, E):
        pair = 2 * GROUP * P
        self.N, self.E = N, E
        self.EP, self.NP = -(-E // pair) * pair, -(-N // pair) * pair
        self.T = self.EP // P
        assert self.NP - P * GROUP < N and self.EP > E and N < NOWHERE

        def sb(what, shape, dtype=F32):
            return stack.enter_context(nc.sbuf_tensor(what, shape, dtype))
        self.ident = sb("ident", [P, P])
        self.before = sb("before", [P, 2, P], BF16)
        self.rest = sb("rest", [P, 2, P], BF16)
        self.later = sb("later", [P, 2, P])
        self.first_row = sb("first_row", [P, P])
        self.final_row = sb("final_row", [P, P])
        self.pick_row = sb("pick_row", [LASTS, GROUP])
        self.after_row = sb("after_row", [LASTS, GROUP])
        self.edge_rows = sb("edge_rows", [P, 2])
        self.ones_bf = sb("ones_bf", [P, P], BF16)
        self.zeros_bf = sb("zeros_bf", [P, 512], BF16)
        self.zeros_f = sb("zeros_f", [P, 2 * C])
        self.valid = sb("valid", [P, GROUP])
        self.ones = sb("ones", [P, P])
        self.iota = sb("iota", [P, 512])
        self.edge_row = sb("edge_row", [P, self.T])
        self.edge_weight = sb("edge_weight", [P, self.T])
        self.from_x = sb("from_x", [P, self.T], I32)
        self.key_x = sb("key_x", [P, self.T], I32)
        self.i_cheb = sb("i_cheb", [P, self.T], I32)
        self.i_odd = sb("i_odd", [P, self.T], I32)
        self.i_even = sb("i_even", [P, self.T], I32)
        self.w_hop = sb("w_hop", [P, self.T])
        self.w_gcn = sb("w_gcn", [P, self.T])
        self.w_cheb = sb("w_cheb", [P, self.T])
        self.w_cheb2 = sb("w_cheb2", [P, self.T])
        self.s_hop = sb("s_hop", [P, self.T])
        self.s_gcn = sb("s_gcn", [P, self.T])
        self.folded = sb("folded", [C + 1, 4, MIX])
        self.totals = sb("totals", [1, 2 * C])
        self.coefficients = sb("coefficients", [P, 2, C])
        self.stored = nc.alloc_semaphore("output_stored")


def graph_layers(nc, out, x, src, dst, edge_weight, W, b, slope, w2, b2, w3, b3, w4, b4, attn_w, attn_b,
                 fus_w, fus_b, gamma, beta, W_l0, b_l0, W_l1, b_l1, W00, b00, W01, b01, W10, b10, W11, b11):
    with ExitStack() as stack:
        k = Resident(nc, stack, x.shape[0], src.shape[0])
        by_src, by_dst = Side("src", stack, nc, k.T), Side("dst", stack, nc, k.T)

        def table(name, rows, cols):
            return nc.dram_tensor(name, (rows, cols), F32, kind="Internal").ap()
        EP, NP = k.EP, k.NP
        unsorted, half, ordered = (table(n, EP, 4) for n in ("edges_unsorted", "edges_half", "edges_sorted"))
        map_src, map_dst, joined = table("map_src", NP, 2), table("map_dst", NP, 2), table("map_joined", NP, 4)
        hops = table("hops", EP + NP + EP, C)
        hop1, hop2 = table("hop1", EP + P, C), table("hop2", EP + P, C)
        h_rows, feats = table("h_rows", EP, C), table("features", EP, C)
        sums, mixed = table("sums", NP, C), table("mixed", NP, MIX)
        x1, x2, x3, mid, conv = (table(n, NP, C) for n in ("x1", "x2", "x3", "mid", "conv"))

        constants(nc, k)
        fill_rows(nc, k, "fill", [(map_src, (-1.0, 0.0)), (map_dst, (-1.0, 0.0)), (sums, (0.0,)), (mixed, (0.0,)),
                                  (hop1[EP:EP + P, :], (0.0,)), (hop2[EP:EP + P, :], (0.0,))])

        gather_edges(nc, k, src, dst, edge_weight.rearrange("e o -> (e o)"), unsorted)
        for side, field, node_map in ((by_src, 0, map_src), (by_dst, 1, map_dst)):
            low = 256
            high = -(-(k.N + 1) // low)
            assert high <= 512
            radix_pass(nc, k, f"low_{side.name}", unsorted, half, field, 0, low)
            radix_pass(nc, k, f"high_{side.name}", half, ordered, field, 8, high)
            load_side(nc, k, side, ordered, field, k.edge_weight if field == 1 else None)
            edge_pass(nc, k, f"map_{side.name}", side, MapNodes(nc, k, side, node_map), width=2)
        join_maps(nc, k, map_src, map_dst, joined)
        for side in (by_src, by_dst):
            gather_map(nc, k, side, joined)
        prepare(nc, k, by_src, by_dst)

        run_node_pass(nc, k, StartPass(nc, k, "start", x, hops[EP:EP + NP, :], x1))
        gather_rows(nc, k, "keys_x", x, k.key_x, h_rows)
        odd, even = hops[0:EP, :], hops[EP + NP:EP + NP + EP, :]
        hop = dict(weight=k.w_hop, scale=k.s_hop)
        edge_pass(nc, k, "hop_first", by_src, Store(nc, odd, h_rows), table=x, index=k.from_x, **hop)
        with nc.Fori(0, (K_HOPS - 2) // 2):
            edge_pass(nc, k, "hop_even", by_src, Store(nc, even, h_rows), table=hops[0:EP + NP, :], index=k.i_odd, **hop)
            edge_pass(nc, k, "hop_odd", by_src, Store(nc, odd, h_rows), table=hops, index=k.i_even, **hop)
        edge_pass(nc, k, "hop_last", by_src, NormScatter(nc, k, x1, by_src.end, h_rows),
                  table=hops[0:EP + NP, :], index=k.i_odd, **hop)

        edge_pass(nc, k, "gcn", by_dst, Scatter(nc, k, sums, by_dst.end), table=x1, index=by_dst.other,
                  weight=k.w_gcn, scale=k.s_gcn)
        run_node_pass(nc, k, GcnPass(nc, k, "gcn_nodes", x1, sums, joined, W, b, slope, x2))

        fold_weights(nc, k, (w2, w3, w4), (b2, b3, b4), attn_w, attn_b, fus_w, fus_b, k.folded)
        edge_pass(nc, k, "cheb1", by_dst, Store(nc, hop1[0:EP, :]), table=x2, index=by_dst.other, weight=k.w_cheb)
        edge_pass(nc, k, "cheb2", by_dst, Store(nc, hop2[0:EP, :]), table=hop1, index=k.i_cheb, weight=k.w_cheb2)
        edge_pass(nc, k, "cheb3", by_dst, MixHops(nc, k, mixed, by_dst.end, hop1[0:EP, :], hop2[0:EP, :], k.folded),
                  table=hop2, index=k.i_cheb, weight=k.w_cheb2)
        run_node_pass(nc, k, ChebPass(nc, k, "cheb_nodes", x2, mixed, joined, k.folded, k.totals, mid))
        batch_norm(nc, k, k.totals, gamma, beta, k.coefficients)
        run_node_pass(nc, k, NormPass(nc, k, "cheb_norm", x2, mid, k.coefficients, x3))

        edge_features(nc, k, W_l0, b_l0, W_l1, b_l1, feats)
        edge_pass(nc, k, "gine1", by_dst, Scatter(nc, k, sums, by_dst.end), table=x3, index=by_dst.other, added=feats)
        run_node_pass(nc, k, GinePass(nc, k, "gine1_nodes", x3, sums, W00, b00, W01, b01, conv))
        edge_pass(nc, k, "gine2", by_dst, Scatter(nc, k, sums, by_dst.end), table=conv, index=by_dst.other, added=feats)
        run_node_pass(nc, k, GinePass(nc, k, "gine2_nodes", conv, sums, W10, b10, W11, b11, out, skip=x3, final=True))


_INS = ["x", "src", "dst", "edge_weight1", "L1_gnn_W", "L1_gnn_b", "L1_gnn_prelu_a", "L2_gnn_w2", "L2_gnn_b2",
        "L2_gnn_w3", "L2_gnn_b3", "L2_gnn_w4", "L2_gnn_b4", "L2_gnn_attn_w", "L2_gnn_attn_b", "L2_gnn_fus_w",
        "L2_gnn_fus_b", "L2_gnn_bn_gamma", "L2_gnn_bn_beta", "L3_gnn_W_l0", "L3_gnn_b_l0", "L3_gnn_W_l1",
        "L3_gnn_b_l1", "L3_gnn_W00", "L3_gnn_b00", "L3_gnn_W01", "L3_gnn_b01", "L3_gnn_W10", "L3_gnn_b10",
        "L3_gnn_W11", "L3_gnn_b11"]


def kernel(**inputs):
    import numpy as _np
    import concourse.bacc as _bacc
    from concourse import mybir as _mybir
    from concourse.bass_utils import run_bass_kernel_spmd as _run

    nc = _bacc.Bacc("TRN2", target_bir_lowering=False, num_devices=1)
    arrays, args = {}, []
    for name in _INS:
        a = _np.ascontiguousarray(inputs[name])
        arrays[f"in_{name}_dram"] = a
        args.append(nc.dram_tensor(f"in_{name}_dram", a.shape, _mybir.dt.from_np(a.dtype), kind="ExternalInput").ap())
    out = nc.dram_tensor("out_0_dram", arrays["in_x_dram"].shape, F32, kind="ExternalOutput").ap()
    graph_layers(nc, out, *args)
    r = _run(nc, [arrays], core_ids=[0])
    return r.results[0]["out_0_dram"]
```

```python
from contextlib import ExitStack

import concourse.bass as bass
from concourse import mybir

P = 128
C = 96
GROUP = 14
QUADS = ((0, 4), (4, 4), (8, 4), (12, 2))
LASTS = 16
NOWHERE = 1 << 20
K_HOPS, ALPHA, BETA = 10, 0.1, 0.9
THETA = BETA ** K_HOPS + ALPHA * sum(BETA ** i for i in range(K_HOPS))
LN_EPS = 1e-5
BN_EPS = 1e-5

ALU = mybir.AluOpType
ACT = mybir.ActivationFunctionType
F32 = mybir.dt.float32
BF16 = mybir.dt.bfloat16
I32 = mybir.dt.int32
AX_X = mybir.AxisListType.X


class Order:

    def __init__(self, eng, sem):
        self.eng, self.sem, self.count, self.per = eng, sem, 0, None

    def step(self, ins):
        ins.then_inc(self.sem, 1)
        self.count = self.count + 1

    def wait(self):
        self.eng.wait_ge(self.sem, self.count)


def loop(eng, n, body, order=None):
    start = order.count if order else 0
    body(0, True, n == 1)
    per = order.count - start if order else 0
    if n > 2:
        with eng.Fori(1, n - 1) as i:
            if order:
                order.count = i * per + start
            body(i, False, False)
    if n > 1:
        if order:
            order.count = start + (n - 1) * per
        body(n - 1, False, True)


def spread(ap, n):
    return ap.unsqueeze(2).to_broadcast([P, ap.shape[1], n])


class Phase:

    def __init__(self, nc, name, sems):
        self.nc, self.name, self.names = nc, name, sems

    def __enter__(self):
        self.stack = ExitStack()
        self.sems = {s: self.nc.alloc_semaphore(f"{self.name}_{s}") for s in self.names}
        return self

    def sbuf(self, name, shape, dtype=F32):
        return self.stack.enter_context(self.nc.sbuf_tensor(f"{self.name}_{name}", shape, dtype))

    def psum(self, name, shape, dtype=F32):
        return self.stack.enter_context(self.nc.psum_tensor(f"{self.name}_{name}", shape, dtype))

    def block(self):
        return self.stack.enter_context(self.nc.Block())

    def __exit__(self, *failed):
        self.stack.close()
        if not failed[0]:
            self.nc.clear_and_free_semaphores(list(self.sems.values()))
            self.nc.all_engine_barrier()


def constants(nc, k):
    with Phase(nc, "const", ["made", "loaded"]) as ph:
        made, loaded = ph.sems["made"], ph.sems["loaded"]
        block = ph.block()

        @block.gpsimd
        def _(pool):
            nc.gpsimd.memset(k.ident[:, :], 0.0).then_inc(made, 1)
            nc.gpsimd.memset(k.before[:, :, :], 1.0).then_inc(made, 1)
            nc.gpsimd.memset(k.later[:, :, :], 1.0).then_inc(made, 1)
            nc.gpsimd.memset(k.first_row[:, :], 1.0).then_inc(made, 1)
            nc.gpsimd.memset(k.edge_rows[:, :], 0.0).then_inc(made, 1)
            nc.gpsimd.memset(k.ones_bf[:, :], 1.0).then_inc(made, 1)
            nc.gpsimd.memset(k.zeros_bf[:, :], 0.0).then_inc(made, 1)
            nc.gpsimd.memset(k.ones[:, :], 1.0).then_inc(made, 1)
            nc.gpsimd.iota(k.iota[:, :], pattern=[[1, 512]], base=0, channel_multiplier=0,
                           allow_small_or_imprecise_dtypes=True).then_inc(made, 1)
            nc.gpsimd.iota(k.edge_row[:, :], pattern=[[1, k.T]], base=0, channel_multiplier=k.T,
                           allow_small_or_imprecise_dtypes=True).then_inc(made, 1)
            nc.gpsimd.memset(k.zeros_f[:, :], 0.0).then_inc(made, 1)
            nc.gpsimd.memset(k.valid[:, :], 1.0).then_inc(made, 1)
            nc.gpsimd.memset(k.final_row[:, :], 1.0).then_inc(made, 1)
            nc.gpsimd.memset(k.pick_row[:, :], 0.0).then_inc(made, 1)
            nc.gpsimd.memset(k.after_row[:, :], 1.0).then_inc(made, 1)
            pool.wait_ge(made, 15)

            def keep(ap, op, base, cm, step, n, fill):
                nc.gpsimd.affine_select(out=ap, in_=ap, compare_op=op, fill=fill, base=base,
                                        pattern=[[step, n]], channel_multiplier=cm).then_inc(made, 1)

            keep(k.ident[:, :], ALU.not_equal, 0, 1, -1, P, 1.0)
            keep(k.before[:, 0, :], ALU.is_gt, 0, -1, 1, P, 0.0)
            keep(k.before[:, 1, :], ALU.is_gt, 0, 1, -1, P, 0.0)
            keep(k.later[:, 0, :], ALU.is_gt, 0, -1, 1, P, 0.0)
            keep(k.later[:, 1, :], ALU.is_gt, 0, 1, -1, P, 0.0)
            keep(k.first_row[:, :], ALU.is_equal, 0, 1, 0, P, 0.0)
            keep(k.edge_rows[:, 0:1], ALU.not_equal, 0, 1, 0, 1, 1.0)
            keep(k.edge_rows[:, 1:2], ALU.not_equal, 1 - P, 1, 0, 1, 1.0)
            nc.gpsimd.affine_select(out=k.valid[:, :], in_=k.valid[:, :], compare_op=ALU.is_ge, fill=0.0,
                                    base=k.N - 1 - (k.NP - P * GROUP), pattern=[[-1, GROUP]],
                                    channel_multiplier=-GROUP).then_inc(made, 1)
            keep(k.final_row[:, :], ALU.is_equal, 1 - P, 1, 0, P, 0.0)
            keep(k.pick_row[:, :], ALU.not_equal, 1, -1, 1, GROUP, 1.0)
            keep(k.after_row[:, :], ALU.is_ge, 0, -1, 1, GROUP, 0.0)
            pool.wait_ge(made, 27)
            nc.gpsimd.memset(k.pick_row[0:1, GROUP - 1:GROUP], 1.0).then_inc(made, 1)
            pool.wait_ge(made, 28)

        @block.vector
        def _(dve):
            dve.wait_ge(made, 28)
            nc.vector.tensor_scalar(k.rest[:, :, :], k.before[:, :, :], -1.0, 1.0,
                                    ALU.mult, ALU.add).then_inc(made, 1)
            dve.wait_ge(made, 29)


def gather_edges(nc, k, src, dst, weight, table):
    T, E, N = k.T, k.E, k.N
    full, rem = E // T, E % T
    with Phase(nc, "edges", ["filled", "loaded", "packed", "stored"]) as ph:
        filled, loaded, packed, stored = (ph.sems[s] for s in ph.names)
        ends = ph.sbuf("ends", [P, 2, T], I32)
        weights = ph.sbuf("weights", [P, T])
        rows = ph.sbuf("rows", [P, T, 4])
        block = ph.block()

        @block.sync
        def _(sp):
            sp.wait_ge(filled, 2)
            n = 0
            for what, into in ((src, ends[:, 0, :]), (dst, ends[:, 1, :]), (weight, weights[:, :])):
                sp.dma_start(into[0:full, :], what[0:full * T].rearrange("(p t) -> p t", t=T)).then_inc(loaded, 16)
                n += 16
                if rem:
                    sp.dma_start(into[full:full + 1, 0:rem],
                                 what[full * T:E].rearrange("(p t) -> p t", p=1)).then_inc(loaded, 16)
                    n += 16
            sp.wait_ge(loaded, n)
            sp.wait_ge(packed, 4)
            sp.dma_start(table.rearrange("(p t) c -> p t c", p=P), rows[:, :, :]).then_inc(stored, 16)
            sp.wait_ge(stored, 16)

        @block.vector
        def _(dve):
            nc.vector.memset(ends[:, :, :], N).then_inc(filled, 1)
            nc.vector.memset(weights[:, :], 0.0).then_inc(filled, 1)
            nc.vector.memset(rows[:, :, 3:4], 0.0).then_inc(packed, 1)
            dve.wait_ge(loaded, 16 * (6 if rem else 3))
            nc.vector.tensor_copy(rows[:, :, 0], ends[:, 0, :]).then_inc(packed, 1)
            nc.vector.tensor_copy(rows[:, :, 1], ends[:, 1, :]).then_inc(packed, 1)
            nc.vector.tensor_copy(rows[:, :, 2], weights[:, :]).then_inc(packed, 1)


def radix_pass(nc, k, name, jobs, shift, buckets, beside=None):
    T = k.T
    pairs = T // (2 * GROUP)
    B = buckets
    J = len(jobs)
    sems = ["loaded", "own", "onehot", "counted", "prefix", "hot", "total", "rows_ready"]
    sems += [f"{what}{j}" for what in ("partial", "read", "added") for j in range(J)]
    sems += [f"scattered{h}{j}" for h in range(2) for j in range(J)]
    with Phase(nc, name, sems + (beside.SEMS if beside else [])) as ph:
        s = ph.sems
        scattered = [[s[f"scattered{h}{j}"] for j in range(J)] for h in range(2)]
        edges = ph.sbuf("edges", [P, J, T, 4])
        key = ph.sbuf("key", [P, J, T], I32)
        digit = ph.sbuf("digit", [P, J, T])
        hot = ph.sbuf("hot", [P, 2, J, 2, B], BF16)
        sums = ph.sbuf("sums", [P, 2, J, B])
        base = ph.sbuf("base", [P, J, B])
        product = ph.sbuf("product", [P, J, 2, B], BF16)
        rank = ph.sbuf("rank", [P, J, GROUP])
        whole = ph.sbuf("whole", [P, J, GROUP], I32)
        bits = ph.sbuf("bits", [P, 3, J, GROUP], I32)
        turned = ph.sbuf("turned", [P, J, GROUP])
        row = ph.sbuf("row", [P, 2, J, GROUP], I32)
        moved = ph.sbuf("moved", [P, 2, J, GROUP, 4])
        count = [ph.psum(f"count{j}", [P, 512]) for j in range(J)]
        running = [ph.psum(f"running{j}", [P, 512]) for j in range(J)]
        if beside:
            beside.buffers(ph)
        block = ph.block()

        def make_hot(tile_pair, slot):
            return nc.vector.tensor_tensor(
                hot[:, slot, :, :, :], k.iota[:, 0:B].unsqueeze(1).unsqueeze(1).to_broadcast([P, J, 2, B]),
                digit[:, :, bass.ds(tile_pair * 2, 2)].unsqueeze(3).to_broadcast([P, J, 2, B]), ALU.is_equal)

        @block.sync
        def _(sp):
            for j, (unsorted, _, _) in enumerate(jobs):
                sp.dma_start(edges[:, j, :, :], unsorted.rearrange("(p t) c -> p t c", p=P)).then_inc(s["loaded"], 16)
            sp.wait_ge(s["loaded"], 16 * J)

        if beside:
            @block.scalar
            def _(act):
                beside.scalar(ph, act)

        @block.vector
        def _(dve):
            own = Order(dve, s["own"])
            dve.wait_ge(s["loaded"], 16 * J)
            for j, (_, _, field) in enumerate(jobs):
                own.step(nc.vector.tensor_copy(key[:, j, :], edges[:, j, :, field]))
            own.wait()
            own.step(nc.vector.tensor_scalar(key[:, :, :], key[:, :, :], shift, digit_mask(B),
                                             ALU.logical_shift_right, ALU.bitwise_and))
            own.wait()
            own.step(nc.vector.tensor_copy(digit[:, :, :], key[:, :, :]))
            own.wait()

            def histogram(i, first, last):
                for g in range(GROUP):
                    if not (first and g < 2):
                        dve.wait_ge(s["counted"], i * GROUP + g - 1)
                    make_hot(i * GROUP + g, g % 2).then_inc(s["onehot"], 1)
            loop(dve, pairs, histogram)

            dve.wait_ge(s["total"], J)
            for j in range(J):
                own.step(nc.vector.tensor_copy(sums[:, 0, j, :], count[j][:, 0:B]))
            at, reach = 0, 1
            while reach < B:
                own.wait()
                own.step(nc.vector.tensor_copy(sums[:, 1 - at, :, 0:reach], sums[:, at, :, 0:reach]))
                own.step(nc.vector.tensor_tensor(sums[:, 1 - at, :, reach:B], sums[:, at, :, reach:B],
                                                 sums[:, at, :, 0:B - reach], ALU.add))
                at, reach = 1 - at, reach * 2
            own.wait()
            for j in range(J):
                nc.vector.tensor_tensor(base[:, j, :], sums[:, at, j, :], count[j][:, 0:B], ALU.subtract)\
                  .then_inc(s["prefix"], 1)

            def ranks(i, first, last):
                for h in range(2):
                    for j in range(J):
                        if not first:
                            dve.wait_ge(scattered[h][j], i * (16 * GROUP))
                        own.step(nc.vector.tensor_copy(moved[:, h, j, :, :],
                                                       edges[:, j, bass.ds((i * 2 + h) * GROUP, GROUP), :]))
                    for g in range(GROUP):
                        t = h * GROUP + g
                        if t % 2 == 0:
                            if not (first and t < 4):
                                for j in range(J):
                                    dve.wait_ge(s[f"added{j}"], i * (2 * GROUP) + t - 2)
                            make_hot(i * GROUP + t // 2, (t // 2) % 2).then_inc(s["hot"], 1)
                            dve.wait_ge(s["hot"], i * GROUP + t // 2 + 1)
                        for j in range(J):
                            dve.wait_ge(s[f"partial{j}"], i * (2 * GROUP) + t + 1)
                            nc.vector.tensor_tensor_reduce(
                                product[:, j, t % 2, :], running[j][:, 0:B], hot[:, (t // 2) % 2, j, t % 2, :], 1.0, 0.0,
                                ALU.mult, ALU.add, rank[:, j, g:g + 1]).then_inc(s[f"read{j}"], 1)
                    for j in range(J):
                        dve.wait_ge(s[f"read{j}"], i * (2 * GROUP) + (h + 1) * GROUP)
                    own.step(nc.vector.tensor_copy(whole[:, :, :], rank[:, :, :]))
                    own.wait()
                    own.step(nc.vector.tensor_scalar(bits[:, 0, :, :], whole[:, :, :], P - 1, None, ALU.bitwise_and))
                    own.step(nc.vector.tensor_scalar(bits[:, 1, :, :], whole[:, :, :], 7, None, ALU.logical_shift_right))
                    own.step(nc.vector.tensor_scalar(bits[:, 2, :, :], whole[:, :, :], 7, 1,
                                                     ALU.logical_shift_right, ALU.bitwise_and))
                    own.wait()
                    own.step(nc.vector.tensor_scalar(turned[:, :, :], bits[:, 0, :, :], -2.0, P - 1.0, ALU.mult, ALU.add))
                    own.wait()
                    own.step(nc.vector.tensor_tensor(turned[:, :, :], turned[:, :, :], bits[:, 2, :, :], ALU.mult))
                    own.wait()
                    own.step(nc.vector.tensor_tensor(turned[:, :, :], turned[:, :, :], bits[:, 0, :, :], ALU.add))
                    own.wait()
                    nc.vector.scalar_tensor_tensor(row[:, h, :, :], turned[:, :, :], float(T), bits[:, 1, :, :],
                                                   ALU.mult, ALU.add).then_inc(s["rows_ready"], 1)
            loop(dve, pairs, ranks, own)

        @block.tensor
        def _(pe):
            for j in range(J):
                nc.tensor.matmul(count[j][:, 0:B], k.zeros_bf[:, 0:P], k.zeros_bf[:, 0:B], start=True, stop=False)

            def histogram(i, first, last):
                for g in range(GROUP):
                    pe.wait_ge(s["onehot"], i * GROUP + g + 1)
                    for j in range(J):
                        for n in range(2):
                            ins = nc.tensor.matmul(count[j][:, 0:B], k.ones_bf[:, :], hot[:, g % 2, j, n, :],
                                                   start=False, stop=False)
                    ins.then_inc(s["counted"], 1)
            loop(pe, pairs, histogram)
            for j in range(J):
                nc.tensor.matmul(count[j][:, 0:B], k.zeros_bf[:, 0:P], k.zeros_bf[:, 0:B], start=False, stop=True)\
                  .then_inc(s["total"], 1)
            pe.wait_ge(s["prefix"], J)
            for j in range(J):
                nc.tensor.matmul(running[j][:, 0:B], k.first_row[:, :], base[:, j, :], start=True, stop=True)

            def ranks(i, first, last):
                for t in range(2 * GROUP):
                    if t % 2 == 0:
                        pe.wait_ge(s["hot"], i * GROUP + t // 2 + 1)
                    for j in range(J):
                        if not (first and t == 0):
                            b = (t - 1) % (2 * GROUP)
                            pe.wait_ge(s[f"read{j}"], i * (2 * GROUP) + t)
                            nc.tensor.matmul(running[j][:, 0:B], k.rest[:, b % 2, :], hot[:, (b // 2) % 2, j, b % 2, :],
                                             start=False, stop=True, skip_group_check=True).then_inc(s[f"added{j}"], 1)
                        nc.tensor.matmul(running[j][:, 0:B], k.before[:, t % 2, :], hot[:, (t // 2) % 2, j, t % 2, :],
                                         start=False, stop=True, skip_group_check=True).then_inc(s[f"partial{j}"], 1)
            loop(pe, pairs, ranks)

        @block.gpsimd
        def _(pool):
            if beside:
                beside.pool(ph, pool)

            def scatter(i, first, last):
                for h in range(2):
                    pool.wait_ge(s["rows_ready"], i * 2 + h + 1)
                    pool.nop(nofuse=True)
                    for j, (_, by_rank, _) in enumerate(jobs):
                        for g in range(GROUP):
                            pool.indirect_dma_start(
                                out=by_rank[:, :], out_offset=bass.IndirectOffsetOnAxis(ap=row[:, h, j, g:g + 1], axis=0),
                                in_=moved[:, h, j, g, :], in_offset=None).then_inc(scattered[h][j], 16)
            loop(pool, pairs, scatter)
            for h in range(2):
                for j in range(J):
                    pool.wait_ge(scattered[h][j], pairs * 16 * GROUP)


def digit_mask(buckets):
    return (1 << (buckets - 1).bit_length()) - 1


class Side:

    def __init__(self, name, stack, nc, T):
        def sb(what, shape, dtype=F32):
            return stack.enter_context(nc.sbuf_tensor(f"{name}_{what}", shape, dtype))
        self.name = name
        self.key = sb("key", [P, T])
        self.other = sb("other", [P, T], I32)
        self.carry = sb("carry", [P, T + 1])
        self.end = sb("end", [P, T], I32)
        self.degree = sb("degree", [P, T])
        self.in_last = sb("in_last", [P, T])
        self.last_keys = sb("last_keys", [LASTS, T])
        self.met = sb("met", [P, T, 4])


def edge_pass(nc, k, name, side, finish, width=C, table=None, index=None, weight=None, added=None, scale=None):
    T, W = k.T, width
    pairs = T // (2 * GROUP)
    sems = ["own", "gathered0", "gathered1", "features0", "features1", "staged", "scaled", "keys", "onehot",
            "weighed", "finish_own", "lasts", "carried", "summed", "copied", "pool_own", "targets", "act_own"] + finish.SEMS
    with Phase(nc, name, sems) as ph:
        s = ph.sems
        gathered = (s["gathered0"], s["gathered1"])
        features = (s["features0"], s["features1"])
        rows = ph.sbuf("rows", [P, 2, GROUP, W])
        raw = rows if table is None else ph.sbuf("raw", [P, 2, GROUP, W])
        same = ph.sbuf("same", [P, 2, 4, P])
        follows = ph.sbuf("follows", [LASTS, 2, 4, P])
        picks = ph.sbuf("picks", [P, 2, GROUP, LASTS])
        keys = ph.sbuf("keys", [P, 2, GROUP])
        last_keys = ph.sbuf("last_keys", [LASTS, 2, GROUP])
        lasts = ph.sbuf("lasts", [LASTS, 2, W])
        held = ph.sbuf("held", [1, W])
        sums = ph.sbuf("sums", [P, 2, GROUP, W])
        if scale is not None:
            scales = ph.sbuf("scales", [P, 2, GROUP])
        if table is not None:
            wanted = ph.sbuf("wanted", [P, 2, GROUP], I32)
        if added is not None:
            feats = ph.sbuf("feats", [P, 2, GROUP, W])
            added_rows = added.rearrange("(p t) c -> p t c", p=P)
        turned = [ph.psum(f"turned{n}", [P, 4, P]) for n in range(2)]
        total = [ph.psum(f"total{n}", [P, 4, W]) for n in range(2)]
        lasting = ph.psum("lasting", [LASTS, W])
        ph.edge = dict(side=side, sums=sums, same=same, keys=keys, pairs=pairs)
        finish.buffers(ph, k)
        block = ph.block()

        @block.sync
        def _(sp):
            def body(i, first, last):
                for h in range(2):
                    if added is not None:
                        if not first:
                            sp.wait_ge(s["weighed"], i * 2 + h - 1)
                        sp.dma_start(feats[:, h, :, :], added_rows[:, bass.ds((i * 2 + h) * GROUP, GROUP), :])\
                          .then_inc(features[h], 16)
                    finish.sync(ph, sp, i, h, first)
            loop(sp, pairs, body)
            finish.sync_end(ph, sp)

        @block.gpsimd
        def _(pool):
            own = Order(pool, s["pool_own"])

            def gather(i, h, first):
                if not first:
                    pool.wait_ge(s["weighed"], i * 2 + h - 1)
                own.step(nc.gpsimd.tensor_copy(wanted[:, h, :], index[:, bass.ds((i * 2 + h) * GROUP, GROUP)]))
                own.wait()
                pool.nop(nofuse=True)
                for g in range(GROUP):
                    pool.indirect_dma_start(
                        out=raw[:, h, g, :], out_offset=None, in_=table,
                        in_offset=bass.IndirectOffsetOnAxis(ap=wanted[:, h, g:g + 1], axis=0))\
                        .then_inc(gathered[h], 16)

            if table is not None:
                gather(0, 0, True)

            def body(i, first, last):
                if table is not None:
                    gather(i, 1, first)
                finish.pool(ph, pool, i, 0, first)
                if table is not None and not last:
                    gather(i + 1, 0, False)
                finish.pool(ph, pool, i, 1, first)
            loop(pool, pairs, body, own)
            finish.pool_end(ph, pool)

        @block.vector
        def _(dve):
            own = Order(dve, s["own"])
            own.step(nc.vector.memset(picks[:, :, :, :], 0.0))
            if table is None:
                own.step(nc.vector.memset(rows[:, :, :, :], 1.0))
            own.wait()
            late = Order(dve, s["finish_own"])

            def finish_late(i, h):
                if late.per is not None:
                    late.count = (i * 2 + h) * late.per
                finish.vector(ph, dve, late, i, h, False)
                if late.per is None:
                    late.per = late.count

            def body(i, first, last):
                for h in range(2):
                    b = i * 2 + h
                    at = bass.ds(b * GROUP, GROUP)
                    if not first:
                        dve.wait_ge(s["summed"], i * 8 + h * 4 - 4)
                    nc.vector.tensor_copy(keys[:, h, :], side.key[:, at]).then_inc(s["staged"], 1)
                    own.step(nc.vector.tensor_copy(last_keys[:, h, :], side.last_keys[:, at]))
                    diagonal = picks[:, h, :, :].rearrange("p g l -> p (g l)")[:, 1:2 + (GROUP - 1) * (LASTS + 1):LASTS + 1]
                    own.step(nc.vector.tensor_copy(diagonal, side.in_last[:, at]))
                    if scale is not None:
                        if not first:
                            dve.wait_ge(s["copied"], i * 8 + h * 4 - 4)
                        nc.vector.tensor_copy(scales[:, h, :], scale[:, at]).then_inc(s["scaled"], 1)
                    if table is not None:
                        dve.wait_ge(gathered[h], i * (16 * GROUP) + 16 * GROUP)
                    if weight is not None:
                        own.step(nc.vector.tensor_tensor(rows[:, h, :, :], raw[:, h, :, :],
                                                         spread(weight[:, at], W), ALU.mult))
                    if added is not None:
                        dve.wait_ge(features[h], i * 16 + 16)
                        own.step(nc.vector.tensor_tensor(rows[:, h, :, :], raw[:, h, :, :],
                                                         feats[:, h, :, :], ALU.add))
                        own.wait()
                        own.step(nc.vector.tensor_scalar(rows[:, h, :, :], rows[:, h, :, :], 0.0, None, ALU.max))
                    own.wait()
                    dve.sem_inc(s["weighed"], 1)
                    if finish.late and not (first and h == 0):
                        finish_late(i if h else i - 1, 1 - h)

                    for q, (g0, n) in enumerate(QUADS):
                        dve.wait_ge(s["keys"], i * 8 + h * 4 + q + 1)
                        if not (first and h == 0 and q < 2):
                            dve.wait_ge(s["summed"], i * 8 + h * 4 + q - 1)
                        nc.vector.tensor_tensor(same[:, q % 2, 0:n, :], turned[q % 2][:, 0:n, :],
                                                spread(keys[:, h, g0:g0 + n], P), ALU.is_equal)\
                          .then_inc(s["onehot"], 1)
                        nc.vector.tensor_tensor(follows[:, q % 2, 0:n, :], turned[q % 2][0:LASTS, 0:n, :],
                                                last_keys[:, h, g0:g0 + n].unsqueeze(2).to_broadcast([LASTS, n, P]),
                                                ALU.is_equal).then_inc(s["onehot"], 1)
                        finish.quad(ph, dve, own, i, h, q, g0, n)
                    if not finish.late:
                        finish.vector(ph, dve, own, i, h, first)
            loop(dve, pairs, body, own)
            if finish.late:
                finish_late(pairs - 1, 1)

        @block.tensor
        def _(pe):
            def turn(i, h, q, first):
                g0, n = QUADS[q]
                if q == 0:
                    pe.wait_ge(s["staged"], i * 2 + h + 1)
                if not (first and h == 0 and q < 2):
                    pe.wait_ge(s["onehot"], i * 16 + h * 8 + 2 * q - 2)
                for g in range(g0, g0 + n):
                    ins = nc.tensor.transpose(turned[q % 2][:, g - g0, :], keys[:, h, g:g + 1].to_broadcast([P, P]),
                                              k.ident[:, :])
                ins.then_inc(s["keys"], 1)

            def body(i, first, last):
                for h in range(2):
                    turn(i, h, 0, first)
                    turn(i, h, 1, first)
                    pe.wait_ge(s["weighed"], i * 2 + h + 1)
                    if not (first and h == 0):
                        pe.wait_ge(s["carried"], i * 2 + h)
                    for g in range(GROUP):
                        ins = nc.tensor.matmul(lasting[:, :], picks[:, h, g, :], rows[:, h, g, :],
                                               start=(g == 0), stop=(g == GROUP - 1))
                    ins.then_inc(s["lasts"], 1)
                    for q, (g0, n) in enumerate(QUADS):
                        pe.wait_ge(s["onehot"], i * 16 + h * 8 + 2 * q + 2)
                        if q == 0:
                            pe.wait_ge(s["carried"], i * 2 + h + 1)
                        if not (first and h == 0 and q < 2):
                            pe.wait_ge(s["copied"], i * 8 + h * 4 + q - 1)
                        for g in range(g0, g0 + n):
                            nc.tensor.matmul(total[q % 2][:, g - g0, :], same[:, q % 2, g - g0, :], rows[:, h, g, :],
                                             start=True, stop=False)
                            ins = nc.tensor.matmul(total[q % 2][:, g - g0, :], follows[:, q % 2, g - g0, :],
                                                   lasts[:, h, :], start=False, stop=True)
                        ins.then_inc(s["summed"], 1)
                        if q + 2 < len(QUADS):
                            turn(i, h, q + 2, first)
                    finish.tensor(ph, pe, i, h, first)
            loop(pe, pairs, body)

        @block.scalar
        def _(act):
            own = Order(act, s["act_own"])
            own.step(nc.scalar.activation(held[:, :], k.zeros_f[0:1, 0:W], ACT.Copy))

            def body(i, first, last):
                for h in range(2):
                    act.wait_ge(s["lasts"], i * 2 + h + 1)
                    own.wait()
                    own.step(nc.scalar.activation(lasts[:, h, :], lasting[:, :], ACT.Copy))
                    own.wait()
                    nc.scalar.activation(lasts[0:1, h, :], held[:, :], ACT.Copy).then_inc(s["carried"], 1)
                    if scale is not None:
                        act.wait_ge(s["scaled"], i * 2 + h + 1)
                    finish.slot_free(ph, act, i, h, first)
                    for q, (g0, n) in enumerate(QUADS):
                        act.wait_ge(s["summed"], i * 8 + h * 4 + q + 1)
                        if q == len(QUADS) - 1:
                            act.wait_ge(s["carried"], i * 2 + h + 1)
                            own.step(nc.scalar.activation(held[:, :], total[q % 2][0:1, n - 1, :], ACT.Copy))
                        if scale is None:
                            nc.scalar.activation(sums[:, h, g0:g0 + n, :], total[q % 2][:, 0:n, :], ACT.Copy)\
                              .then_inc(s["copied"], 1)
                            continue
                        for g in range(g0, g0 + n):
                            ins = nc.scalar.activation(sums[:, h, g, :], total[q % 2][:, g - g0, :], ACT.Copy,
                                                       scale=scales[:, h, g:g + 1])
                        ins.then_inc(s["copied"], 1)
                    finish.scalar(ph, act, own, i, h, first)
            loop(act, pairs, body, own)


class Finish:
    SEMS = []
    late = True

    def buffers(self, ph, k): pass
    def sync(self, ph, sp, i, h, first): pass
    def sync_end(self, ph, sp): pass
    def pool(self, ph, pool, i, h, first): pass
    def pool_end(self, ph, pool): pass
    def quad(self, ph, dve, own, i, h, q, g0, n): pass
    def vector(self, ph, dve, own, i, h, first): pass
    def tensor(self, ph, pe, i, h, first): pass
    def slot_free(self, ph, act, i, h, first): pass
    def scalar(self, ph, act, own, i, h, first): pass


class Store(Finish):
    SEMS = ["stored0", "stored1", "residual0", "residual1", "finished"]

    def __init__(self, nc, out, residual=None):
        self.nc, self.out, self.residual = nc, out.rearrange("(p t) c -> p t c", p=P), residual
        if residual is not None:
            self.residual = residual.rearrange("(p t) c -> p t c", p=P)

    def buffers(self, ph, k):
        if self.residual is not None:
            self.res = ph.sbuf("res", [P, 2, GROUP, C])

    def sync(self, ph, sp, i, h, first):
        s = ph.sems
        b = i * 2 + h
        if self.residual is not None:
            if not first:
                sp.wait_ge(s["finished"], b - 1)
            sp.dma_start(self.res[:, h, :, :], self.residual[:, bass.ds(b * GROUP, GROUP), :])\
              .then_inc(s[f"residual{h}"], 16)
            sp.wait_ge(s["finished"], b + 1)
        else:
            sp.wait_ge(s["copied"], b * 4 + 4)
        sp.dma_start(self.out[:, bass.ds(b * GROUP, GROUP), :], ph.edge["sums"][:, h, :, :]).then_inc(s[f"stored{h}"], 16)

    def sync_end(self, ph, sp):
        for h in range(2):
            sp.wait_ge(ph.sems[f"stored{h}"], 16 * ph.edge["pairs"])

    def vector(self, ph, dve, own, i, h, first):
        if self.residual is not None:
            s, sums = ph.sems, ph.edge["sums"]
            dve.wait_ge(s["copied"], (i * 2 + h) * 4 + 4)
            dve.wait_ge(s[f"residual{h}"], i * 16 + 16)
            self.nc.vector.scalar_tensor_tensor(sums[:, h, :, :], self.res[:, h, :, :], ALPHA, sums[:, h, :, :],
                                                ALU.mult, ALU.add).then_inc(s["finished"], 1)

    def slot_free(self, ph, act, i, h, first):
        if not first:
            act.wait_ge(ph.sems[f"stored{h}"], i * 16)


class Scatter(Finish):
    SEMS = ["scattered0", "scattered1"]

    def __init__(self, nc, k, out, end):
        self.nc, self.k, self.out, self.end = nc, k, out, end

    def buffers(self, ph, k):
        self.target = ph.sbuf("target", [P, 2, GROUP], I32)

    def pool(self, ph, pool, i, h, first):
        s = ph.sems
        b = i * 2 + h
        if not first:
            pool.wait_ge(s[f"scattered{h}"], i * (16 * GROUP))
        self.nc.gpsimd.tensor_copy(self.target[:, h, :], self.end[:, bass.ds(b * GROUP, GROUP)])\
            .then_inc(s["targets"], 1)
        pool.wait_ge(s["targets"], b + 1)
        self.ready(ph, pool, b)
        pool.nop(nofuse=True)
        for g in range(GROUP):
            pool.indirect_dma_start(
                out=self.out, out_offset=bass.IndirectOffsetOnAxis(ap=self.target[:, h, g:g + 1], axis=0),
                in_=self.rows(ph, h, g), in_offset=None, bounds_check=self.k.N - 1, oob_is_err=False)\
                .then_inc(s[f"scattered{h}"], 16)

    def ready(self, ph, pool, b):
        pool.wait_ge(ph.sems["copied"], b * 4 + 4)

    def rows(self, ph, h, g):
        return ph.edge["sums"][:, h, g, :]

    def pool_end(self, ph, pool):
        for h in range(2):
            pool.wait_ge(ph.sems[f"scattered{h}"], 16 * GROUP * ph.edge["pairs"])

    def slot_free(self, ph, act, i, h, first):
        if not first:
            act.wait_ge(ph.sems[f"scattered{h}"], i * (16 * GROUP))


class MapNodes(Finish):
    SEMS = ["scattered0", "scattered1", "rows_ready"]
    late = False

    def __init__(self, nc, k, side, out):
        self.nc, self.k, self.side, self.out = nc, k, side, out

    def buffers(self, ph, k):
        self.after = ph.sbuf("after", [P, 4, P])
        self.later = ph.sbuf("later", [P, GROUP])
        self.target = ph.sbuf("target", [P, 2, GROUP], I32)
        self.entry = ph.sbuf("entry", [P, 2, GROUP, 2])

    def quad(self, ph, dve, own, i, h, q, g0, n):
        nc, s = self.nc, ph.sems
        dve.wait_ge(s["onehot"], i * 16 + h * 8 + 2 * q + 2)
        own.step(nc.vector.tensor_tensor(
            self.after[:, 0:n, :].rearrange("p (a b) q -> p a b q", b=2),
            ph.edge["same"][:, q % 2, 0:n, :].rearrange("p (a b) q -> p a b q", b=2),
            self.k.later[:, :, :].unsqueeze(1).to_broadcast([P, n // 2, 2, P]), ALU.mult))
        own.wait()
        own.step(nc.vector.tensor_reduce(self.later[:, g0:g0 + n], self.after[:, 0:n, :], AX_X, ALU.add))

    def vector(self, ph, dve, own, i, h, first):
        nc, s, side = self.nc, ph.sems, self.side
        b = i * 2 + h
        at = bass.ds(b * GROUP, GROUP)
        own.wait()
        if not first:
            dve.wait_ge(s[f"scattered{h}"], i * (16 * GROUP))
        own.step(nc.vector.tensor_tensor(self.later[:, :], self.later[:, :],
                                         side.carry[:, bass.ds(b * GROUP + 1, GROUP)], ALU.add))
        own.wait()
        own.step(nc.vector.scalar_tensor_tensor(self.target[:, h, :], self.later[:, :], float(NOWHERE),
                                                ph.edge["keys"][:, h, :], ALU.mult, ALU.add))
        own.step(nc.vector.tensor_copy(self.entry[:, h, :, 0], self.k.edge_row[:, at]))
        dve.wait_ge(s["copied"], b * 4 + 4)
        own.step(nc.vector.tensor_copy(self.entry[:, h, :, 1], ph.edge["sums"][:, h, :, 0]))
        own.wait()
        own.step(nc.vector.tensor_copy(side.end[:, at], self.target[:, h, :]))
        own.step(nc.vector.tensor_copy(side.degree[:, at], self.entry[:, h, :, 1]))
        own.wait()
        dve.sem_inc(s["rows_ready"], 1)

    def slot_free(self, ph, act, i, h, first):
        if not first:
            act.wait_ge(ph.sems["rows_ready"], i * 2 + h - 1)

    def pool(self, ph, pool, i, h, first):
        pool.wait_ge(ph.sems["rows_ready"], i * 2 + h + 1)
        pool.nop(nofuse=True)
        for g in range(GROUP):
            pool.indirect_dma_start(
                out=self.out, out_offset=bass.IndirectOffsetOnAxis(ap=self.target[:, h, g:g + 1], axis=0),
                in_=self.entry[:, h, g, :], in_offset=None, bounds_check=self.k.N - 1, oob_is_err=False)\
                .then_inc(ph.sems[f"scattered{h}"], 16)

    def pool_end(self, ph, pool):
        for h in range(2):
            pool.wait_ge(ph.sems[f"scattered{h}"], 16 * GROUP * ph.edge["pairs"])


def load_side(nc, k, side, table, field, weight=None):
    T = k.T
    nb = T // GROUP
    with Phase(nc, f"load_{side.name}", ["loaded", "own", "keyed", "spread"]) as ph:
        s = ph.sems
        edges = ph.sbuf("edges", [P, T, 4])
        masked = ph.sbuf("masked", [LASTS, nb, GROUP])
        picked = ph.sbuf("picked", [LASTS, nb])
        shifted = ph.sbuf("shifted", [LASTS, nb])
        last_key = ph.psum("last_key", [P, T])
        block = ph.block()

        @block.sync
        def _(sp):
            sp.dma_start(edges[:, :, :], table.rearrange("(p t) c -> p t c", p=P)).then_inc(s["loaded"], 16)
            sp.wait_ge(s["loaded"], 16)

        @block.vector
        def _(dve):
            own = Order(dve, s["own"])
            own.step(nc.vector.memset(side.carry[:, :], 0.0))
            dve.wait_ge(s["loaded"], 16)
            own.step(nc.vector.tensor_copy(side.key[:, :], edges[:, :, field]))
            own.step(nc.vector.tensor_copy(side.other[:, :], edges[:, :, 1 - field]))
            if weight is not None:
                own.step(nc.vector.tensor_copy(weight[:, :], edges[:, :, 2]))
            own.wait()
            own.step(nc.vector.tensor_tensor(side.carry[:, 1:T], side.key[:, 1:T], side.key[:, 0:T - 1], ALU.is_equal))
            own.wait()
            even = side.carry[:, 0:T].rearrange("p (a b) -> p a b", b=2)
            own.step(nc.vector.tensor_tensor(even, even, k.edge_rows[:, :].unsqueeze(1).to_broadcast([P, T // 2, 2]),
                                             ALU.mult))
            own.wait()
            dve.sem_inc(s["keyed"], 1)
            dve.wait_ge(s["spread"], 1)
            own.step(nc.vector.tensor_tensor(side.in_last[:, :], side.key[:, :], last_key[:, :], ALU.is_equal))
            own.step(nc.vector.tensor_tensor(masked[:, :, :], last_key[0:LASTS, :].rearrange("p (b g) -> p b g", g=GROUP),
                                             k.pick_row[:, :].unsqueeze(1).to_broadcast([LASTS, nb, GROUP]), ALU.mult))
            own.wait()
            own.step(nc.vector.tensor_reduce(picked[:, :], masked[:, :, :], AX_X, ALU.add))
            own.wait()
            own.step(nc.vector.tensor_scalar(shifted[:, :], picked[:, :], 1.0, None, ALU.add))
            own.wait()
            own.step(nc.vector.tensor_scalar(shifted[0:1, 1:nb], picked[0:1, 0:nb - 1], 1.0, None, ALU.add))
            own.step(nc.vector.memset(shifted[0:1, 0:1], 0.0))
            own.wait()
            own.step(nc.vector.tensor_tensor(
                side.last_keys[:, :].rearrange("p (b g) -> p b g", g=GROUP),
                shifted[:, :].unsqueeze(2).to_broadcast([LASTS, nb, GROUP]),
                k.after_row[:, :].unsqueeze(1).to_broadcast([LASTS, nb, GROUP]), ALU.mult))
            own.wait()
            own.step(nc.vector.tensor_scalar(side.last_keys[:, :], side.last_keys[:, :], -1.0, None, ALU.add))
            own.wait()

        @block.tensor
        def _(pe):
            pe.wait_ge(s["keyed"], 1)
            for odd in range(2):
                ins = nc.tensor.matmul(last_key[:, odd:T:2], (k.first_row if odd else k.final_row)[:, :],
                                       side.key[:, odd:T:2], start=(odd == 0), stop=(odd == 1), skip_group_check=True)
            ins.then_inc(s["spread"], 1)


class FillRows:
    SEMS = ["fill_made", "fill_stored"]

    def __init__(self, nc, fills):
        self.nc, self.fills = nc, fills

    def buffers(self, ph):
        self.tiles = []
        for n, (table, values) in enumerate(self.fills):
            rows = table.shape[0] // P
            per = max(d for d in range(1, rows + 1) if rows % d == 0 and d * table.shape[1] <= 4096)
            self.tiles.append((ph.sbuf(f"fill{n}", [P, per, table.shape[1]]), per, rows // per, values))

    def pool(self, ph, pool):
        for tile, per, times, values in self.tiles:
            for c, value in enumerate(values):
                whole = tile[:, :, :] if len(values) == 1 else tile[:, :, c:c + 1]
                self.nc.gpsimd.memset(whole, value).then_inc(ph.sems["fill_made"], 1)

    def scalar(self, ph, act):
        stored = ph.sems["fill_stored"]
        act.wait_ge(ph.sems["fill_made"], sum(len(values) for _, values in self.fills))
        n = 0
        for (table, _), (tile, per, times, _) in zip(self.fills, self.tiles):
            for m in range(times):
                act.dma_start(table[m * per * P:(m + 1) * per * P, :].rearrange("(p t) c -> p t c", p=P),
                              tile[:, :, :]).then_inc(stored, 16)
                n += 16
        act.wait_ge(stored, n)


def join_maps(nc, k, by_src, by_dst, joined):
    n = k.NP // P
    with Phase(nc, "join", ["loaded", "joined", "stored"]) as ph:
        s = ph.sems
        one = ph.sbuf("one", [P, n, 2])
        two = ph.sbuf("two", [P, n, 2])
        both = ph.sbuf("both", [P, n, 4])
        block = ph.block()

        @block.sync
        def _(sp):
            sp.dma_start(one[:, :, :], by_src.rearrange("(p t) c -> p t c", p=P)).then_inc(s["loaded"], 16)
            sp.dma_start(two[:, :, :], by_dst.rearrange("(p t) c -> p t c", p=P)).then_inc(s["loaded"], 16)
            sp.wait_ge(s["joined"], 2)
            sp.dma_start(joined.rearrange("(p t) c -> p t c", p=P), both[:, :, :]).then_inc(s["stored"], 16)
            sp.wait_ge(s["stored"], 16)

        @block.vector
        def _(dve):
            dve.wait_ge(s["loaded"], 32)
            nc.vector.tensor_copy(both[:, :, 0:2], one[:, :, :]).then_inc(s["joined"], 1)
            nc.vector.tensor_copy(both[:, :, 2:4], two[:, :, :]).then_inc(s["joined"], 1)


class GatherMap:

    def __init__(self, nc, k, side, joined):
        self.nc, self.side, self.joined, self.pairs = nc, side, joined, k.T // (2 * GROUP)
        self.SEMS = [f"{side.name}_{what}" for what in ("staged", "got0", "got1", "kept")]

    def buffers(self, ph):
        self.wanted = ph.sbuf(f"{self.side.name}_wanted", [P, 2, GROUP], I32)
        self.got = ph.sbuf(f"{self.side.name}_got", [P, 2, GROUP, 4])

    def pool(self, ph, pool):
        nc, side = self.nc, self.side
        staged, got0, got1, kept = (ph.sems[n] for n in self.SEMS)
        gathered = (got0, got1)

        def keep(i, h):
            pool.wait_ge(gathered[h], i * (16 * GROUP) + 16 * GROUP)
            nc.gpsimd.tensor_copy(side.met[:, bass.ds((i * 2 + h) * GROUP, GROUP), :], self.got[:, h, :, :])\
              .then_inc(kept, 1)

        def body(i, first, last):
            for h in range(2):
                if not first:
                    pool.wait_ge(kept, i * 2 + h - 1)
                nc.gpsimd.tensor_copy(self.wanted[:, h, :], side.other[:, bass.ds((i * 2 + h) * GROUP, GROUP)])\
                  .then_inc(staged, 1)
                pool.wait_ge(staged, i * 2 + h + 1)
                pool.nop(nofuse=True)
                for g in range(GROUP):
                    pool.indirect_dma_start(
                        out=self.got[:, h, g, :], out_offset=None, in_=self.joined,
                        in_offset=bass.IndirectOffsetOnAxis(ap=self.wanted[:, h, g:g + 1], axis=0))\
                        .then_inc(gathered[h], 16)
                if not (first and h == 0):
                    keep(i if h else i - 1, 1 - h)
        loop(pool, self.pairs, body)
        keep(self.pairs - 1, 1)
        pool.wait_ge(kept, 2 * self.pairs)


def norm_buffers(ph):
    return (ph.sbuf("stats", [P, GROUP, 6]), ph.sbuf("moments", [P, 2, GROUP, 2]),
            ph.sbuf("spread", [P, 2, GROUP]), ph.sbuf("inverse", [P, 2, GROUP]), ph.sbuf("shift", [P, 2, GROUP]),
            ph.sbuf("varied", [P, 2, GROUP]))


NORM_SEMS = ["moments", "spread", "inverted", "coefficients", "normed"]


def norm_moments(nc, ph, dve, own, bufs, rows, h):
    stats, moments, deviation, inverse, shift, varied = bufs
    for g in range(GROUP):
        own.step(nc.vector.bn_stats(stats[:, g, :], rows[:, g, :]))
    own.wait()
    dve.nop(nofuse=True)
    for g in range(GROUP):
        own.step(nc.vector.bn_aggr(moments[:, h, g, :], stats[:, g, :]))
    own.wait()
    nc.vector.tensor_scalar(varied[:, h, :], moments[:, h, :, 1], LN_EPS, None, ALU.add).then_inc(ph.sems["moments"], 1)


def norm_coefficients(nc, ph, dve, bufs, b, h):
    s = ph.sems
    stats, moments, deviation, inverse, shift, varied = bufs
    dve.wait_ge(s["moments"], b + 1)
    dve.wait_ge(s["spread"], b + 1)
    nc.vector.reciprocal(inverse[:, h, :], deviation[:, h, :]).then_inc(s["inverted"], 1)
    dve.wait_ge(s["inverted"], b + 1)
    nc.vector.scalar_tensor_tensor(shift[:, h, :], moments[:, h, :, 0], -1.0, inverse[:, h, :],
                                   ALU.mult, ALU.mult).then_inc(s["coefficients"], 1)


def norm_root(nc, ph, act, bufs, b, h):
    act.wait_ge(ph.sems["moments"], b + 1)
    nc.scalar.activation(bufs[2][:, h, :], bufs[5][:, h, :], ACT.Sqrt).then_inc(ph.sems["spread"], 1)


def norm_apply(nc, ph, act, bufs, rows, out, b, h, part=(0, GROUP)):
    act.wait_ge(ph.sems["coefficients"], b + 1)
    for g in range(*part):
        ins = nc.scalar.activation(out[:, g, :], rows[:, g, :], ACT.Identity,
                                   bias=bufs[4][:, h, g:g + 1], scale=bufs[3][:, h, g:g + 1])
    if part[1] == GROUP:
        ins.then_inc(ph.sems["normed"], 1)


class NormScatter(Scatter):
    SEMS = Scatter.SEMS + NORM_SEMS + ["residual0", "residual1", "mixed"]
    late = False

    def __init__(self, nc, k, out, end, residual):
        super().__init__(nc, k, out, end)
        self.residual = residual.rearrange("(p t) c -> p t c", p=P)

    def buffers(self, ph, k):
        super().buffers(ph, k)
        self.norm = norm_buffers(ph)
        self.res = ph.sbuf("res", [P, 2, GROUP, C])
        self.normed = ph.sbuf("normed", [P, 2, GROUP, C])

    def sync(self, ph, sp, i, h, first):
        if not first:
            sp.wait_ge(ph.sems["mixed"], i * 2 + h - 1)
        sp.dma_start(self.res[:, h, :, :], self.residual[:, bass.ds((i * 2 + h) * GROUP, GROUP), :])\
          .then_inc(ph.sems[f"residual{h}"], 16)

    def vector(self, ph, dve, own, i, h, first):
        nc, s, sums = self.nc, ph.sems, ph.edge["sums"]
        b = i * 2 + h
        dve.wait_ge(s["copied"], b * 4 + 4)
        dve.wait_ge(s[f"residual{h}"], i * 16 + 16)
        own.step(nc.vector.scalar_tensor_tensor(sums[:, h, :, :], self.res[:, h, :, :], ALPHA, sums[:, h, :, :],
                                                ALU.mult, ALU.add))
        own.wait()
        nc.vector.scalar_tensor_tensor(sums[:, h, :, :], sums[:, h, :, :], 1.0 / THETA, self.res[:, h, :, :],
                                       ALU.mult, ALU.add).then_inc(s["mixed"], 1)
        dve.wait_ge(s["mixed"], b + 1)
        norm_moments(nc, ph, dve, own, self.norm, sums[:, h], h)
        norm_coefficients(nc, ph, dve, self.norm, b, h)

    def scalar(self, ph, act, own, i, h, first):
        b = i * 2 + h
        norm_root(self.nc, ph, act, self.norm, b, h)
        if not first:
            act.wait_ge(ph.sems[f"scattered{h}"], i * (16 * GROUP))
        norm_apply(self.nc, ph, act, self.norm, ph.edge["sums"][:, h], self.normed[:, h], b, h)

    def slot_free(self, ph, act, i, h, first):
        if not first:
            act.wait_ge(ph.sems["normed"], i * 2 + h - 1)

    def ready(self, ph, pool, b):
        pool.wait_ge(ph.sems["normed"], b + 1)

    def rows(self, ph, h, g):
        return self.normed[:, h, g, :]


class MixHops(Scatter):
    SEMS = Scatter.SEMS + ["hops0", "hops1", "hop_turned", "hop_copied", "mixed", "mixed_out"]

    def __init__(self, nc, k, out, end, hop1, hop2, folded):
        super().__init__(nc, k, out, end)
        self.hops = [hop.rearrange("(p t) c -> p t c", p=P) for hop in (hop1, hop2)]
        self.folded = folded

    def buffers(self, ph, k):
        super().buffers(ph, k)
        self.loaded = ph.sbuf("hops", [P, 2, 2, GROUP, C])
        self.turned = ph.sbuf("hops_turned", [C, 2, 3, P])
        self.mixed = ph.sbuf("mixed", [P, 2, GROUP, MIX])
        self.turning = ph.psum("turning", [C, 3, P])
        self.mixing = [ph.psum(f"mixing{n}", [P, 512]) for n in range(2)]

    def sync(self, ph, sp, i, h, first):
        s = ph.sems
        if not first:
            sp.wait_ge(s["mixed"], i * (2 * GROUP) + (h - 1) * GROUP)
        for j in range(2):
            sp.dma_start(self.loaded[:, h, j, :, :], self.hops[j][:, bass.ds((i * 2 + h) * GROUP, GROUP), :])\
              .then_inc(s[f"hops{h}"], 16)

    def tensor(self, ph, pe, i, h, first):
        nc, s = self.nc, ph.sems
        pe.wait_ge(s[f"hops{h}"], i * 32 + 32)
        pe.wait_ge(s["copied"], (i * 2 + h) * 4 + 4)

        def turn(g):
            for j in range(3):
                source = self.loaded[:, h, j, g, :] if j < 2 else ph.edge["sums"][:, h, g, :]
                ins = nc.tensor.transpose(self.turning[:, j, :], source, self.k.ident[:, :])
            ins.then_inc(s["hop_turned"], 1)
        if not (first and h == 0):
            pe.wait_ge(s["hop_copied"], i * (2 * GROUP) + h * GROUP)
        turn(0)
        for g in range(GROUP):
            t = h * GROUP + g
            pe.wait_ge(s["hop_copied"], i * (2 * GROUP) + t + 1)
            if g + 1 < GROUP:
                turn(g + 1)
            if not (first and t < 2):
                pe.wait_ge(s["mixed_out"], i * (2 * GROUP) + t - 1)
            for j in range(3):
                ins = nc.tensor.matmul(self.mixing[t % 2][:, 0:MIX], self.turned[:, t % 2, j, :],
                                       self.folded[0:C, j + 1, :], start=(j == 0), stop=(j == 2))
            ins.then_inc(s["mixed"], 1)

    def scalar(self, ph, act, own, i, h, first):
        nc, s = self.nc, ph.sems
        if not first:
            act.wait_ge(s[f"scattered{h}"], i * (16 * GROUP))

        def copy(g):
            t = h * GROUP + g
            act.wait_ge(s["hop_turned"], i * (2 * GROUP) + t + 1)
            nc.scalar.activation(self.turned[:, t % 2, :, :], self.turning[:, :, :], ACT.Copy).then_inc(s["hop_copied"], 1)
        copy(0)
        for g in range(GROUP):
            t = h * GROUP + g
            if g + 1 < GROUP:
                copy(g + 1)
            act.wait_ge(s["mixed"], i * (2 * GROUP) + t + 1)
            nc.scalar.activation(self.mixed[:, h, g, :], self.mixing[t % 2][:, 0:MIX], ACT.Copy).then_inc(s["mixed_out"], 1)

    def slot_free(self, ph, act, i, h, first):
        if not first:
            act.wait_ge(ph.sems["mixed"], i * (2 * GROUP) + (h - 1) * GROUP)

    def ready(self, ph, pool, b):
        pool.wait_ge(ph.sems["mixed_out"], b * GROUP + GROUP)

    def rows(self, ph, h, g):
        return self.mixed[:, h, g, :]


MIX = 3 * C + 4


def prepare(nc, k, src, dst):
    with Phase(nc, "prepare", ["own", "rooted", "degrees"]) as ph:
        s = ph.sems
        T = k.T
        deg = ph.sbuf("deg", [P, 6, T])
        root = ph.sbuf("root", [P, 6, T])
        inv = ph.sbuf("inv", [P, 6, T])
        lost = ph.sbuf("lost", [P, T])
        place = ph.sbuf("place", [P, T])
        block = ph.block()

        @block.vector
        def _(dve):
            own = Order(dve, s["own"])
            own.step(nc.vector.tensor_scalar(k.from_x[:, :], src.other[:, :], float(k.N - 1), None, ALU.min))
            own.step(nc.vector.tensor_scalar(k.key_x[:, :], src.key[:, :], float(k.N - 1), None, ALU.min))
            own.step(nc.vector.tensor_scalar(deg[:, 0, :], src.met[:, :, 3], 1.0, None, ALU.max))
            own.step(nc.vector.tensor_scalar(deg[:, 1, :], src.degree[:, :], 1.0, None, ALU.max))
            own.step(nc.vector.tensor_scalar(deg[:, 2, :], dst.met[:, :, 3], 1.0, None, ALU.add))
            own.step(nc.vector.tensor_scalar(deg[:, 3, :], dst.degree[:, :], 1.0, None, ALU.add))
            own.step(nc.vector.tensor_scalar(deg[:, 4, :], dst.met[:, :, 1], 1.0, None, ALU.max))
            own.wait()
            dve.sem_inc(s["degrees"], 1)
            dve.wait_ge(s["rooted"], 1)
            own.step(nc.vector.reciprocal(inv[:, 0:5, :], root[:, 0:5, :]))
            own.wait()
            own.step(nc.vector.tensor_scalar(k.w_hop[:, :], inv[:, 0, :], BETA, None, ALU.mult))
            own.step(nc.vector.tensor_copy(k.s_hop[:, :], inv[:, 1, :]))
            own.step(nc.vector.tensor_copy(k.w_gcn[:, :], inv[:, 2, :]))
            own.step(nc.vector.tensor_copy(k.s_gcn[:, :], inv[:, 3, :]))
            own.step(nc.vector.tensor_scalar(lost[:, :], dst.met[:, :, 1], 0.0, None, ALU.is_gt))
            own.wait()
            own.step(nc.vector.tensor_tensor(k.w_cheb[:, :], inv[:, 4, :], lost[:, :], ALU.mult))
            own.wait()
            own.step(nc.vector.scalar_tensor_tensor(k.w_cheb2[:, :], k.w_cheb[:, :], -1.0, k.w_cheb[:, :],
                                                    ALU.mult, ALU.mult))
            own.step(nc.vector.tensor_scalar(lost[:, :], dst.met[:, :, 2], 0.0, float(k.EP + 1), ALU.is_lt, ALU.mult))
            own.wait()
            own.step(nc.vector.tensor_tensor(k.i_cheb[:, :], dst.met[:, :, 2], lost[:, :], ALU.add))
            own.wait()
            own.step(nc.vector.tensor_scalar(lost[:, :], src.met[:, :, 0], 0.0, None, ALU.is_lt))
            own.step(nc.vector.tensor_scalar(place[:, :], src.other[:, :], float(k.EP + 1), None, ALU.add))
            own.wait()
            own.step(nc.vector.tensor_tensor(place[:, :], place[:, :], lost[:, :], ALU.mult))
            own.wait()
            own.step(nc.vector.tensor_tensor(k.i_odd[:, :], place[:, :], src.met[:, :, 0], ALU.add))
            own.step(nc.vector.tensor_scalar(lost[:, :], lost[:, :], -float(k.EP + k.NP), float(k.EP + k.NP),
                                             ALU.mult, ALU.add))
            own.wait()
            own.step(nc.vector.tensor_tensor(place[:, :], place[:, :], lost[:, :], ALU.add))
            own.wait()
            own.step(nc.vector.tensor_tensor(k.i_even[:, :], place[:, :], src.met[:, :, 0], ALU.add))
            own.wait()

        @block.scalar
        def _(act):
            act.wait_ge(s["degrees"], 1)
            nc.scalar.activation(root[:, 0:5, :], deg[:, 0:5, :], ACT.Sqrt).then_inc(s["rooted"], 1)


class GatherRows:
    SEMS = ["rows_staged", "rows_got0", "rows_got1", "rows_stored0", "rows_stored1"]

    def __init__(self, nc, k, table, index, out):
        self.nc, self.table, self.index, self.pairs = nc, table, index, k.T // (2 * GROUP)
        self.out = out.rearrange("(p t) c -> p t c", p=P)

    def buffers(self, ph):
        self.wanted = ph.sbuf("rows_wanted", [P, 2, GROUP], I32)
        self.got = ph.sbuf("rows_got", [P, 2, GROUP, C])

    def pool(self, ph, pool):
        nc = self.nc
        staged, got0, got1, stored0, stored1 = (ph.sems[n] for n in self.SEMS)
        gathered, stored = (got0, got1), (stored0, stored1)

        def store(i, h):
            pool.wait_ge(gathered[h], i * (16 * GROUP) + 16 * GROUP)
            pool.dma_start(self.out[:, bass.ds((i * 2 + h) * GROUP, GROUP), :], self.got[:, h, :, :])\
                .then_inc(stored[h], 16)

        def body(i, first, last):
            for h in range(2):
                if not first:
                    pool.wait_ge(stored[h], i * 16)
                nc.gpsimd.tensor_copy(self.wanted[:, h, :], self.index[:, bass.ds((i * 2 + h) * GROUP, GROUP)])\
                  .then_inc(staged, 1)
                pool.wait_ge(staged, i * 2 + h + 1)
                pool.nop(nofuse=True)
                for g in range(GROUP):
                    pool.indirect_dma_start(
                        out=self.got[:, h, g, :], out_offset=None, in_=self.table,
                        in_offset=bass.IndirectOffsetOnAxis(ap=self.wanted[:, h, g:g + 1], axis=0))\
                        .then_inc(gathered[h], 16)
                if not (first and h == 0):
                    store(i if h else i - 1, 1 - h)
        loop(pool, self.pairs, body)
        store(self.pairs - 1, 1)
        for h in range(2):
            pool.wait_ge(stored[h], 16 * self.pairs)


def edge_features(nc, k, W0, b0, W1, b1, out, beside):
    pairs = k.T // (2 * GROUP)
    out_rows = out.rearrange("(p t) c -> p t c", p=P)
    with Phase(nc, "features", ["loaded", "staged", "turned", "relu", "product", "biased", "s0", "s1"]
               + [n for job in beside for n in job.SEMS]) as ph:
        s = ph.sems
        stored = (s["s0"], s["s1"])
        w0 = ph.sbuf("w0", [C, 1])
        c0 = ph.sbuf("c0", [C, 1])
        w1 = ph.sbuf("w1", [C, C])
        c1 = ph.sbuf("c1", [P, C])
        weights = ph.sbuf("weights", [P, 2, GROUP])
        hidden = ph.sbuf("hidden", [C, 2, 4, P])
        made = ph.sbuf("made", [P, 2, GROUP, C])
        turned = [ph.psum(f"turned{n}", [C, 4, P]) for n in range(2)]
        product = [ph.psum(f"product{n}", [P, 4, C]) for n in range(2)]
        for job in beside:
            job.buffers(ph)
        block = ph.block()

        @block.gpsimd
        def _(pool):
            for job in beside:
                job.pool(ph, pool)

        @block.sync
        def _(sp):
            with nc.allow_non_contiguous_dma(reason="one column of 96"):
                sp.dma_start(w0[:, :], W0.rearrange("o c -> c o")).then_inc(s["loaded"], 16)
                sp.dma_start(c0[:, :], b0.rearrange("(c o) -> c o", o=1)).then_inc(s["loaded"], 16)
            sp.dma_start(w1[:, :], W1).then_inc(s["loaded"], 16)
            sp.dma_start(c1[:, :], b1.rearrange("(o c) -> o c", o=1).to_broadcast([P, C])).then_inc(s["loaded"], 16)

            def body(i, first, last):
                for h in range(2):
                    sp.wait_ge(s["biased"], i * 8 + h * 4 + 4)
                    sp.dma_start(out_rows[:, bass.ds((i * 2 + h) * GROUP, GROUP), :], made[:, h, :, :])\
                      .then_inc(stored[h], 16)
            loop(sp, pairs, body)
            for h in range(2):
                sp.wait_ge(stored[h], 16 * pairs)

        @block.vector
        def _(dve):
            dve.wait_ge(s["loaded"], 64)

            def body(i, first, last):
                for h in range(2):
                    if not first:
                        dve.wait_ge(s["turned"], i * 8 + h * 4 - 4)
                        dve.wait_ge(stored[h], i * 16)
                    nc.vector.tensor_copy(weights[:, h, :], k.edge_weight[:, bass.ds((i * 2 + h) * GROUP, GROUP)])\
                      .then_inc(s["staged"], 1)
                    for q, (g0, n) in enumerate(QUADS):
                        dve.wait_ge(s["product"], i * 8 + h * 4 + q + 1)
                        nc.vector.tensor_tensor(made[:, h, g0:g0 + n, :], product[q % 2][:, 0:n, :],
                                                c1[:, :].unsqueeze(1).to_broadcast([P, n, C]), ALU.add)\
                          .then_inc(s["biased"], 1)
            loop(dve, pairs, body)

        @block.scalar
        def _(act):
            act.wait_ge(s["loaded"], 64)

            def body(i, first, last):
                for h in range(2):
                    for q, (g0, n) in enumerate(QUADS):
                        at = i * 8 + h * 4 + q
                        act.wait_ge(s["turned"], at + 1)
                        if not (first and h * 4 + q < 2):
                            act.wait_ge(s["product"], at - 1)
                        nc.scalar.activation(hidden[:, q % 2, 0:n, :], turned[q % 2][:, 0:n, :], ACT.Relu,
                                             bias=c0[:, 0:1], scale=w0[:, 0:1]).then_inc(s["relu"], 1)
            loop(act, pairs, body)

        @block.tensor
        def _(pe):
            pe.wait_ge(s["loaded"], 64)

            def body(i, first, last):
                for h in range(2):
                    pe.wait_ge(s["staged"], i * 2 + h + 1)
                    for q, (g0, n) in enumerate(QUADS):
                        at = i * 8 + h * 4 + q
                        if not (first and h * 4 + q < 2):
                            pe.wait_ge(s["relu"], at - 1)
                        for g in range(g0, g0 + n):
                            ins = nc.tensor.transpose(turned[q % 2][:, g - g0, :],
                                                      weights[:, h, g:g + 1].to_broadcast([P, C]), k.ident[:, :])
                        ins.then_inc(s["turned"], 1)
                        pe.wait_ge(s["relu"], at + 1)
                        if not (first and h * 4 + q < 2):
                            pe.wait_ge(s["biased"], at - 1)
                        for j in range(n):
                            ins = nc.tensor.matmul(product[q % 2][:, j, :], hidden[:, q % 2, j, :], w1[:, :],
                                                   start=True, stop=True)
                        ins.then_inc(s["product"], 1)
            loop(pe, pairs, body)


def fold_weights(nc, k, w, b, attn_w, attn_b, fus_w, fus_b, folded):
    terms = {(0, 0): [(0, 1.0)], (0, 1): [(0, 1.0), (2, -1.0)], (0, 2): [(0, 1.0), (2, -1.0)],
             (1, 0): [(1, 1.0)], (1, 1): [(1, 1.0)], (1, 2): [(1, 1.0), (3, -3.0)],
             (2, 1): [(2, 2.0)], (2, 2): [(2, 2.0)], (3, 2): [(3, 4.0)]}
    made = [(i, j) for i in range(3) for j in range(i + 2)]
    slot = {ij: n for n, ij in enumerate(made)}
    order = sorted(terms)
    with Phase(nc, "fold", ["loaded", "own", "turned", "copied", "combined", "multiplied", "folded"]) as ph:
        s = ph.sems
        raw = ph.sbuf("raw", [C, len(made), C])
        flat = ph.sbuf("flat", [C, len(made), C])
        right = ph.sbuf("right", [C, 3, C + 4])
        left = ph.sbuf("left", [C, 3, 3, C + 1])
        extra = ph.sbuf("extra", [C + 1, MIX])
        turned = ph.psum("turned", [C, C])
        product = ph.psum("product", [C + 1, 512])
        block = ph.block()

        @block.sync
        def _(sp):
            n = 0
            for i, j in made:
                sp.dma_start(raw[:, slot[i, j], :], w[i][j]).then_inc(s["loaded"], 16)
                n += 16
            sp.wait_ge(s["own"], 3)
            for i in range(3):
                sp.dma_start(right[:, i, 0:C], fus_w[i * C:(i + 1) * C, :]).then_inc(s["loaded"], 16)
                with nc.allow_non_contiguous_dma(reason="small"):
                    sp.dma_start(right[:, i, C:C + 3], attn_w[i * C:(i + 1) * C, :]).then_inc(s["loaded"], 16)
                    sp.dma_start(left[:, 0, i, C:C + 1], b[i].rearrange("(c o) -> c o", o=1)).then_inc(s["loaded"], 16)
                sp.dma_start(extra[C:C + 1, i * C:(i + 1) * C], fus_b.rearrange("(o c) -> o c", o=1))\
                  .then_inc(s["loaded"], 16)
                n += 64
            sp.dma_start(extra[C:C + 1, 3 * C:3 * C + 3], attn_b.rearrange("(o c) -> o c", o=1)).then_inc(s["loaded"], 16)
            sp.wait_ge(s["loaded"], n + 16)

        n_loaded = 16 * (len(made) + 13)

        @block.vector
        def _(dve):
            own = Order(dve, s["own"])
            own.step(nc.vector.memset(right[:, :, C + 3:C + 4], 0.0))
            own.step(nc.vector.memset(extra[:, :], 0.0))
            own.step(nc.vector.memset(folded[:, :, :], 0.0))
            dve.wait_ge(s["loaded"], n_loaded)
            for n in range(len(made)):
                dve.wait_ge(s["turned"], n + 1)
                nc.vector.tensor_copy(flat[:, n, :], turned[:, :]).then_inc(s["copied"], 1)
            dve.wait_ge(s["copied"], len(made))
            for j in range(4):
                here = [i for jj, i in order if jj == j]
                if j > 0:
                    dve.wait_ge(s["folded"], j)
                for i in here:
                    parts = terms[j, i]
                    a, fa = parts[0]
                    own.step(nc.vector.tensor_scalar(left[:, j % 3, i, 0:C], flat[:, slot[i, a], :], fa, None, ALU.mult))
                    for a, fa in parts[1:]:
                        own.wait()
                        own.step(nc.vector.scalar_tensor_tensor(left[:, j % 3, i, 0:C], flat[:, slot[i, a], :], fa,
                                                                left[:, j % 3, i, 0:C], ALU.mult, ALU.add))
                own.wait()
                dve.sem_inc(s["combined"], 1)
                dve.wait_ge(s["multiplied"], j + 1)
                M = C + 1 if j == 0 else C
                lo = min(here) * C
                if j == 0:
                    nc.vector.tensor_tensor(folded[0:M, j, :], product[0:M, 0:MIX], extra[0:M, :], ALU.add)\
                      .then_inc(s["folded"], 1)
                else:
                    nc.vector.tensor_copy(folded[0:M, j, lo:MIX], product[0:M, lo:MIX]).then_inc(s["folded"], 1)
            dve.wait_ge(s["folded"], 4)

        @block.tensor
        def _(pe):
            pe.wait_ge(s["loaded"], n_loaded)
            for n in range(len(made)):
                if n:
                    pe.wait_ge(s["copied"], n)
                nc.tensor.transpose(turned[:, :], raw[:, n, :], k.ident[0:C, 0:C]).then_inc(s["turned"], 1)
            for j in range(4):
                here = [i for jj, i in order if jj == j]
                pe.wait_ge(s["combined"], j + 1)
                if j:
                    pe.wait_ge(s["folded"], j)
                M = C + 1 if j == 0 else C
                for i in here:
                    nc.tensor.matmul(product[0:M, i * C:(i + 1) * C], left[:, j % 3, i, 0:M], right[:, i, 0:C],
                                     start=True, stop=True)
                for i in here:
                    ins = nc.tensor.matmul(product[0:M, 3 * C:MIX], left[:, j % 3, i, 0:M], right[:, i, C:C + 4],
                                           start=(i == here[0]), stop=(i == here[-1]))
                ins.then_inc(s["multiplied"], 1)


class NodePass:
    weights = None
    width = C
    hidden = None
    norm = False
    SEMS = []
    loads = ()
    late = ()
    freed_by_turn = False
    out_table = None
    also = None

    def __init__(self, nc, k, name):
        self.nc, self.k, self.name = nc, k, name

    def buffers(self, ph): pass
    def setup_sync(self, ph, sp): return 0
    def before(self, ph, dve, own, i, h, first): pass
    def take(self, ph, dve, own, i, h, q, first, product, g0, n): pass
    def after(self, ph, dve, own, i, h, first, last): pass
    def scalar_extra(self, ph, act, b, h): pass
    def scalar_setup(self, ph, act): pass
    def tensor_extra(self, ph, pe, b, h, last): pass
    def tensor_setup(self, ph, pe): pass
    def scalar_before(self, ph, act, b, h): pass
    def vector_end(self, ph, dve, own): pass


def node_rows(table, b):
    return table.rearrange("(b p g) c -> p b (g c)", p=P, g=GROUP)[:, bass.ds(b, 1), :]


def flat(tile):
    return tile.rearrange("p g c -> p (g c)").unsqueeze(1)


def partial_rows(k, table, tile, load):
    start = k.NP - P * GROUP
    full, rem = (k.N - start) // GROUP, (k.N - start) % GROUP
    pairs = [(tile[0:full, :, :], table[start:start + full * GROUP, :].rearrange("(p g) c -> p g c", g=GROUP))]
    if rem:
        pairs.append((tile[full:full + 1, 0:rem, :],
                      table[start + full * GROUP:k.N, :].rearrange("(p g) c -> p g c", p=1)))
    return [(a, b) if load else (b, a) for a, b in pairs]


def whole_table(k, table):
    return table[0:k.NP - P * GROUP, :]


def quad_from(i, h, q, first, ahead=0):
    t = h * len(QUADS) + q + ahead
    pair = 2 * len(QUADS)
    return (i + t // pair if t >= pair else i), (t % pair) // len(QUADS), t % len(QUADS), first and t < pair


def run_node_pass(nc, k, d, beside=()):
    pairs = k.NP // (2 * P * GROUP)
    assert pairs > 1
    names = ["own", "setup", "used", "turned", "copied", "product", "hidden", "activated", "given", "taken",
             "rows_done", "freed", "spare", "cleared"] + [f"in{h}" for h in range(2)] + [f"out{h}" for h in range(2)] + NORM_SEMS
    if d.also is not None:
        names += ["also0", "also1", "second"]
    if d.late:
        names += ["late0", "late1", "late_used"]
    with Phase(nc, d.name, names + d.SEMS + [n for job in beside for n in job.SEMS]) as ph:
        s = ph.sems
        arrived = (s["in0"], s["in1"])
        left = (s["out0"], s["out1"])
        ph.tiles = {n: ph.sbuf(n, [P, 2, GROUP, cols]) for n, _, cols in d.loads + d.late}
        ph.rows = ph.sbuf("rows", [P, 2, GROUP, C])
        ph.normed = ph.sbuf("normed", [P, 2, GROUP, C]) if d.norm else None
        ph.norm = norm_buffers(ph) if d.norm else None
        d.buffers(ph)
        for job in beside:
            job.buffers(ph)
        multiplies = d.weights is not None
        if multiplies:
            K = d.weights.shape[0]
            turned_rows = ph.sbuf("turned_rows", [K, 2, 4, P])
            turned = [ph.psum(f"turned{n}", [C, 4, P]) for n in range(2)]
            per = 4 if d.width <= C else 1
            slots = 4
            product = [ph.psum(f"product{n}", [P, per, d.width if per > 1 else 512]) for n in range(slots)]
            if d.hidden is not None:
                hidden_rows = ph.sbuf("hidden_rows", [C, 2, 4, P])
                hidden = [ph.psum(f"hidden{n}", [C, 4, P]) for n in range(2)]
        block = ph.block()
        per_block = len(d.loads)

        @block.sync
        def _(sp):
            n_setup = d.setup_sync(ph, sp)
            assert n_setup == d.n_setup

            def body(i, first, last):
                for h in range(2):
                    b = i * 2 + h
                    if not first:
                        if d.freed_by_turn:
                            sp.wait_ge(s["turned"], i * 8 + h * 4 - 4)
                        else:
                            sp.wait_ge(s["used"], b - 1)
                    for n, table, cols in d.loads:
                        if table.shape[0] == k.N and last and h == 1:
                            sp.wait_ge(s["cleared"], 1)
                            parts = partial_rows(k, table, ph.tiles[n][:, h, :, :], True)
                            for m, (into, what) in enumerate(parts):
                                sp.dma_start(into, what).then_inc(arrived[h], 16)
                        else:
                            src = whole_table(k, table) if table.shape[0] == k.N else table
                            sp.dma_start(flat(ph.tiles[n][:, h, :, :]), node_rows(src, b)).then_inc(arrived[h], 16)
                    if d.late and not first:
                        sp.wait_ge(s["late_used"], b - 1)
                    for n, table, cols in d.late:
                        sp.dma_start(flat(ph.tiles[n][:, h, :, :]), node_rows(table, b)).then_inc(s[f"late{h}"], 16)
                    if d.also is not None and not (first and h == 0):
                        store_second(b - 1, 1 - h)

            def store_second(b, h):
                sp.wait_ge(s["second"], b + 1)
                sp.dma_start(node_rows(d.also, b), flat(ph.second[:, h, :, :])).then_inc(s[f"also{h}"], 16)
            loop(sp, pairs, body)
            if d.also is not None:
                store_second(2 * pairs - 1, 1)
                for h in range(2):
                    sp.wait_ge(s[f"also{h}"], 16 * pairs)

        @block.gpsimd
        def _(pool):
            if not multiplies:
                for job in beside:
                    job.pool(ph, pool)
                return
            pool.sem_inc(s["freed"], 2)

            def body(i, first, last):
                for h in range(2):
                    b = i * 2 + h
                    done = s["normed"] if d.norm else s["rows_done"]
                    tile = ph.normed if d.norm else ph.rows
                    pool.wait_ge(done, b + 1)
                    if d.out_table.shape[0] == k.N and last and h == 1:
                        for into, what in partial_rows(k, d.out_table, tile[:, h, :, :], False):
                            pool.dma_start(into, what).then_inc(k.stored if d.final else left[h], 16)
                    else:
                        table = whole_table(k, d.out_table) if d.out_table.shape[0] == k.N else d.out_table
                        pool.dma_start(node_rows(table, b), flat(tile[:, h, :, :])).then_inc(left[h], 16)
                    if not (d.final and last and h == 1):
                        pool.wait_ge(left[h], i * 16 + 16)
                        pool.sem_inc(s["freed"], 1)
            loop(pool, pairs, body)
            if d.final:
                start = k.NP - P * GROUP
                pool.wait_ge(k.stored, 32 if (k.N - start) % GROUP else 16)

        @block.vector
        def _(dve):
            own = Order(dve, s["own"])
            if d.n_setup:
                dve.wait_ge(s["setup"], 16 * d.n_setup)
            if multiplies and d.weights.shape[0] == C + 1:
                nc.vector.memset(turned_rows[C:C + 1, :, :, :], 1.0).then_inc(s["spare"], 1)

            def start(i, h, first, last):
                b = i * 2 + h
                extra = 0
                for n, table, cols in d.loads:
                    if table.shape[0] == k.N and last and h == 1:
                        if not first:
                            dve.wait_ge(s["used"], b - 1)
                        nc.vector.memset(ph.tiles[n][:, h, :, :], 0.0).then_inc(s["cleared"], 1)
                        extra = len(partial_rows(k, table, ph.tiles[n][:, h, :, :], True)) - 1
                dve.wait_ge(arrived[h], i * (16 * per_block) + 16 * (per_block + extra))
                if not multiplies and not first:
                    dve.wait_ge(s["normed"], b - 1)
                d.before(ph, dve, own, i, h, first)

            def start_next(i, h, first, last):
                if h == 0:
                    start(i, 1, first, last)
                elif not last:
                    start(i + 1, 0, False, False)

            def body(i, first, last):
                for h in range(2):
                    b = i * 2 + h
                    follows = not (first and h == 0)
                    if d.late:
                        dve.wait_ge(s[f"late{h}"], i * (16 * len(d.late)) + 16 * len(d.late))
                    if not multiplies:
                        start(i, h, first, last)
                    elif d.width <= C:
                        for q, (g0, n) in enumerate(QUADS):
                            at = i * 8 + h * 4 + q
                            dve.wait_ge(s["product"], at + 1)
                            if q == 0 and not first:
                                if d.norm:
                                    dve.wait_ge(s["normed"], b - 1)
                                else:
                                    dve.wait_ge(s["freed"], b + 1)
                            d.take(ph, dve, own, i, h, q, first, product[q % slots], g0, n).then_inc(s["taken"], 1)
                            if q == 2 and d.norm and follows:
                                norm_coefficients(nc, ph, dve, ph.norm, b - 1, 1 - h)
                            if q == (1 if d.hidden is not None else 2):
                                start_next(i, h, first, last)
                    else:
                        for g in range(GROUP):
                            dve.wait_ge(s["product"], (i * 2 + h) * GROUP + g + 1)
                            d.take(ph, dve, own, i, h, 0, first, product[(h * GROUP + g) % slots], g, 1)\
                             .then_inc(s["taken"], 1)
                            if g == QUADS[2][0] + QUADS[2][1] - 1:
                                start_next(i, h, first, last)
                        if not first:
                            dve.wait_ge(s["freed"], b + 1)
                    d.after(ph, dve, own, i, h, first, last)
                    if d.norm:
                        own.wait()
                        norm_moments(nc, ph, dve, own, ph.norm, ph.rows[:, h], h)
                        if not multiplies:
                            norm_coefficients(nc, ph, dve, ph.norm, b, h)
            if multiplies:
                start(0, 0, True, False)
            loop(dve, pairs, body, own)
            if d.norm and multiplies:
                norm_coefficients(nc, ph, dve, ph.norm, 2 * pairs - 1, 1)
            d.vector_end(ph, dve, own)

        @block.scalar
        def _(act):
            d.scalar_setup(ph, act)

            def copy(i, h, q, first):
                n = QUADS[q][1]
                at = i * 8 + h * 4 + q
                act.wait_ge(s["turned"], at + 1)
                if not (first and h * 4 + q < 2):
                    if d.hidden is not None:
                        act.wait_ge(s["hidden"], at - 1)
                    elif d.width <= C:
                        act.wait_ge(s["product"], at - 1)
                    else:
                        back = (h * 4 + q - 2) % 8
                        done = (back // 4) * GROUP + QUADS[back % 4][0] + QUADS[back % 4][1]
                        act.wait_ge(s["product"], i * (2 * GROUP) + done - (2 * GROUP if h * 4 + q < 2 else 0))
                nc.scalar.activation(turned_rows[0:C, q % 2, 0:n, :], turned[q % 2][:, 0:n, :], ACT.Copy)\
                  .then_inc(s["copied"], 1)

            def activate(i, h, q, first):
                n = QUADS[q][1]
                at = i * 8 + h * 4 + q
                act.wait_ge(s["hidden"], at + 1)
                if not (first and h * 4 + q < 2):
                    act.wait_ge(s["product"], at - 1)
                nc.scalar.activation(hidden_rows[:, q % 2, 0:n, :], hidden[q % 2][:, 0:n, :], ACT.Relu,
                                     bias=d.hidden[1][:, 0:1]).then_inc(s["activated"], 1)

            def norm(h, b, part):
                if part[0] == 0:
                    act.wait_ge(s["freed"], b + 1)
                norm_apply(nc, ph, act, ph.norm, ph.rows[:, h], ph.normed[:, h], b, h, part)

            def body(i, first, last):
                for h in range(2):
                    b = i * 2 + h
                    follows = not (first and h == 0)
                    if not multiplies:
                        norm_root(nc, ph, act, ph.norm, b, h)
                        if not first:
                            act.wait_ge(left[h], i * 16)
                        norm_apply(nc, ph, act, ph.norm, ph.rows[:, h], ph.normed[:, h], b, h)
                        act.wait_ge(s["normed"], b + 1)
                        act.dma_start(node_rows(d.out_table, b), flat(ph.normed[:, h, :, :])).then_inc(left[h], 16)
                        continue
                    for q in range(len(QUADS)):
                        if d.hidden is None:
                            copy(i, h, q, first)
                        else:
                            if not (last and h == 1 and q == 3):
                                activate(*quad_from(i, h, q, first, 1))
                            if not (last and h == 1 and q >= 2):
                                copy(*quad_from(i, h, q, first, 2))
                        if q == 1 and follows:
                            d.scalar_extra(ph, act, b - 1, 1 - h)
                        if q == 2:
                            if h == 0:
                                d.scalar_before(ph, act, b + 1, 1)
                            elif not last:
                                d.scalar_before(ph, act, b + 1, 0)
                        if d.norm and follows:
                            if q == 0 and not first:
                                norm(h, b - 2, (GROUP // 2, GROUP))
                            elif q == 2:
                                norm_root(nc, ph, act, ph.norm, b - 1, 1 - h)
                            elif q == 3:
                                norm(1 - h, b - 1, (0, GROUP // 2))
            if multiplies:
                d.scalar_before(ph, act, 0, 0)
                if d.hidden is not None:
                    copy(0, 0, 0, True)
                    copy(0, 0, 1, True)
                    activate(0, 0, 0, True)
            loop(act, pairs, body)
            if not multiplies:
                for h in range(2):
                    act.wait_ge(left[h], 16 * pairs)
                return
            last = 2 * pairs - 1
            d.scalar_extra(ph, act, last, 1)
            if d.norm:
                norm(0, last - 1, (GROUP // 2, GROUP))
                norm_root(nc, ph, act, ph.norm, last, 1)
                norm(1, last, (0, GROUP))

        @block.tensor
        def _(pe):
            if not multiplies:
                return
            if d.n_setup:
                pe.wait_ge(s["setup"], 16 * d.n_setup)
            if d.weights.shape[0] == C + 1:
                pe.wait_ge(s["spare"], 1)
            d.tensor_setup(ph, pe)

            def turn(i, h, q, first):
                g0, n = QUADS[q]
                if q == 0:
                    pe.wait_ge(s["given"], i * 2 + h + 1)
                if not (first and h * 4 + q < 2):
                    pe.wait_ge(s["copied"], i * 8 + h * 4 + q - 1)
                for g in range(g0, g0 + n):
                    ins = nc.tensor.transpose(turned[q % 2][:, g - g0, :], ph.given[:, h, g, :], k.ident[:, :])
                ins.then_inc(s["turned"], 1)

            def hide(i, h, q, first):
                n = QUADS[q][1]
                at = i * 8 + h * 4 + q
                pe.wait_ge(s["copied"], at + 1)
                if not (first and h * 4 + q < 2):
                    pe.wait_ge(s["activated"], at - 1)
                nc.tensor.matmul(hidden[q % 2][:, 0:n, :].rearrange("c g p -> c (g p)"), d.hidden[0][:, :],
                                 turned_rows[0:C, q % 2, 0:n, :].rearrange("c g p -> c (g p)"),
                                 start=True, stop=True).then_inc(s["hidden"], 1)

            def multiply(i, h, q, first):
                g0, n = QUADS[q]
                at = i * 8 + h * 4 + q
                if d.hidden is not None:
                    pe.wait_ge(s["activated"], at + 1)
                    left_side = hidden_rows
                else:
                    pe.wait_ge(s["copied"], at + 1)
                    left_side = turned_rows
                if d.width <= C:
                    if not first:
                        pe.wait_ge(s["taken"], at - slots + 1)
                    elif h * 4 + q >= slots:
                        pe.wait_ge(s["taken"], at - slots + 1)
                    for j in range(n):
                        ins = nc.tensor.matmul(product[q % slots][:, j, 0:d.width], left_side[:, q % 2, j, :], d.weights,
                                               start=True, stop=True)
                    ins.then_inc(s["product"], 1)
                else:
                    for j in range(n):
                        t = h * GROUP + g0 + j
                        if not (first and t < slots):
                            pe.wait_ge(s["taken"], i * (2 * GROUP) + t - slots + 1)
                        nc.tensor.matmul(product[t % slots][:, 0, 0:d.width], left_side[:, q % 2, j, :], d.weights,
                                         start=True, stop=True).then_inc(s["product"], 1)

            lead = 2 if d.hidden is not None else 1

            def body(i, first, last):
                for h in range(2):
                    for q in range(len(QUADS)):
                        crosses = q + lead > 3
                        if crosses and q == 3:
                            multiply(i, h, q, first)
                        if d.hidden is not None and not (last and h == 1 and q == 3):
                            hide(*quad_from(i, h, q, first, 1))
                        if crosses and q < 3:
                            multiply(i, h, q, first)
                        if not (last and h == 1 and crosses):
                            turn(*quad_from(i, h, q, first, lead))
                        if not crosses:
                            multiply(i, h, q, first)
                        if q == 1 and not (first and h == 0):
                            d.tensor_extra(ph, pe, i * 2 + h - 1, 1 - h, False)
            turn(0, 0, 0, True)
            if d.hidden is not None:
                turn(0, 0, 1, True)
                hide(0, 0, 0, True)
            loop(pe, pairs, body)
            d.tensor_extra(ph, pe, 2 * pairs - 1, 1, True)


def row_of(vector):
    return vector.rearrange("(o c) -> o c", o=1).to_broadcast([P, vector.shape[0]])


class StartPass(NodePass):
    norm, n_setup, final = True, 0, False

    def __init__(self, nc, k, name, x, scaled, out):
        super().__init__(nc, k, name)
        self.loads, self.also, self.out_table = (("x", x, C),), scaled, out

    def buffers(self, ph):
        ph.second = ph.sbuf("second", [P, 2, GROUP, C])

    def before(self, ph, dve, own, i, h, first):
        nc = self.nc
        if not first:
            dve.wait_ge(ph.sems[f"also{h}"], i * 16)
        nc.vector.tensor_scalar(ph.second[:, h, :, :], ph.tiles["x"][:, h, :, :], ALPHA, None, ALU.mult)\
          .then_inc(ph.sems["second"], 1)
        own.step(nc.vector.tensor_scalar(ph.rows[:, h, :, :], ph.tiles["x"][:, h, :, :], 1.0 + ALPHA / THETA, None,
                                         ALU.mult))
        dve.wait_ge(ph.sems["second"], i * 2 + h + 1)
        own.wait()
        dve.sem_inc(ph.sems["used"], 1)


class GcnPass(NodePass):
    norm, n_setup, final = True, 3, False

    def __init__(self, nc, k, name, x, sums, joined, W, b, slope, out):
        super().__init__(nc, k, name)
        self.loads, self.late, self.out_table = (("x", x, C), ("sums", sums, C), ("map", joined, 4)), (("skip", x, C),), out
        self.W, self.b, self.slope = W, b, slope

    def buffers(self, ph):
        self.w = ph.sbuf("w", [C + 1, C])
        self.weights = self.w[:, :]
        self.a = ph.sbuf("a", [P, 1])
        ph.given = ph.sbuf("given", [P, 2, GROUP, C])
        self.degree = ph.sbuf("degree", [P, GROUP])
        self.low = ph.sbuf("low", [P, GROUP, C])

    def setup_sync(self, ph, sp):
        sp.dma_start(self.w[0:C, :], self.W).then_inc(ph.sems["setup"], 16)
        sp.dma_start(self.w[C:C + 1, :], self.b.rearrange("(o c) -> o c", o=1)).then_inc(ph.sems["setup"], 16)
        sp.dma_start(self.a[:, :], row_of(self.slope)).then_inc(ph.sems["setup"], 16)
        return 3

    def before(self, ph, dve, own, i, h, first):
        nc, x, sums = self.nc, ph.tiles["x"], ph.tiles["sums"]
        own.step(nc.vector.tensor_scalar(self.degree[:, :], ph.tiles["map"][:, h, :, 3], 1.0, None, ALU.add))
        own.wait()
        own.step(nc.vector.reciprocal(self.degree[:, :], self.degree[:, :]))
        own.wait()
        own.step(nc.vector.tensor_tensor(self.low[:, :, :], x[:, h, :, :], spread(self.degree[:, :], C), ALU.mult))
        own.wait()
        nc.vector.tensor_tensor(ph.given[:, h, :, :], sums[:, h, :, :], self.low[:, :, :], ALU.add)\
          .then_inc(ph.sems["given"], 1)
        dve.wait_ge(ph.sems["given"], i * 2 + h + 1)
        dve.sem_inc(ph.sems["used"], 1)

    def take(self, ph, dve, own, i, h, q, first, product, g0, n):
        return self.nc.vector.tensor_copy(ph.rows[:, h, g0:g0 + n, :], product[:, 0:n, :])

    def after(self, ph, dve, own, i, h, first, last):
        nc, rows = self.nc, ph.rows[:, h, :, :]
        dve.wait_ge(ph.sems["taken"], i * 8 + h * 4 + 4)
        own.step(nc.vector.tensor_scalar(self.low[:, :, :], rows, 0.0, self.a[:, 0:1], ALU.min, ALU.mult))
        own.wait()
        own.step(nc.vector.scalar_tensor_tensor(rows, rows, 0.0, self.low[:, :, :], ALU.max, ALU.add))
        own.wait()
        own.step(nc.vector.tensor_tensor(rows, rows, ph.tiles["skip"][:, h, :, :], ALU.add))
        own.wait()
        dve.sem_inc(ph.sems["late_used"], 1)


class ChebPass(NodePass):
    norm, n_setup, final, width, freed_by_turn = False, 0, False, MIX, True
    SEMS = ["scored", "exponent", "shaped", "squared", "counted"]

    def __init__(self, nc, k, name, x, mixed, joined, folded, totals, out):
        super().__init__(nc, k, name)
        self.loads, self.late, self.out_table = (("x", x, C), ("map", joined, 4)), (("mixed", mixed, MIX),), out
        self.weights, self.totals = folded[:, 0, :], totals
        self.hidden = None

    def buffers(self, ph):
        ph.given = ph.tiles["x"]
        self.root = ph.sbuf("root", [P, 2, GROUP])
        self.factor = ph.sbuf("factor", [P, 2, GROUP])
        self.has = ph.sbuf("has", [P, GROUP])
        self.score = ph.sbuf("score", [P, 2, GROUP, 3])
        self.most = ph.sbuf("most", [P, GROUP])
        self.part = ph.sbuf("part", [P, GROUP, C])
        self.square = ph.sbuf("square", [P, 2, GROUP, C])
        self.valid = ph.sbuf("valid", [P, GROUP])
        self.total = ph.psum("total", [1, 512])

    def before(self, ph, dve, own, i, h, first):
        nc, s = self.nc, ph.sems
        b = i * 2 + h
        own.step(nc.vector.tensor_scalar(self.factor[:, h, :], ph.tiles["map"][:, h, :, 1], 1.0, None, ALU.max))
        own.step(nc.vector.tensor_scalar(self.has[:, :], ph.tiles["map"][:, h, :, 1], 0.0, -1.0, ALU.is_gt, ALU.mult))
        own.wait()
        dve.sem_inc(s["given"], 1)
        dve.wait_ge(s["shaped"], b + 1)
        own.step(nc.vector.reciprocal(self.factor[:, h, :], self.root[:, h, :]))
        own.wait()
        own.step(nc.vector.tensor_tensor(self.factor[:, h, :], self.factor[:, h, :], self.has[:, :], ALU.mult))
        own.wait()

    def take(self, ph, dve, own, i, h, q, first, product, g, n):
        mixed = ph.tiles["mixed"]
        return self.nc.vector.scalar_tensor_tensor(mixed[:, h, g, :], mixed[:, h, g, :], self.factor[:, h, g:g + 1],
                                                   product[:, 0, 0:MIX], ALU.mult, ALU.add)

    def after(self, ph, dve, own, i, h, first, last):
        nc, s, mixed, rows = self.nc, ph.sems, ph.tiles["mixed"], ph.rows[:, h, :, :]
        b = i * 2 + h
        score = self.score[:, h, :, :]
        dve.wait_ge(s["taken"], b * GROUP + GROUP)
        scores = mixed[:, h, :, 3 * C:3 * C + 3]
        own.step(nc.vector.tensor_reduce(self.most[:, :], scores, AX_X, ALU.max))
        own.wait()
        nc.vector.tensor_tensor(score, scores, spread(self.most[:, :], 3), ALU.subtract).then_inc(s["scored"], 1)
        dve.wait_ge(s["exponent"], b + 1)
        own.step(nc.vector.tensor_reduce(self.most[:, :], score, AX_X, ALU.add))
        own.wait()
        own.step(nc.vector.reciprocal(self.most[:, :], self.most[:, :]))
        own.wait()
        own.step(nc.vector.tensor_tensor(score, score, spread(self.most[:, :], 3), ALU.mult))
        own.wait()
        if not first:
            dve.wait_ge(s["counted"], b - 1)
        own.step(nc.vector.tensor_tensor(rows, mixed[:, h, :, 0:C], spread(score[:, :, 0], C), ALU.mult))
        for n in (1, 2):
            own.step(nc.vector.tensor_tensor(self.part[:, :, :], mixed[:, h, :, n * C:(n + 1) * C],
                                             spread(score[:, :, n], C), ALU.mult))
            own.wait()
            own.step(nc.vector.tensor_tensor(rows, rows, self.part[:, :, :], ALU.add))
            own.wait()
        dve.sem_inc(s["late_used"], 1)
        own.step(nc.vector.tensor_tensor(self.square[:, h, :, :], rows, rows, ALU.mult))
        own.wait()
        dve.sem_inc(s["squared"], 1)
        dve.sem_inc(s["rows_done"], 1)

    def scalar_before(self, ph, act, b, h):
        act.wait_ge(ph.sems["given"], b + 1)
        self.nc.scalar.activation(self.root[:, h, :], self.factor[:, h, :], ACT.Sqrt).then_inc(ph.sems["shaped"], 1)

    def scalar_extra(self, ph, act, b, h):
        act.wait_ge(ph.sems["scored"], b + 1)
        self.nc.scalar.activation(self.score[:, h, :, :], self.score[:, h, :, :], ACT.Exp).then_inc(ph.sems["exponent"], 1)

    def tensor_setup(self, ph, pe):
        for n in range(2):
            self.nc.tensor.matmul(self.total[0:1, n * C:(n + 1) * C], self.k.zeros_f[:, 0:1],
                                  self.k.zeros_f[:, n * C:(n + 1) * C], start=True, stop=False, skip_group_check=True)

    def tensor_extra(self, ph, pe, b, h, last):
        nc = self.nc
        pe.wait_ge(ph.sems["squared"], b + 1)
        for g in range(GROUP):
            count = self.k.valid[:, g:g + 1] if last else self.k.ones[:, 0:1]
            for n, source in enumerate((ph.rows, self.square)):
                ins = nc.tensor.matmul(self.total[0:1, n * C:(n + 1) * C], count, source[:, h, g, :],
                                       start=False, stop=(last and g == GROUP - 1),
                                       skip_group_check=True)
        ins.then_inc(ph.sems["counted"], 1)

    def vector_end(self, ph, dve, own):
        dve.wait_ge(ph.sems["counted"], self.k.NP // (P * GROUP))
        own.step(self.nc.vector.tensor_copy(self.totals[:, :], self.total[0:1, 0:2 * C]))
        own.wait()


class NormPass(NodePass):
    norm, n_setup, final = True, 0, False

    def __init__(self, nc, k, name, x, h, coefficients, out):
        super().__init__(nc, k, name)
        self.loads, self.out_table, self.co = (("x", x, C), ("h", h, C)), out, coefficients

    def before(self, ph, dve, own, i, h, first):
        nc, rows, mid = self.nc, ph.rows[:, h, :, :], ph.tiles["h"][:, h, :, :]
        wide = lambda n: self.co[:, n, :].unsqueeze(1).to_broadcast([P, GROUP, C])
        own.step(nc.vector.tensor_tensor(mid, mid, wide(0), ALU.mult))
        own.wait()
        own.step(nc.vector.tensor_tensor(mid, mid, wide(1), ALU.add))
        own.wait()
        own.step(nc.vector.scalar_tensor_tensor(rows, mid, 0.0, ph.tiles["x"][:, h, :, :], ALU.max, ALU.add))
        own.wait()
        dve.sem_inc(ph.sems["used"], 1)


class GinePass(NodePass):
    n_setup = 4

    def __init__(self, nc, k, name, x, sums, W0, b0, W1, b1, out, skip=None, final=False):
        super().__init__(nc, k, name)
        self.loads = (("x", x, C), ("sums", sums, C))
        self.late = (("skip", skip, C),) if skip is not None else ()
        self.out_table, self.skip, self.final, self.norm = out, skip, final, skip is not None
        self.sources = (W0, b0, W1, b1)

    def buffers(self, ph):
        self.w0, self.w1 = ph.sbuf("w0", [C, C]), ph.sbuf("w1", [C, C])
        self.c0, self.c1 = ph.sbuf("c0", [C, 1]), ph.sbuf("c1", [P, C])
        self.weights, self.hidden = self.w1[:, :], (self.w0, self.c0)
        ph.given = ph.sbuf("given", [P, 2, GROUP, C])

    def setup_sync(self, ph, sp):
        W0, b0, W1, b1 = self.sources
        setup = ph.sems["setup"]
        sp.dma_start(self.w0[:, :], W0).then_inc(setup, 16)
        sp.dma_start(self.w1[:, :], W1).then_inc(setup, 16)
        with self.nc.allow_non_contiguous_dma(reason="one column of 96"):
            sp.dma_start(self.c0[:, :], b0.rearrange("(c o) -> c o", o=1)).then_inc(setup, 16)
        sp.dma_start(self.c1[:, :], row_of(b1)).then_inc(setup, 16)
        return 4

    def scalar_setup(self, ph, act):
        act.wait_ge(ph.sems["setup"], 64)

    def before(self, ph, dve, own, i, h, first):
        sums = ph.tiles["sums"]
        self.nc.vector.tensor_tensor(ph.given[:, h, :, :], sums[:, h, :, :], ph.tiles["x"][:, h, :, :], ALU.add)\
            .then_inc(ph.sems["given"], 1)
        dve.wait_ge(ph.sems["given"], i * 2 + h + 1)
        dve.sem_inc(ph.sems["used"], 1)

    def take(self, ph, dve, own, i, h, q, first, product, g0, n):
        return self.nc.vector.tensor_tensor(ph.rows[:, h, g0:g0 + n, :], product[:, 0:n, :],
                                            self.c1[:, :].unsqueeze(1).to_broadcast([P, n, C]), ALU.add)

    def after(self, ph, dve, own, i, h, first, last):
        nc, rows = self.nc, ph.rows[:, h, :, :]
        dve.wait_ge(ph.sems["taken"], i * 8 + h * 4 + 4)
        if self.skip is not None:
            own.step(nc.vector.scalar_tensor_tensor(rows, rows, 0.0, ph.tiles["skip"][:, h, :, :], ALU.max, ALU.add))
            own.wait()
            dve.sem_inc(ph.sems["late_used"], 1)
        else:
            own.step(nc.vector.tensor_scalar(rows, rows, 0.0, None, ALU.max))
            own.wait()
            dve.sem_inc(ph.sems["rows_done"], 1)


def batch_norm(nc, k, totals, gamma, beta, coefficients):
    with Phase(nc, "batch", ["loaded", "own", "rooted", "varied", "ready", "wide"]) as ph:
        s = ph.sems
        given = ph.sbuf("given", [1, 2, C])
        mean = ph.sbuf("mean", [1, 2, C])
        square = ph.sbuf("square", [1, C])
        root = ph.sbuf("root", [1, C])
        pair = ph.sbuf("pair", [1, 2, C])
        wide = ph.psum("wide_rows", [P, 512])
        block = ph.block()

        @block.sync
        def _(sp):
            sp.dma_start(given[:, 0, :], gamma.rearrange("(o c) -> o c", o=1)).then_inc(s["loaded"], 16)
            sp.dma_start(given[:, 1, :], beta.rearrange("(o c) -> o c", o=1)).then_inc(s["loaded"], 16)
            sp.wait_ge(s["loaded"], 32)

        @block.vector
        def _(dve):
            own = Order(dve, s["own"])
            own.step(nc.vector.tensor_scalar(mean[:, :, :].rearrange("p a c -> p (a c)"), totals[:, :], 1.0 / k.N, None,
                                             ALU.mult))
            own.wait()
            own.step(nc.vector.tensor_tensor(square[:, :], mean[:, 0, :], mean[:, 0, :], ALU.mult))
            own.wait()
            own.step(nc.vector.scalar_tensor_tensor(square[:, :], mean[:, 1, :], BN_EPS, square[:, :],
                                                    ALU.add, ALU.subtract))
            own.wait()
            dve.sem_inc(s["varied"], 1)
            dve.wait_ge(s["rooted"], 1)
            dve.wait_ge(s["loaded"], 32)
            own.step(nc.vector.reciprocal(square[:, :], root[:, :]))
            own.wait()
            own.step(nc.vector.tensor_tensor(pair[:, 0, :], square[:, :], given[:, 0, :], ALU.mult))
            own.wait()
            own.step(nc.vector.tensor_tensor(square[:, :], mean[:, 0, :], pair[:, 0, :], ALU.mult))
            own.wait()
            nc.vector.tensor_tensor(pair[:, 1, :], given[:, 1, :], square[:, :], ALU.subtract).then_inc(s["ready"], 1)
            dve.wait_ge(s["wide"], 1)
            own.step(nc.vector.tensor_copy(coefficients[:, :, :].rearrange("p a c -> p (a c)"), wide[:, 0:2 * C]))
            own.wait()

        @block.scalar
        def _(act):
            act.wait_ge(s["varied"], 1)
            nc.scalar.activation(root[:, :], square[:, :], ACT.Sqrt).then_inc(s["rooted"], 1)

        @block.tensor
        def _(pe):
            pe.wait_ge(s["ready"], 1)
            nc.tensor.matmul(wide[:, 0:2 * C], k.ones[0:1, :], pair[:, :, :].rearrange("p a c -> p (a c)"),
                             start=True, stop=True).then_inc(s["wide"], 1)


class Resident:

    def __init__(self, nc, stack, N, E):
        pair = 2 * GROUP * P
        self.N, self.E = N, E
        self.EP, self.NP = -(-E // pair) * pair, -(-N // pair) * pair
        self.T = self.EP // P
        assert self.NP - P * GROUP < N and self.EP > E and N < NOWHERE

        def sb(what, shape, dtype=F32):
            return stack.enter_context(nc.sbuf_tensor(what, shape, dtype))
        self.ident = sb("ident", [P, P])
        self.before = sb("before", [P, 2, P], BF16)
        self.rest = sb("rest", [P, 2, P], BF16)
        self.later = sb("later", [P, 2, P])
        self.first_row = sb("first_row", [P, P])
        self.final_row = sb("final_row", [P, P])
        self.pick_row = sb("pick_row", [LASTS, GROUP])
        self.after_row = sb("after_row", [LASTS, GROUP])
        self.edge_rows = sb("edge_rows", [P, 2])
        self.ones_bf = sb("ones_bf", [P, P], BF16)
        self.zeros_bf = sb("zeros_bf", [P, 512], BF16)
        self.zeros_f = sb("zeros_f", [P, 2 * C])
        self.valid = sb("valid", [P, GROUP])
        self.ones = sb("ones", [P, P])
        self.iota = sb("iota", [P, 512])
        self.edge_row = sb("edge_row", [P, self.T])
        self.edge_weight = sb("edge_weight", [P, self.T])
        self.from_x = sb("from_x", [P, self.T], I32)
        self.key_x = sb("key_x", [P, self.T], I32)
        self.i_cheb = sb("i_cheb", [P, self.T], I32)
        self.i_odd = sb("i_odd", [P, self.T], I32)
        self.i_even = sb("i_even", [P, self.T], I32)
        self.w_hop = sb("w_hop", [P, self.T])
        self.w_gcn = sb("w_gcn", [P, self.T])
        self.w_cheb = sb("w_cheb", [P, self.T])
        self.w_cheb2 = sb("w_cheb2", [P, self.T])
        self.s_hop = sb("s_hop", [P, self.T])
        self.s_gcn = sb("s_gcn", [P, self.T])
        self.folded = sb("folded", [C + 1, 4, MIX])
        self.totals = sb("totals", [1, 2 * C])
        self.coefficients = sb("coefficients", [P, 2, C])
        self.stored = nc.alloc_semaphore("output_stored")


def graph_layers(nc, out, x, src, dst, edge_weight, W, b, slope, w2, b2, w3, b3, w4, b4, attn_w, attn_b,
                 fus_w, fus_b, gamma, beta, W_l0, b_l0, W_l1, b_l1, W00, b00, W01, b01, W10, b10, W11, b11):
    with ExitStack() as stack:
        k = Resident(nc, stack, x.shape[0], src.shape[0])
        by_src, by_dst = Side("src", stack, nc, k.T), Side("dst", stack, nc, k.T)

        def table(name, rows, cols):
            return nc.dram_tensor(name, (rows, cols), F32, kind="Internal").ap()
        EP, NP = k.EP, k.NP
        unsorted = table("edges_unsorted", EP, 4)
        half_src, half_dst, ordered_src, ordered_dst = (
            table(n, EP, 4) for n in ("edges_half_src", "edges_half_dst", "edges_by_src", "edges_by_dst"))
        map_src, map_dst, joined = table("map_src", NP, 2), table("map_dst", NP, 2), table("map_joined", NP, 4)
        hops = table("hops", EP + NP + EP, C)
        hop1, hop2 = table("hop1", EP + P, C), table("hop2", EP + P, C)
        h_rows, feats = table("h_rows", EP, C), table("features", EP, C)
        sums, mixed = table("sums", NP, C), table("mixed", NP, MIX)
        x1, x2, x3, mid, conv = (table(n, NP, C) for n in ("x1", "x2", "x3", "mid", "conv"))

        constants(nc, k)
        fills = FillRows(nc, [(map_src, (-1.0, 0.0)), (map_dst, (-1.0, 0.0)), (sums, (0.0,)), (mixed, (0.0,)),
                              (hop1[EP:EP + P, :], (0.0,)), (hop2[EP:EP + P, :], (0.0,))])

        gather_edges(nc, k, src, dst, edge_weight.rearrange("e o -> (e o)"), unsorted)
        low = 256
        high = -(-(k.N + 1) // low)
        assert high <= 512
        radix_pass(nc, k, "low", [(unsorted, half_src, 0), (unsorted, half_dst, 1)], 0, low, fills)
        radix_pass(nc, k, "high", [(half_src, ordered_src, 0), (half_dst, ordered_dst, 1)], 8, high)
        for side, field, node_map, ordered in ((by_src, 0, map_src, ordered_src), (by_dst, 1, map_dst, ordered_dst)):
            load_side(nc, k, side, ordered, field, k.edge_weight if field == 1 else None)
            edge_pass(nc, k, f"map_{side.name}", side, MapNodes(nc, k, side, node_map), width=2)
        join_maps(nc, k, map_src, map_dst, joined)
        edge_features(nc, k, W_l0, b_l0, W_l1, b_l1, feats, [GatherMap(nc, k, side, joined) for side in (by_src, by_dst)])
        prepare(nc, k, by_src, by_dst)

        run_node_pass(nc, k, StartPass(nc, k, "start", x, hops[EP:EP + NP, :], x1),
                      beside=[GatherRows(nc, k, x, k.key_x, h_rows)])
        odd, even = hops[0:EP, :], hops[EP + NP:EP + NP + EP, :]
        hop = dict(weight=k.w_hop, scale=k.s_hop)
        edge_pass(nc, k, "hop_first", by_src, Store(nc, odd, h_rows), table=x, index=k.from_x, **hop)
        with nc.Fori(0, (K_HOPS - 2) // 2):
            edge_pass(nc, k, "hop_even", by_src, Store(nc, even, h_rows), table=hops[0:EP + NP, :], index=k.i_odd, **hop)
            edge_pass(nc, k, "hop_odd", by_src, Store(nc, odd, h_rows), table=hops, index=k.i_even, **hop)
        edge_pass(nc, k, "hop_last", by_src, NormScatter(nc, k, x1, by_src.end, h_rows),
                  table=hops[0:EP + NP, :], index=k.i_odd, **hop)

        edge_pass(nc, k, "gcn", by_dst, Scatter(nc, k, sums, by_dst.end), table=x1, index=by_dst.other,
                  weight=k.w_gcn, scale=k.s_gcn)
        run_node_pass(nc, k, GcnPass(nc, k, "gcn_nodes", x1, sums, joined, W, b, slope, x2))

        fold_weights(nc, k, (w2, w3, w4), (b2, b3, b4), attn_w, attn_b, fus_w, fus_b, k.folded)
        edge_pass(nc, k, "cheb1", by_dst, Store(nc, hop1[0:EP, :]), table=x2, index=by_dst.other, weight=k.w_cheb)
        edge_pass(nc, k, "cheb2", by_dst, Store(nc, hop2[0:EP, :]), table=hop1, index=k.i_cheb, weight=k.w_cheb2)
        edge_pass(nc, k, "cheb3", by_dst, MixHops(nc, k, mixed, by_dst.end, hop1[0:EP, :], hop2[0:EP, :], k.folded),
                  table=hop2, index=k.i_cheb, weight=k.w_cheb2)
        run_node_pass(nc, k, ChebPass(nc, k, "cheb_nodes", x2, mixed, joined, k.folded, k.totals, mid))
        batch_norm(nc, k, k.totals, gamma, beta, k.coefficients)
        run_node_pass(nc, k, NormPass(nc, k, "cheb_norm", x2, mid, k.coefficients, x3))

        edge_pass(nc, k, "gine1", by_dst, Scatter(nc, k, sums, by_dst.end), table=x3, index=by_dst.other, added=feats)
        run_node_pass(nc, k, GinePass(nc, k, "gine1_nodes", x3, sums, W00, b00, W01, b01, conv))
        edge_pass(nc, k, "gine2", by_dst, Scatter(nc, k, sums, by_dst.end), table=conv, index=by_dst.other, added=feats)
        run_node_pass(nc, k, GinePass(nc, k, "gine2_nodes", conv, sums, W10, b10, W11, b11, out, skip=x3, final=True))


_INS = ["x", "src", "dst", "edge_weight1", "L1_gnn_W", "L1_gnn_b", "L1_gnn_prelu_a", "L2_gnn_w2", "L2_gnn_b2",
        "L2_gnn_w3", "L2_gnn_b3", "L2_gnn_w4", "L2_gnn_b4", "L2_gnn_attn_w", "L2_gnn_attn_b", "L2_gnn_fus_w",
        "L2_gnn_fus_b", "L2_gnn_bn_gamma", "L2_gnn_bn_beta", "L3_gnn_W_l0", "L3_gnn_b_l0", "L3_gnn_W_l1",
        "L3_gnn_b_l1", "L3_gnn_W00", "L3_gnn_b00", "L3_gnn_W01", "L3_gnn_b01", "L3_gnn_W10", "L3_gnn_b10",
        "L3_gnn_W11", "L3_gnn_b11"]


def kernel(**inputs):
    import numpy as _np
    import concourse.bacc as _bacc
    from concourse import mybir as _mybir
    from concourse.bass_utils import run_bass_kernel_spmd as _run

    nc = _bacc.Bacc("TRN2", target_bir_lowering=False, num_devices=1)
    arrays, args = {}, []
    for name in _INS:
        a = _np.ascontiguousarray(inputs[name])
        arrays[f"in_{name}_dram"] = a
        args.append(nc.dram_tensor(f"in_{name}_dram", a.shape, _mybir.dt.from_np(a.dtype), kind="ExternalInput").ap())
    out = nc.dram_tensor("out_0_dram", arrays["in_x_dram"].shape, F32, kind="ExternalOutput").ap()
    graph_layers(nc, out, *args)
    r = _run(nc, [arrays], core_ids=[0])
    return r.results[0]["out_0_dram"]
```
